# Optimizing a Trainium2 kernel written in Bass

```python
import numpy as np
import jax
import jax.numpy as jnp

def _softmax(x, axis=-1):
    return jax.nn.softmax(x, axis=axis)

def _gelu(x):
    return jax.nn.gelu(x, approximate=True)

def _silu(x):
    return jax.nn.silu(x)

def _sigmoid(x):
    return jax.nn.sigmoid(x)

def _layernorm(x, axis=-1, eps=1e-05):
    m = jnp.mean(x, axis=axis, keepdims=True)
    v = jnp.var(x, axis=axis, keepdims=True)
    return (x - m) / jnp.sqrt(v + eps)

def _scatter_add(tgt, idx, src, axis=0):
    return tgt.at[idx].add(src)

def _segment_sum(src, seg, n):
    return jax.ops.segment_sum(src, seg, n)
kernel_name = 'mk_gnn_resnorm_d4_gnn_r32_a80f78'

def setup_inputs(seed: int=0):
    np.random.seed(seed)
    _w = jnp.asarray

    def _rec_inputs():
        import jax
        import jax.numpy as jnp
        _gk = jax.random.key(seed)
        x = -0.000202 + 1 * jax.random.normal(jax.random.fold_in(_gk, 1), (3125, 128), jnp.float32)
        src = jax.random.randint(jax.random.fold_in(_gk, 2), (100000,), 0, 3125, jnp.int32)
        dst = jnp.minimum((3125 * jax.random.uniform(jax.random.fold_in(_gk, 3), (100000,)) ** 2.0).astype(jnp.int32), 99999)
        _o = jnp.argsort(dst, stable=True)
        src = src[_o]
        dst = dst[_o]
        edge_attr_64 = 0.000127647 + 1.00004 * jax.random.normal(jax.random.fold_in(_gk, 11), (100000, 64), jnp.float32)
        edge_weight = jax.random.uniform(jax.random.fold_in(_gk, 13), (100000,), jnp.float32, 0.0, 4.99999)
        node_type_100 = jax.random.randint(jax.random.fold_in(_gk, 14), (3125,), 0, 100, jnp.int32)
        return (x, src, dst, edge_attr_64, edge_weight, node_type_100)
    x, src, dst, edge_attr_64, edge_weight, node_type_100 = _rec_inputs()

    def _L0_gnn_setup():
        import jax, jax.numpy as jnp
        import numpy as np
        N_NODES = 50000
        N_EDGES = 25000
        D = 128
        N_LAYERS = 5

        def _max_agg_conv(x, src, dst, W, b, n_nodes):
            h = jnp.einsum('nd,od->no', x, W) + b
            m = jax.ops.segment_max(h[src], dst, num_segments=n_nodes)
            return jnp.where(jnp.isneginf(m), 0.0, m)
        key = jax.random.key(seed)
        k1, k2, k3, k4 = jax.random.split(key, 4)
        x = jax.random.normal(k1, (N_NODES, D), dtype=jnp.float32)
        edge_index = jax.random.randint(k2, (2, N_EDGES), 0, N_NODES, dtype=jnp.int64)
        Ws = jax.random.normal(k3, (N_LAYERS, D, D), dtype=jnp.float32) * (1.0 / np.sqrt(D))
        bs = jax.random.normal(k4, (N_LAYERS, D), dtype=jnp.float32) * 0.01
        return {'x': x, 'edge_index': edge_index, 'Ws': Ws, 'bs': bs}
    _L0_gnn_all = _L0_gnn_setup()
    _L0_gnn_in = {k: v for k, v in _L0_gnn_all.items() if k in ('Ws', 'bs')}
    del _L0_gnn_all

    def _L1_gnn_setup():
        import jax, jax.numpy as jnp
        import numpy as np
        N = 50000
        E = 25000
        IN = 128
        HID = 128
        OUT = 128
        HEADS = 4
        NEG_SLOPE = 0.2

        def gat_conv(x, ei, W, a_src, a_dst, b, concat):
            n = x.shape[0]
            H, C = a_src.shape
            h = (x @ W).reshape(n, H, C)
            src, dst = (ei[0], ei[1])
            alpha_s = jnp.einsum('nhc,hc->nh', h, a_src)
            alpha_d = jnp.einsum('nhc,hc->nh', h, a_dst)
            e = jax.nn.leaky_relu(alpha_s[src] + alpha_d[dst], NEG_SLOPE)
            m = jax.ops.segment_max(e, dst, num_segments=n)
            p = jnp.exp(e - m[dst])
            denom = jax.ops.segment_sum(p, dst, num_segments=n)
            alpha = p / (denom[dst] + 1e-16)
            out = jax.ops.segment_sum(h[src] * alpha[:, :, None], dst, num_segments=n)
            out = out.reshape(n, H * C) if concat else out.mean(axis=1)
            return out + b
        key = jax.random.key(seed)
        ks = jax.random.split(key, 16)

        def glorot(k, shape):
            fan = shape[0] if len(shape) == 2 else int(np.prod(shape))
            return jax.random.normal(k, shape, jnp.float32) * np.float32(1.0 / np.sqrt(fan))
        C = HID // HEADS
        x = jax.random.normal(ks[0], (N, IN), jnp.float32)
        edge_index = jax.random.randint(ks[1], (2, E), 0, N, jnp.int32)
        return {'x': x, 'edge_index': edge_index, 'W1': glorot(ks[2], (IN, HID)), 'as1': glorot(ks[3], (HEADS, C)), 'ad1': glorot(ks[4], (HEADS, C)), 'b1': jnp.zeros((HID,), jnp.float32), 'W2': glorot(ks[5], (HID, HID)), 'as2': glorot(ks[6], (HEADS, C)), 'ad2': glorot(ks[7], (HEADS, C)), 'b2': jnp.zeros((HID,), jnp.float32), 'W3': glorot(ks[8], (HID, OUT)), 'as3': glorot(ks[9], (1, OUT)), 'ad3': glorot(ks[10], (1, OUT)), 'b3': jnp.zeros((OUT,), jnp.float32)}
    _L1_gnn_all = _L1_gnn_setup()
    _L1_gnn_in = {k: v for k, v in _L1_gnn_all.items() if k in ('W1', 'as1', 'ad1', 'b1', 'W2', 'as2', 'ad2', 'b2', 'W3', 'as3', 'ad3', 'b3')}
    del _L1_gnn_all

    def _L2_gnn_setup():
        import jax, jax.numpy as jnp
        import numpy as np
        STOP = 5.0
        N_NODES = 3125
        N_EDGES = 20000
        HIDDEN = 128
        NUM_RBF = 64
        MAX_Z = 100
        key = jax.random.key(seed)
        ks = jax.random.split(key, 10)
        z = jax.random.randint(ks[0], (N_NODES,), 0, MAX_Z)
        x = jax.random.normal(ks[1], (N_NODES, HIDDEN), dtype=jnp.float32)
        edge_index = jax.random.randint(ks[2], (2, N_EDGES), 0, N_NODES)
        edge_weight = jax.random.uniform(ks[3], (N_EDGES,), dtype=jnp.float32) * STOP
        edge_attr = jax.random.normal(ks[4], (N_EDGES, NUM_RBF), dtype=jnp.float32)
        emb = jax.random.normal(ks[5], (MAX_Z, HIDDEN), dtype=jnp.float32)
        Wd = jax.random.normal(ks[6], (NUM_RBF, HIDDEN), dtype=jnp.float32) / np.sqrt(NUM_RBF)
        bd = jax.random.normal(ks[7], (HIDDEN,), dtype=jnp.float32) * 0.01
        Wc = jax.random.normal(ks[8], (2 * HIDDEN, HIDDEN), dtype=jnp.float32) / np.sqrt(2 * HIDDEN)
        bc = jax.random.normal(ks[9], (HIDDEN,), dtype=jnp.float32) * 0.01
        return {'z': z, 'x': x, 'edge_index': edge_index, 'edge_weight': edge_weight, 'edge_attr': edge_attr, 'emb': emb, 'Wd': Wd, 'bd': bd, 'Wc': Wc, 'bc': bc}
    _L2_gnn_all = _L2_gnn_setup()
    _L2_gnn_in = {k: v for k, v in _L2_gnn_all.items() if k in ('emb', 'Wd', 'bd', 'Wc', 'bc')}
    del _L2_gnn_all

    def _L3_gnn_setup():
        import jax, jax.numpy as jnp
        import numpy as np
        N = 3125
        E = 50000
        D_IN = 128
        D_OUT = 128
        key = jax.random.key(seed)
        k1, k2, k3, k4, k5, k6 = jax.random.split(key, 6)
        x = jax.random.normal(k1, (N, D_IN), dtype=jnp.float32)
        edge_index = jax.random.randint(k2, (2, E), 0, N, dtype=jnp.int32)
        W1 = jax.random.normal(k3, (D_IN, D_OUT), dtype=jnp.float32) / np.sqrt(D_IN)
        b1 = jnp.zeros((D_OUT,), dtype=jnp.float32)
        W2 = jax.random.normal(k4, (D_OUT, D_OUT), dtype=jnp.float32) / np.sqrt(D_OUT)
        b2 = jnp.zeros((D_OUT,), dtype=jnp.float32)
        return {'x': x, 'edge_index': edge_index, 'W1': W1, 'b1': b1, 'W2': W2, 'b2': b2}
    _L3_gnn_all = _L3_gnn_setup()
    _L3_gnn_in = {k: v for k, v in _L3_gnn_all.items() if k in ('W1', 'b1', 'W2', 'b2')}
    del _L3_gnn_all
    return {'x': x, 'src': src, 'dst': dst, 'edge_attr_64': edge_attr_64, 'edge_weight': edge_weight, 'node_type_100': node_type_100, 'L0_gnn_Ws': _L0_gnn_in['Ws'], 'L0_gnn_bs': _L0_gnn_in['bs'], 'L1_gnn_W1': _L1_gnn_in['W1'], 'L1_gnn_as1': _L1_gnn_in['as1'], 'L1_gnn_ad1': _L1_gnn_in['ad1'], 'L1_gnn_b1': _L1_gnn_in['b1'], 'L1_gnn_W2': _L1_gnn_in['W2'], 'L1_gnn_as2': _L1_gnn_in['as2'], 'L1_gnn_ad2': _L1_gnn_in['ad2'], 'L1_gnn_b2': _L1_gnn_in['b2'], 'L1_gnn_W3': _L1_gnn_in['W3'], 'L1_gnn_as3': _L1_gnn_in['as3'], 'L1_gnn_ad3': _L1_gnn_in['ad3'], 'L1_gnn_b3': _L1_gnn_in['b3'], 'L2_gnn_emb': _L2_gnn_in['emb'], 'L2_gnn_Wd': _L2_gnn_in['Wd'], 'L2_gnn_bd': _L2_gnn_in['bd'], 'L2_gnn_Wc': _L2_gnn_in['Wc'], 'L2_gnn_bc': _L2_gnn_in['bc'], 'L3_gnn_W1': _L3_gnn_in['W1'], 'L3_gnn_b1': _L3_gnn_in['b1'], 'L3_gnn_W2': _L3_gnn_in['W2'], 'L3_gnn_b2': _L3_gnn_in['b2']}

def reference(x, src, dst, edge_attr_64, edge_weight, node_type_100, L0_gnn_Ws, L0_gnn_bs, L1_gnn_W1, L1_gnn_as1, L1_gnn_ad1, L1_gnn_b1, L1_gnn_W2, L1_gnn_as2, L1_gnn_ad2, L1_gnn_b2, L1_gnn_W3, L1_gnn_as3, L1_gnn_ad3, L1_gnn_b3, L2_gnn_emb, L2_gnn_Wd, L2_gnn_bd, L2_gnn_Wc, L2_gnn_bc, L3_gnn_W1, L3_gnn_b1, L3_gnn_W2, L3_gnn_b2):
    import jax
    import jax.numpy as jnp

    def _L0_gnn_ref(x, edge_index, Ws, bs):
        import jax, jax.numpy as jnp
        import numpy as np
        N_NODES = 50000
        N_EDGES = 25000
        D = 128
        N_LAYERS = 5

        def _max_agg_conv(x, src, dst, W, b, n_nodes):
            h = jnp.einsum('nd,od->no', x, W) + b
            m = jax.ops.segment_max(h[src], dst, num_segments=n_nodes)
            return jnp.where(jnp.isneginf(m), 0.0, m)
        src = edge_index[0]
        dst = edge_index[1]
        n = x.shape[0]
        for i in range(N_LAYERS - 1):
            x = _max_agg_conv(x, src, dst, Ws[i], bs[i], n)
            x = jax.nn.silu(x)
        x = _max_agg_conv(x, src, dst, Ws[N_LAYERS - 1], bs[N_LAYERS - 1], n)
        return x

    def _L1_gnn_ref(x, edge_index, W1, as1, ad1, b1, W2, as2, ad2, b2, W3, as3, ad3, b3):
        import jax, jax.numpy as jnp
        import numpy as np
        N = 50000
        E = 25000
        IN = 128
        HID = 128
        OUT = 128
        HEADS = 4
        NEG_SLOPE = 0.2

        def gat_conv(x, ei, W, a_src, a_dst, b, concat):
            n = x.shape[0]
            H, C = a_src.shape
            h = (x @ W).reshape(n, H, C)
            src, dst = (ei[0], ei[1])
            alpha_s = jnp.einsum('nhc,hc->nh', h, a_src)
            alpha_d = jnp.einsum('nhc,hc->nh', h, a_dst)
            e = jax.nn.leaky_relu(alpha_s[src] + alpha_d[dst], NEG_SLOPE)
            m = jax.ops.segment_max(e, dst, num_segments=n)
            p = jnp.exp(e - m[dst])
            denom = jax.ops.segment_sum(p, dst, num_segments=n)
            alpha = p / (denom[dst] + 1e-16)
            out = jax.ops.segment_sum(h[src] * alpha[:, :, None], dst, num_segments=n)
            out = out.reshape(n, H * C) if concat else out.mean(axis=1)
            return out + b
        n = x.shape[0]
        loops = jnp.arange(n, dtype=edge_index.dtype)
        ei = jnp.concatenate([edge_index, jnp.stack([loops, loops])], axis=1)
        h = jax.nn.relu(gat_conv(x, ei, W1, as1, ad1, b1, True))
        h = jax.nn.relu(gat_conv(h, ei, W2, as2, ad2, b2, True))
        return gat_conv(h, ei, W3, as3, ad3, b3, False)

    def _L2_gnn_ref(z, x, edge_index, edge_weight, edge_attr, emb, Wd, bd, Wc, bc):
        import jax, jax.numpy as jnp
        import numpy as np
        STOP = 5.0
        N_NODES = 3125
        N_EDGES = 20000
        HIDDEN = 128
        NUM_RBF = 64
        MAX_Z = 100
        row, col = (edge_index[0], edge_index[1])
        mask = (row != col).astype(edge_weight.dtype)
        C = 0.5 * (jnp.cos(edge_weight * jnp.pi / STOP) + 1.0)
        C = C * (edge_weight < STOP).astype(edge_weight.dtype)
        W = (edge_attr @ Wd + bd) * (C * mask)[:, None]
        xn = emb[z][row] * W
        agg = jax.ops.segment_sum(xn, col, num_segments=x.shape[0])
        return jnp.concatenate([x, agg], axis=-1) @ Wc + bc

    def _L3_gnn_ref(x, edge_index, W1, b1, W2, b2):
        import jax, jax.numpy as jnp
        import numpy as np
        N = 3125
        E = 50000
        D_IN = 128
        D_OUT = 128
        n = x.shape[0]
        loops = jnp.arange(n, dtype=edge_index.dtype)
        row = jnp.concatenate([edge_index[0], loops])
        col = jnp.concatenate([edge_index[1], loops])
        deg = jax.ops.segment_sum(jnp.ones_like(col, dtype=x.dtype), col, num_segments=n)
        dinv = jnp.where(deg > 0, jax.lax.rsqrt(deg), 0.0)
        norm = dinv[row] * dinv[col]

        def gcn_layer(h, W, b):
            h = h @ W
            msg = h[row] * norm[:, None]
            agg = jax.ops.segment_sum(msg, col, num_segments=n)
            return agg + b
        h = gcn_layer(x, W1, b1)
        return gcn_layer(h, W2, b2)
    edge_index = jnp.stack([src, dst])
    x = _layernorm(x + _L0_gnn_ref(x, edge_index, L0_gnn_Ws, L0_gnn_bs), axis=-1)
    x = _layernorm(x + _L1_gnn_ref(x, edge_index, L1_gnn_W1, L1_gnn_as1, L1_gnn_ad1, L1_gnn_b1, L1_gnn_W2, L1_gnn_as2, L1_gnn_ad2, L1_gnn_b2, L1_gnn_W3, L1_gnn_as3, L1_gnn_ad3, L1_gnn_b3), axis=-1)
    x = _layernorm(x + _L2_gnn_ref(node_type_100, x, edge_index, edge_weight, edge_attr_64, L2_gnn_emb, L2_gnn_Wd, L2_gnn_bd, L2_gnn_Wc, L2_gnn_bc), axis=-1)
    x = _layernorm(x + _L3_gnn_ref(x, edge_index, L3_gnn_W1, L3_gnn_b1, L3_gnn_W2, L3_gnn_b2), axis=-1)
    return x

_drawn_inputs = setup_inputs


def setup_inputs(seed=0):
    import zlib

    import numpy as np

    out = dict(_drawn_inputs(seed))
    spreads = {'L1_gnn_b1': (0.0, 0.1),
     'L1_gnn_b2': (0.0, 0.1),
     'L1_gnn_b3': (0.0, 0.1),
     'L3_gnn_b1': (0.0, 0.1),
     'L3_gnn_b2': (0.0, 0.1)}
    factors = {'L0_gnn_bs': 8.0,
     'L1_gnn_ad1': 3.999,
     'L1_gnn_as2': 3.106,
     'L1_gnn_ad2': 8.0,
     'L1_gnn_as3': 8.0,
     'L1_gnn_ad3': 8.0,
     'L2_gnn_bd': 5.533,
     'L2_gnn_bc': 8.0}
    for name, (base, spread) in spreads.items():
        noise = np.random.default_rng([zlib.crc32(name.encode()), seed]).standard_normal(out[name].shape)
        drawn = base * np.exp(spread * noise) if base else spread * noise
        out[name] = jnp.asarray(drawn.astype(out[name].dtype))
    for name, factor in factors.items():
        out[name] = (out[name] * factor).astype(out[name].dtype)
    return out
```

```python
from contextlib import ExitStack

import numpy as np
import concourse.bass as bass
from concourse import mybir

P = 128
N, E, D = 3125, 100000, 128
NB = -(-N // P)
NP_ = NB * P
T = 784
EP = P * T
SLOTS = 4
CT = 14
CT0 = 7
NRBF, NTYPE = 64, 100
SKIP = 1 << 20
BIG = 3.0e38
GB = 3
NG = -(-NB // GB)
NL0 = 5
GSZ, SSZ = 1904, 1904

PASSES = [dict(kind="first", H=0, RW=2 * D, W=D, CT=CT0)]
PASSES += [dict(kind="max", H=0, RW=D, W=D, CT=CT) for _ in range(NL0 - 1)]
PASSES += [dict(kind="gat", H=h, RW=D + 2 * h, W=D + 2 * h, CT=CT) for h in (4, 4, 1)]
PASSES += [dict(kind="sum", H=0, RW=D, W=D, CT=CT) for _ in range(2)]
NPASS = len(PASSES)
for k, ps in enumerate(PASSES):
    ps["ITER"] = T // ps["CT"] // SLOTS
    ps["slot_base"] = sum(q["ITER"] for q in PASSES[:k])
    ps["gath_base"] = 16 * (T // SLOTS) * k
    ps["chunk_base"] = SLOTS * ps["slot_base"]
CF = 8
NDENSE = 11
DENSE_OF_PASS = [0, 1, 2, 3, 4, 5, 6, 7, 9, 10]
WIDTH = [D] * 5 + [D + 8, D + 8, D + 2] + [D] * 3


def program(nc, A, out):
    fp32, i32 = mybir.dt.float32, mybir.dt.int32
    ALU, ACT, AX = mybir.AluOpType, mybir.ActivationFunctionType, mybir.AxisListType
    ctx = ExitStack()
    with ctx:
        def sb(name, shape, dt=fp32):
            return ctx.enter_context(nc.sbuf_tensor(name, shape, dt))

        def sem(name):
            return ctx.enter_context(nc.semaphore(name))

        def dram(name, shape):
            return nc.dram_tensor(name, shape, fp32, kind="Internal").ap()

        table = {w: dram(f"table{w}", (NP_, w)) for w in (2 * D, D, D + 8, D + 2)}
        runs = {w: dram(f"runs{w}", (EP, w)) for w in (D, D + 8, D + 2)}
        runs_cf = dram("runs_cf", (EP, D))
        starts_ad = {h: dram(f"starts_ad{h}", (EP, h)) for h in (4, 1)}

        src_i = sb("src_i", [P, T + SLOTS * CT], i32)
        dst_f = sb("dst_f", [P, T])
        keep01 = sb("keep01", [P, T])
        keepM = sb("keepM", [P, T])
        gate = sb("gate", [P, T])
        idx = [sb(f"idx{b}", [P, CT], i32) for b in range(SLOTS)]
        G = [sb(f"G{b}", [P, GSZ]) for b in range(SLOTS)]
        S_all = sb("S_all", [P, SLOTS * SSZ])
        S = [S_all[:, b * SSZ:(b + 1) * SSZ] for b in range(SLOTS)]
        X = sb("X", [P, NB, D])
        XRES = sb("XRES", [P, NB, D])
        R = sb("R", [P, NB * (D + 8)])
        Hx = sb("Hx", [P, NB * (D + 8)])
        dst_i = Hx[:, 0:T].bitcast(i32)
        xT = sb("xT", [P, NP_])
        aggT = sb("aggT", [P, NP_])
        AGG = S_all[:, 0:NB * D].rearrange("p (b d) -> p b d", d=D)
        ad_e = sb("ad_e", [P, 4, T])
        ident = sb("ident", [P, P])
        shift = sb("shift", [P, P])
        wrap = sb("wrap", [P, P])
        WR = sb("WR", [P, NDENSE + 1, D + 8])
        bias = sb("bias", [P, NDENSE, D])
        w_raw = aggT[:, 3 * T:3 * T + NL0 * D].rearrange("p (l d) -> p l d", d=D)
        wT = sb("wT", [P, D])
        att = sb("att", [P, 3, 2])
        att_m = sb("att_m", [P, 3, 8])
        head_of = sb("head_of", [P, 4])
        head_rows = sb("head_rows", [4, P])
        ones_row = sb("ones_row", [1, P])
        wd = sb("wd", [NRBF + 1, D])
        eaT = sb("eaT", [NRBF + 1, 2, CT0 * P])
        ea_all = sb("ea_all", [P, SLOTS * CT0 * NRBF])
        ea = [ea_all[:, b * CT0 * NRBF:(b + 1) * CT0 * NRBF] for b in range(SLOTS)]
        nval = sb("nval", [P, NB])
        ztype = sb("ztype", [P, NB], i32)
        small = sb("small", [P, 64])
        nodes = sb("nodes", [P, 16, NB])
        nodes_i = sb("nodes_i", [P, 3, NB], i32)
        edge_i = sb("edge_i", [P, 3], i32)
        kB01 = sb("kB01", [P, P])
        kBM = sb("kBM", [P, P])
        V = sb("V", [P, P + 1])
        V2 = sb("V2", [P, P + 1])
        mV = sb("mV", [4, P + 1])
        dV = sb("dV", [4, P + 1])
        DD = sb("DD", [4, 2, P])
        EE = sb("EE", [4, 2, P])
        prevm = sb("prevm", [4, P])
        denT = sb("denT", [4, P])
        FX = sb("FX", [P, D + 8])
        FX2 = sb("FX2", [P, D + 8])
        ad0 = sb("ad0", [P, D + 8])
        fxm = sb("fxm", [P, 3, 4])
        fxe = sb("fxe", [P, 2, 4])
        zc = sb("zc", [P, CT, 4])
        ec = sb("ec", [P, CT, 4])
        mbuf = sb("mbuf", [P, CT + 1, 4])
        mp = sb("mp", [P, CT, 4])
        dc = sb("dc", [P, 2, CT, 4])
        pc = sb("pc", [P, 2, CT, 4])
        tmpr = sb("tmpr", [P, D])
        stats = sb("stats", [P, NB, 6])
        mv = sb("mv", [P, NB, 2])
        na = ea_all[:, 0:8 * NB * 4].rearrange("p (q n) -> p q n", q=8)
        PS = ctx.enter_context(nc.psum_tensor("PS", [P, 8, 512], fp32))

        (N_CNT, N_END, N_START, N_DEG, N_HAS, N_DINV, N_P, N_T0, N_T1) = range(9)
        def nd(i):
            return nodes[:, i, :]

        setup_in = sem("setup_in")
        ready_const = sem("ready_const")
        chain_v = sem("chain_v")
        chain_g = sem("chain_g")
        ends_rows = [sem(f"ends_rows{b}") for b in range(SLOTS)]
        ends_used = sem("ends_used")
        emb_rows = sem("emb_rows")
        emb_stored = sem("emb_stored")
        part_ready = sem("part_ready")
        part_rows = sem("part_rows")
        flag_ready = sem("flag_ready")
        flag_rows = sem("flag_rows")
        p_ready = sem("p_ready")
        cnt_ready = sem("cnt_ready")
        start_ps = sem("start_ps")
        nodes_ready = sem("nodes_ready")
        fix_ready = sem("fix_ready")
        deg_ready = sem("deg_ready")
        dinv_root = sem("dinv_root")
        cos_arg = sem("cos_arg")
        go = sem("go")
        cos_done = sem("cos_done")
        w_ps = sem("w_ps")
        w_sb = sem("w_sb")
        att_ready = sem("att_ready")
        zero_ready = sem("zero_ready")
        zero_stored = sem("zero_stored")
        x_ready = sem("x_ready")
        xT_ps = sem("xT_ps")
        xT_sb = sem("xT_sb")
        h_ps = sem("h_ps")
        h_sb = sem("h_sb")
        agg_ready = sem("agg_ready")
        aggT_ps = sem("aggT_ps")
        aggT_sb = sem("aggT_sb")
        table_stored = sem("table_stored")
        ad_scattered = sem("ad_scattered")
        ad_first = sem("ad_first")
        ad_loaded = sem("ad_loaded")
        idx_staged = [sem(f"idx_staged{b}") for b in range(SLOTS)]
        gathered = [sem(f"gathered{b}") for b in range(SLOTS)]
        chunk_done = [sem(f"chunk_done{b}") for b in range(SLOTS)]
        run_stored = [sem(f"run_stored{b}") for b in range(SLOTS)]
        ea_in = [sem(f"ea_in{b}") for b in range(SLOTS)]
        ea_ps = sem("ea_ps")
        ea_sb = sem("ea_sb")
        filt_ps = sem("filt_ps")
        filt_used = sem("filt_used")
        soft_arg = sem("soft_arg")
        soft_exp = sem("soft_exp")
        tail_T = sem("tail_T")
        tail_V = sem("tail_V")
        tail_C = sem("tail_C")
        tail_B = sem("tail_B")
        tail_arg = sem("tail_arg")
        tail_exp = sem("tail_exp")
        fix_in = sem("fix_in")
        fix_arg = sem("fix_arg")
        fix_exp = sem("fix_exp")
        fix_new = sem("fix_new")
        fix_out = sem("fix_out")
        end_in = sem("end_in")
        post_arg = sem("post_arg")
        post_exp = sem("post_exp")
        ln_var = sem("ln_var")
        ln_std = sem("ln_std")
        out_ready = sem("out_ready")
        out_stored = sem("out_stored")

        def rows(buf, w):
            return buf[:, 0:NB * w].rearrange("p (b w) -> p b w", w=w)

        def node_rows(ap):
            return ap.rearrange("(b p) w -> p b w", p=P)

        def blocks(g):
            return range(GB * g, min(NB, GB * g + GB))

        def src_of(d):
            return XRES if d in (0, 5, 8, 9) else X

        def g_rows(b, ps):
            return G[b][:, 0:ps["CT"] * ps["RW"]].rearrange("p (t w) -> p t w", w=ps["RW"])

        def s_rows(b, ps):
            return S[b][:, 0:ps["CT"] * ps["W"]].rearrange("p (t w) -> p t w", w=ps["W"])

        def s_cf(b):
            return S[b][:, CT0 * D:2 * CT0 * D].rearrange("p (t w) -> p t w", w=D)

        def ps_rows(bank, g, w):
            return PS[:, bank, 0:w * len(blocks(g))].rearrange("p (b w) -> p b w", w=w)

        def end_gathers(k):
            return 16 * NB * (k + 2)

        block = ctx.enter_context(nc.Block())

        N_SETUP = 0

        @block.sync
        def _(sp):
            nonlocal N_SETUP
            def load(dst, src):
                nonlocal N_SETUP
                N_SETUP += 1
                sp.dma_start(dst, src).then_inc(setup_in, 16)

            load(dst_i[:, :], A["dst"].rearrange("(p t) -> p t", t=T))
            load(src_i[:, 0:T], A["src"].rearrange("(p t) -> p t", t=T))
            load(gate[:, :], A["edge_weight"].rearrange("(p t) -> p t", t=T))
            load(XRES[:, :, :], node_rows(A["x"]))
            load(w_raw[:, :, :], A["L0_gnn_Ws"].rearrange("l o d -> o l d"))
            with nc.allow_non_contiguous_dma(reason="small vectors, once"):
                load(ztype[:, :], A["node_type_100"].rearrange("(b p) -> p b", p=P))
                for j in range(3):
                    load(att[:, j, 0:1], A[f"L1_gnn_as{j + 1}"].rearrange("h (c o) -> (h c) o", o=1))
                    load(att[:, j, 1:2], A[f"L1_gnn_ad{j + 1}"].rearrange("h (c o) -> (h c) o", o=1))
            for j in range(3):
                load(WR[:, 5 + j, 0:D], A[f"L1_gnn_W{j + 1}"])
                load(bias[:, 5 + j, :], A[f"L1_gnn_b{j + 1}"].rearrange("(o d) -> o d", o=1).to_broadcast([P, D]))
            load(WR[:, 8, 0:D], A["L2_gnn_Wc"][0:D, :])
            load(WR[:, NDENSE, 0:D], A["L2_gnn_Wc"][D:2 * D, :])
            load(WR[:, 9, 0:D], A["L3_gnn_W1"])
            load(WR[:, 10, 0:D], A["L3_gnn_W2"])
            for d, n in ((8, "L2_gnn_bc"), (9, "L3_gnn_b1"), (10, "L3_gnn_b2")):
                load(bias[:, d, :], A[n].rearrange("(o d) -> o d", o=1).to_broadcast([P, D]))
            for l in range(NL0):
                load(bias[:, l, :], A["L0_gnn_bs"][l:l + 1, :].to_broadcast([P, D]))
            load(wd[0:NRBF, :], A["L2_gnn_Wd"])
            load(wd[NRBF:NRBF + 1, :], A["L2_gnn_bd"].rearrange("(o d) -> o d", o=1))
            ea_view = A["edge_attr_64"].rearrange("(p t) c -> p (t c)", t=T)

            def load_ea(c, b):
                sp.dma_start(ea[b][:, :], ea_view[:, bass.ds(c * CT0 * NRBF, CT0 * NRBF)]).then_inc(ea_in[b], 16)

            for b in range(SLOTS):
                load_ea(b, b)
            sp.wait_ge(zero_ready, 1)
            for h in (4, 1):
                sp.dma_start(starts_ad[h].rearrange("(p t) h -> p (t h)", t=T), ad_e[:, :, :].rearrange("p h t -> p (h t)")[:, 0:T * h]).then_inc(zero_stored, 16)
            sp.wait_ge(emb_rows, 16 * NB)
            sp.dma_start(node_rows(table[2 * D])[:, :, D:2 * D], AGG[:, :, :]).then_inc(emb_stored, 16)

            for k, ps in enumerate(PASSES):
                ct, w, H, base = ps["CT"], ps["W"], ps["H"], ps["slot_base"]
                d = DENSE_OF_PASS[k]
                sp.wait_ge(h_sb, NG * (d + 1))
                sp.dma_start(node_rows(table[ps["RW"]])[:, :, 0:WIDTH[d]], rows(Hx, WIDTH[d])).then_inc(table_stored, 16)
                if H:
                    j = k - 5
                    sp.wait_ge(ad_scattered, 16 * NB * (j + 1))
                    sp.dma_start(R[:, 0:T * H], starts_ad[H].rearrange("(p t) h -> p (t h)", t=T)).then_inc(ad_loaded, 16)
                run_view = runs[w].rearrange("(p t) w -> p (t w)", t=T)
                cf_view = runs_cf.rearrange("(p t) w -> p (t w)", t=T)

                def store(i, last=False):
                    for b in range(SLOTS):
                        c = i * SLOTS + b
                        sp.wait_ge(chunk_done[b], base + i + 1)
                        sp.dma_start(run_view[:, bass.ds(c * ct * w, ct * w)], S[b][:, 0:ct * w]).then_inc(run_stored[b], 16)
                        if ps["kind"] == "first":
                            sp.dma_start(cf_view[:, bass.ds(c * ct * w, ct * w)], S[b][:, ct * w:2 * ct * w]).then_inc(run_stored[b], 16)
                            if not last:
                                sp.wait_ge(ea_ps, c + 1)
                                load_ea(c + SLOTS, b)

                store(0)
                with sp.Fori(1, ps["ITER"] - 1) as i:
                    store(i)
                store(ps["ITER"] - 1, last=True)
            sp.wait_ge(out_ready, 1)
            full = N // P
            sp.dma_start(out[0:full * P, :].rearrange("(b p) d -> p b d", p=P), X[:, 0:full, :]).then_inc(out_stored, 16)
            sp.dma_start(out[full * P:N, :], X[0:N - full * P, full, :]).then_inc(out_stored, 16)
            sp.wait_ge(out_stored, 32)

        @block.gpsimd
        def _(gp):
            count = 0

            def link(ins):
                nonlocal count
                count += 1
                ins.then_inc(chain_g, 1)
                gp.wait_ge(chain_g, count)

            link(nc.gpsimd.memset(ident[:, :], 0.0))
            link(nc.gpsimd.memset(shift[:, :], 0.0))
            link(nc.gpsimd.memset(wrap[:, :], 0.0))
            link(nc.gpsimd.memset(head_of[:, :], 1.0))
            link(nc.gpsimd.memset(head_rows[:, :], 1.0))
            for tile, base in ((ident, 0), (shift, 1), (wrap, -(P - 1))):
                link(nc.gpsimd.affine_select(out=tile[:, :], in_=tile[:, :], compare_op=ALU.not_equal, fill=1.0,
                                             base=base, pattern=[[-1, P]], channel_multiplier=1))
            C = D // 4
            link(nc.gpsimd.affine_select(out=head_of[:, :], in_=head_of[:, :], compare_op=ALU.is_ge, fill=0.0,
                                         base=0, pattern=[[-C, 4]], channel_multiplier=1))
            link(nc.gpsimd.affine_select(out=head_of[:, :], in_=head_of[:, :], compare_op=ALU.is_ge, fill=0.0,
                                         base=C - 1, pattern=[[C, 4]], channel_multiplier=-1))
            link(nc.gpsimd.affine_select(out=head_rows[:, :], in_=head_rows[:, :], compare_op=ALU.is_ge, fill=0.0,
                                         base=0, pattern=[[1, P]], channel_multiplier=-C))
            link(nc.gpsimd.affine_select(out=head_rows[:, :], in_=head_rows[:, :], compare_op=ALU.is_ge, fill=0.0,
                                         base=C - 1, pattern=[[-1, P]], channel_multiplier=C))
            link(nc.gpsimd.iota(small[:, 0:1], pattern=[[0, 1]], base=0, channel_multiplier=T, allow_small_or_imprecise_dtypes=True))
            nc.gpsimd.iota(nval[:, :], pattern=[[P, NB]], base=0, channel_multiplier=1,
                           allow_small_or_imprecise_dtypes=True).then_inc(ready_const, 1)

            def gather(dst, src, ix, s):
                gp.indirect_dma_start(out=dst, out_offset=None, in_=src,
                                      in_offset=bass.IndirectOffsetOnAxis(ap=ix, axis=0)).then_inc(s, 16)

            gp.wait_ge(setup_in, 16 * N_SETUP)
            for b in range(NB):
                gather(AGG[:, b, :], A["L2_gnn_emb"], ztype[:, b:b + 1], emb_rows)
            gp.wait_ge(p_ready, 1)
            for b in range(NB):
                if b >= SLOTS:
                    gp.wait_ge(ends_used, b - SLOTS + 1)
                gather(G[b % SLOTS][:, 0:T].bitcast(i32), A["dst"].rearrange("(p t) -> p t", t=T),
                       nodes_i[:, 2, b:b + 1], ends_rows[b % SLOTS])
            gp.wait_ge(ends_used, NB)
            gp.wait_ge(nodes_ready, 1)

            for k, ps in enumerate(PASSES):
                ct, w, H, base, rw = ps["CT"], ps["W"], ps["H"], ps["slot_base"], ps["RW"]
                gp.wait_ge(table_stored, 16 * (k + 1))
                if k == 0:
                    gp.wait_ge(emb_stored, 16)
                if H:
                    j = k - 5
                    gp.wait_ge(h_sb, NG * (DENSE_OF_PASS[k] + 1))
                    gp.wait_ge(zero_stored, 32)
                    hv = rows(Hx, rw)
                    for b in range(NB):
                        gp.indirect_dma_start(out=starts_ad[H], out_offset=bass.IndirectOffsetOnAxis(ap=nodes_i[:, 1, b:b + 1], axis=0),
                                              in_=hv[:, b, D + H:D + 2 * H], in_offset=None,
                                              bounds_check=EP - 1, oob_is_err=False).then_inc(ad_scattered, 16)
                    gather(ad0[:, 0:rw], table[rw], edge_i[:, 2:3], ad_first)

                def gathers(i, first=False):
                    for b in range(SLOTS):
                        gr = g_rows(b, ps)
                        if not (first and k == 0):
                            gp.wait_ge(chunk_done[b], base + i)
                        gp.wait_ge(idx_staged[b], base + i + 1)
                        gp.sem_inc(go, 1)
                        for t in range(ct):
                            gather(gr[:, t, :], table[rw], idx[b][:, t:t + 1], gathered[b])

                gathers(0, first=True)
                with gp.Fori(1, ps["ITER"]) as i:
                    gathers(i)
                seams = [(runs[w], FX)] + ([(runs_cf, FX2)] if ps["kind"] == "first" else [])
                n0 = k + (1 if k else 0)
                for b in range(SLOTS):
                    stored = 16 * (base + ps["ITER"] + PASSES[0]["ITER"])
                    gp.wait_ge(run_stored[b], stored)
                for r, fx in seams:
                    gather(fx[:, 0:w], r, edge_i[:, 0:1], fix_in)
                gp.wait_ge(fix_new, k + 1)
                for r, fx in seams:
                    gp.indirect_dma_start(out=r, out_offset=bass.IndirectOffsetOnAxis(ap=edge_i[:, 1:2], axis=0),
                                          in_=fx[:, 0:w], in_offset=None,
                                          bounds_check=EP - 1, oob_is_err=False).then_inc(fix_out, 16)
                gp.wait_ge(fix_out, 16 * (n0 + len(seams)))
                rv = rows(R, w)
                for b in range(NB):
                    gather(rv[:, b, :], runs[w], nodes_i[:, 0, b:b + 1], end_in)
                if k == 0:
                    for b in range(NB):
                        gather(AGG[:, b, :], runs_cf, nodes_i[:, 0, b:b + 1], end_in)

        @block.scalar
        def _(act):
            act.wait_ge(setup_in, 16 * N_SETUP)
            act.wait_ge(cos_arg, 1)
            nc.scalar.activation(gate[:, :], gate[:, :], ACT.Sin).then_inc(cos_done, 1)
            n_w = 0

            def weight(dst, src):
                nonlocal n_w
                n_w += 1
                act.wait_ge(w_ps, n_w)
                nc.scalar.copy(dst, src).then_inc(w_sb, 1)

            for l in range(NL0):
                weight(WR[:, l, 0:D], PS[:, 4, 0:D])
            for j, h in enumerate((4, 4, 1)):
                weight(wT[:, :], PS[:, 4, 0:D])
                weight(WR[:, 5 + j, D:D + 2 * h], PS[:, 4, 0:2 * h])
            act.wait_ge(deg_ready, 1)
            nc.scalar.activation(nd(N_T0), nd(N_T0), ACT.Sqrt).then_inc(dinv_root, 1)

            def transposed(d, dst, ps_sem, sb_sem, n0):
                for g in range(NG):
                    m = P * len(blocks(g))
                    act.wait_ge(ps_sem, n0 + g + 1)
                    if g == 0 and d >= 1 and sb_sem is xT_sb:
                        act.wait_ge(h_ps, NG * d)
                    nc.scalar.copy(dst[:, GB * P * g:GB * P * g + m], PS[:, g % 2, 0:m]).then_inc(sb_sem, 1)

            n_tail = n_fix = n_soft = n_post = n_ln = 0
            for k, ps in enumerate(PASSES):
                ct, H, base, kind = ps["CT"], ps["H"], ps["slot_base"], ps["kind"]
                if k == 8:
                    transposed(CF, xT, xT_ps, xT_sb, NG * CF)
                    ln = True
                    n_ln += 1
                    act.wait_ge(ln_var, n_ln)
                    nc.scalar.activation(mv[:, :, 1], mv[:, :, 1], ACT.Sqrt).then_inc(ln_std, 1)
                d = DENSE_OF_PASS[k]
                transposed(d, xT, xT_ps, xT_sb, NG * d)
                gbase = ps["gath_base"]

                def stage(i, b):
                    nc.scalar.copy(idx[b][:, 0:ct], src_i[:, bass.ds((i * SLOTS + b) * ct, ct)]).then_inc(idx_staged[b], 1)

                def chunk_work(i):
                    for b in range(SLOTS):
                        c = i * SLOTS + b
                        if kind == "first":
                            act.wait_ge(ea_ps, c + 1)
                            if not (isinstance(i, int) and c < 2):
                                act.wait_ge(filt_ps, c - 1)
                            for hf, m in ((0, 4), (1, 3)):
                                ins = nc.scalar.copy(eaT[0:NRBF, b % 2, hf * 512:hf * 512 + m * P], PS[0:NRBF, hf, 0:m * P])
                            ins.then_inc(ea_sb, 1)
                        if kind == "gat":
                            act.wait_ge(soft_arg, (k - 5) * SLOTS * ps["ITER"] + c + 1)
                            nc.scalar.activation(pc[:, :, :, 0:H], dc[:, :, :, 0:H], ACT.Exp).then_inc(soft_exp, 1)
                        act.wait_ge(gathered[b], gbase + 16 * ct * (i + 1))
                        stage(i + 1, b)

                for b in range(SLOTS):
                    stage(0, b)
                chunk_work(0)
                if ps["ITER"] > 2:
                    with act.Fori(1, ps["ITER"] - 1) as i:
                        chunk_work(i)
                i = ps["ITER"] - 1
                for b in range(SLOTS):
                    c = i * SLOTS + b
                    if kind == "first":
                        act.wait_ge(ea_ps, c + 1)
                        act.wait_ge(filt_ps, c - 1)
                        for hf, m in ((0, 4), (1, 3)):
                            ins = nc.scalar.copy(eaT[0:NRBF, b % 2, hf * 512:hf * 512 + m * P], PS[0:NRBF, hf, 0:m * P])
                        ins.then_inc(ea_sb, 1)
                    if kind == "gat":
                        act.wait_ge(soft_arg, (k - 5) * SLOTS * ps["ITER"] + c + 1)
                        nc.scalar.activation(pc[:, :, :, 0:H], dc[:, :, :, 0:H], ACT.Exp).then_inc(soft_exp, 1)
                    act.wait_ge(gathered[b], gbase + 16 * ct * (i + 1))
                if kind == "gat":
                    n_tail += 1
                    act.wait_ge(tail_arg, n_tail)
                    nc.scalar.activation(EE[0:H, :, :], DD[0:H, :, :], ACT.Exp).then_inc(tail_exp, 1)
                    n_fix += 1
                    act.wait_ge(fix_arg, n_fix)
                    nc.scalar.activation(fxe[:, :, 0:H], fxm[:, 0:2, 0:H], ACT.Exp).then_inc(fix_exp, 1)
                    n_post += 1
                    act.wait_ge(post_arg, n_post)
                    nc.scalar.activation(na[:, 4:6, 0:NB * H], na[:, 2:4, 0:NB * H], ACT.Exp).then_inc(post_exp, 1)
                if kind in ("first", "max") and k < NL0 - 1:
                    n_post += 0
                    act.wait_ge(agg_ready, k + 2)
                    nc.scalar.activation(X[:, :, :], X[:, :, :], ACT.Silu).then_inc(x_ready, 1)
                if k == 0:
                    transposed(0, aggT, aggT_ps, aggT_sb, 0)
                if k in (4, 7, 9):
                    n_ln += 1
                    act.wait_ge(ln_var, n_ln)
                    nc.scalar.activation(mv[:, :, 1], mv[:, :, 1], ACT.Sqrt).then_inc(ln_std, 1)

        @block.tensor
        def _(pe):
            pe.wait_ge(ready_const, 1)
            pe.wait_ge(part_ready, 1)
            nc.tensor.matmul(PS[:, 5, 0:P], small[:, 1:2].to_broadcast([P, P]), ident[:, :], start=True, stop=True)
            nc.tensor.matmul(PS[:, 5, P:P + 1], shift[:, :], small[:, 1:2], start=True, stop=True).then_inc(part_rows, 1)
            pe.wait_ge(flag_ready, 1)
            nc.tensor.matmul(PS[:, 5, 2 * P:3 * P], small[:, 8:9].to_broadcast([P, P]), ident[:, :], start=True, stop=True).then_inc(flag_rows, 1)
            pe.wait_ge(setup_in, 16 * N_SETUP)
            n_w = 0

            def weight(ins):
                nonlocal n_w
                n_w += 1
                ins.then_inc(w_ps, 1)
                pe.wait_ge(w_sb, n_w)

            for l in range(NL0):
                weight(nc.tensor.transpose(PS[:, 4, 0:D], w_raw[:, l, :], ident[:, :]))
            pe.wait_ge(att_ready, 1)
            for j, h in enumerate((4, 4, 1)):
                weight(nc.tensor.transpose(PS[:, 4, 0:D], WR[:, 5 + j, 0:D], ident[:, :]))
                weight(nc.tensor.matmul(PS[:, 4, 0:2 * h], wT[:, :], att_m[:, j, 0:2 * h], start=True, stop=True))
            pe.wait_ge(cnt_ready, 1)
            nc.tensor.matmul(PS[:, 6, 0:NB], shift[:, :], nd(N_CNT), start=True, stop=False)
            nc.tensor.matmul(PS[:, 6, 0:NB], wrap[:, :], nd(N_T1), start=False, stop=True).then_inc(start_ps, 1)

            def dense(d):
                src, w = src_of(d), WIDTH[d]
                if d:
                    pe.wait_ge(x_ready, d)
                for g in range(NG):
                    if g >= 2:
                        pe.wait_ge(xT_sb, NG * d + g - 1)
                    for n, b in enumerate(blocks(g)):
                        ins = nc.tensor.transpose(PS[:, g % 2, n * P:(n + 1) * P], src[:, b, :], ident[:, :])
                    ins.then_inc(xT_ps, 1)
                    if g:
                        product(d, g - 1)
                product(d, NG - 1)

            def product(d, g):
                w = WIDTH[d]
                pe.wait_ge(xT_sb, NG * d + g + 1)
                if NG * d + g >= 2:
                    pe.wait_ge(h_sb, NG * d + g - 1)
                for n, b in enumerate(blocks(g)):
                    o = PS[:, 2 + (NG * d + g) % 2, n * w:(n + 1) * w]
                    ins = nc.tensor.matmul(o, xT[:, b * P:(b + 1) * P], WR[:, d, 0:w], start=True, stop=(d != CF))
                    if d == CF:
                        ins = nc.tensor.matmul(o, aggT[:, b * P:(b + 1) * P], WR[:, NDENSE, 0:w], start=False, stop=True)
                ins.then_inc(h_ps, 1)

            for k, ps in enumerate(PASSES):
                H, kind, w = ps["H"], ps["kind"], ps["W"]
                if k == 8:
                    dense(CF)
                dense(DENSE_OF_PASS[k])
                if kind == "first":
                    pe.wait_ge(h_sb, NG)

                    def filters(i, first=False):
                        for b in range(SLOTS):
                            c = i * SLOTS + b
                            pe.wait_ge(ea_in[b], 16 * (i + 1))
                            if not (first and b == 0):
                                pe.wait_ge(ea_sb, c)
                            pe.sem_inc(go, 1)
                            for t in range(CT0):
                                ins = nc.tensor.transpose(PS[0:NRBF, t // 4, (t % 4) * P:(t % 4 + 1) * P],
                                                          ea[b][:, t * NRBF:(t + 1) * NRBF], ident[:, :])
                            ins.then_inc(ea_ps, 1)
                            pe.wait_ge(ea_sb, c + 1)
                            if not (first and b < 2):
                                pe.wait_ge(filt_used, c - 1)
                            for t in range(CT0):
                                ins = nc.tensor.matmul(PS[:, 2 + 2 * (b % 2) + t // 4, (t % 4) * P:(t % 4 + 1) * P],
                                                       eaT[:, b % 2, t * P:(t + 1) * P], wd[:, :], start=True, stop=True)
                            ins.then_inc(filt_ps, 1)

                    filters(0, first=True)
                    with pe.Fori(1, ps["ITER"]) as i:
                        filters(i)
                pe.wait_ge(chunk_done[SLOTS - 1], ps["slot_base"] + ps["ITER"])
                last = s_rows(SLOTS - 1, ps)[:, ps["CT"] - 1, :]
                ins = nc.tensor.transpose(PS[:, 6, 0:P], last[:, 0:D], ident[:, :])
                if kind == "first":
                    ins = nc.tensor.transpose(PS[:, 6, P:2 * P], s_cf(SLOTS - 1)[:, CT0 - 1, :], ident[:, :])
                if H:
                    nc.tensor.transpose(PS[0:H, 6, P:2 * P], last[:, D:D + H], ident[:, :])
                    ins = nc.tensor.transpose(PS[0:H, 6, 2 * P:3 * P], last[:, D + H:D + 2 * H], ident[:, :])
                ins.then_inc(tail_T, 1)
                if H:
                    pe.wait_ge(tail_exp, k - 4)
                    hr = head_rows[0:4, :] if H == 4 else ones_row[0:1, :]
                    nc.tensor.matmul(PS[:, 7, 0:P], hr, EE[0:H, 0, :], start=True, stop=True)
                    nc.tensor.matmul(PS[:, 7, P:2 * P], hr, EE[0:H, 1, :], start=True, stop=True).then_inc(tail_B, 1)
                pe.wait_ge(tail_V, k + 1)
                ins = nc.tensor.transpose(PS[:, 6, 0:P], V[:, 0:P], ident[:, :])
                if kind == "first":
                    ins = nc.tensor.transpose(PS[:, 6, P:2 * P], V2[:, 0:P], ident[:, :])
                if H:
                    nc.tensor.transpose(PS[:, 6, P:P + H], dV[0:H, 0:P], ident[0:H, 0:H])
                    ins = nc.tensor.transpose(PS[:, 6, 2 * P:2 * P + H], mV[0:H, 0:P], ident[0:H, 0:H])
                ins.then_inc(tail_C, 1)
                if k == 0:
                    pe.wait_ge(agg_ready, 1)
                    for g in range(NG):
                        if g >= 2:
                            pe.wait_ge(aggT_sb, g - 1)
                        for n, b in enumerate(blocks(g)):
                            ins = nc.tensor.transpose(PS[:, g % 2, n * P:(n + 1) * P], AGG[:, b, :], ident[:, :])
                        ins.then_inc(aggT_ps, 1)
                    pe.wait_ge(aggT_sb, NG)

        @block.vector
        def _(dve):
            vec = nc.vector
            count = 0

            def link(ins):
                nonlocal count
                count += 1
                ins.then_inc(chain_v, 1)
                dve.wait_ge(chain_v, count)

            def tt(o, a, b, op):
                return vec.tensor_tensor(o, a, b, op)

            def ts(o, a, s1, s2, op0, op1=None):
                return vec.tensor_scalar(o, a, s1, s2, op0, op1) if op1 is not None else vec.tensor_scalar(o, a, s1, None, op0)

            link(vec.memset(ad_e[:, :, :], 0.0))
            vec.memset(src_i[:, T:T + SLOTS * CT], 0).then_inc(zero_ready, 1)
            link(vec.memset(eaT[NRBF:NRBF + 1, :, :], 1.0))
            link(vec.memset(ones_row[:, :], 1.0))
            link(vec.memset(S[SLOTS - 1][:, :], 0.0))
            link(vec.memset(V[:, 0:1], 0.0))
            link(vec.memset(V2[:, 0:1], 0.0))
            link(vec.memset(mV[:, 0:1], -BIG))
            link(vec.memset(dV[:, 0:1], 0.0))
            link(vec.memset(mbuf[:, :, :], 0.0))
            dve.wait_ge(setup_in, 16 * N_SETUP)
            dve.wait_ge(ready_const, 1)
            link(vec.tensor_copy(dst_f[:, :], dst_i[:, :]))
            link(ts(small[:, 1:2], dst_f[:, T - 1:T], 1.0, None, ALU.add))
            ts(small[:, 2:3], dst_f[:, 0:1], 1.0, None, ALU.add).then_inc(part_ready, 1)
            link(tt(keep01[:, 1:T], dst_f[:, 1:T], dst_f[:, 0:T - 1], ALU.is_equal))
            link(vec.memset(keep01[:, 0:1], 0.0))
            link(ts(keepM[:, :], keep01[:, :], 2.0, -1.0, ALU.mult, ALU.add))
            link(ts(keepM[:, :], keepM[:, :], BIG, None, ALU.mult))
            dve.wait_ge(part_rows, 1)
            lastB = xT[:, 0:P]
            link(vec.tensor_copy(lastB, PS[:, 5, 0:P]))
            link(vec.tensor_copy(small[:, 3:4], PS[:, 5, P:P + 1]))
            link(ts(nd(N_T0), nval[:, :], 1.0, None, ALU.add))
            cmp = X[:, :, :]
            link(tt(cmp, lastB.unsqueeze(1).to_broadcast([P, NB, P]), nd(N_T0).unsqueeze(2).to_broadcast([P, NB, P]), ALU.is_le))
            link(vec.tensor_reduce(nd(N_P), cmp, AX.X, ALU.add))
            link(ts(nd(N_P), nd(N_P), float(P - 1), None, ALU.min))
            vec.tensor_copy(nodes_i[:, 2, :], nd(N_P)).then_inc(p_ready, 1)
            link(tt(small[:, 4:5], small[:, 2:3], small[:, 3:4], ALU.is_equal))
            link(tt(small[:, 5:6], small[:, 1:2], small[:, 2:3], ALU.is_equal))
            tt(small[:, 8:9], small[:, 4:5], small[:, 5:6], ALU.mult).then_inc(flag_ready, 1)
            eqf = aggT[:, 0:T]
            link(ts(eqf, dst_f[:, :], dst_f[:, 0:1], None, ALU.is_equal))
            link(vec.tensor_reduce(small[:, 6:7], eqf, AX.X, ALU.add))
            link(tt(small[:, 7:8], small[:, 6:7], small[:, 0:1], ALU.add))
            link(ts(small[:, 7:8], small[:, 7:8], -1.0, None, ALU.add))
            link(ts(small[:, 9:10], small[:, 4:5], -float(SKIP), float(SKIP), ALU.mult, ALU.add))
            link(tt(small[:, 9:10], small[:, 9:10], small[:, 7:8], ALU.add))
            link(vec.tensor_copy(edge_i[:, 0:1], small[:, 7:8]))
            link(vec.tensor_copy(edge_i[:, 1:2], small[:, 9:10]))
            link(vec.tensor_copy(edge_i[:, 2:3], dst_f[:, 0:1]))
            dve.wait_ge(flag_rows, 1)
            link(vec.tensor_copy(kB01[:, :], PS[:, 5, 2 * P:3 * P]))
            link(ts(kBM[:, :], kB01[:, :], 2.0, -1.0, ALU.mult, ALU.add))
            link(ts(kBM[:, :], kBM[:, :], BIG, None, ALU.mult))
            for j, h in enumerate((4, 4, 1)):
                for q in range(2):
                    o = att_m[:, j, q * h:(q + 1) * h]
                    if h == 4:
                        ins = ts(o, head_of[:, :], att[:, j, q:q + 1], None, ALU.mult)
                    else:
                        ins = vec.tensor_copy(o, att[:, j, q:q + 1])
            ins.then_inc(att_ready, 1)
            mask = aggT[:, T:2 * T]
            same = aggT[:, 2 * T:3 * T]
            link(ts(mask, gate[:, :], 5.0, None, ALU.is_lt))
            link(vec.tensor_copy(same, src_i[:, 0:T]))
            link(tt(same, same, dst_f[:, :], ALU.not_equal))
            link(tt(mask, mask, same, ALU.mult))
            link(ts(same.bitcast(i32), gate[:, :], 0.1, None, ALU.mult))
            link(ts(same, same.bitcast(i32), -10.0, None, ALU.mult))
            link(tt(gate[:, :], gate[:, :], same, ALU.add))
            link(ts(same, gate[:, :], -1.0, None, ALU.mult))
            link(tt(gate[:, :], gate[:, :], same, ALU.max))
            link(ts(same, gate[:, :], -1.0, 10.0, ALU.mult, ALU.add))
            link(tt(gate[:, :], gate[:, :], same, ALU.min))
            ts(gate[:, :], gate[:, :], -float(np.pi) / 5.0, float(np.pi) / 2.0, ALU.mult, ALU.add).then_inc(cos_arg, 1)
            dve.wait_ge(cos_done, 1)
            link(ts(gate[:, :], gate[:, :], 0.5, 0.5, ALU.mult, ALU.add))
            link(tt(gate[:, :], gate[:, :], mask, ALU.mult))
            for b in range(NB):
                dve.wait_ge(ends_rows[b % SLOTS], 16 * (b // SLOTS + 1))
                o = R[:, (b % 2) * T:(b % 2 + 1) * T]
                ts(o, G[b % SLOTS][:, 0:T].bitcast(i32), nval[:, b:b + 1], None, ALU.is_le).then_inc(ends_used, 1)
                dve.wait_ge(ends_used, b + 1)
                link(vec.tensor_reduce(nodes[:, N_CNT, b:b + 1], o, AX.X, ALU.add))
            link(ts(nd(N_T0), nd(N_P), float(T), None, ALU.mult))
            link(tt(nd(N_CNT), nd(N_CNT), nd(N_T0), ALU.add))
            link(vec.memset(nodes[:, N_T1, 0:1], 0.0))
            vec.tensor_copy(nodes[:, N_T1, 1:NB], nodes[:, N_CNT, 0:NB - 1]).then_inc(cnt_ready, 1)
            dve.wait_ge(start_ps, 1)
            dve.wait_ge(cnt_ready, 1)
            link(vec.tensor_copy(nd(N_START), PS[:, 6, 0:NB]))
            link(tt(nd(N_DEG), nd(N_CNT), nd(N_START), ALU.subtract))
            link(ts(nd(N_HAS), nd(N_DEG), 1.0, None, ALU.min))
            link(ts(nd(N_END), nd(N_CNT), -1.0, 0.0, ALU.add, ALU.max))
            link(vec.tensor_copy(nodes_i[:, 0, :], nd(N_END)))
            link(ts(nd(N_T1), nd(N_HAS), -float(SKIP), float(SKIP), ALU.mult, ALU.add))
            link(tt(nd(N_T1), nd(N_T1), nd(N_START), ALU.add))
            vec.tensor_copy(nodes_i[:, 1, :], nd(N_T1)).then_inc(nodes_ready, 1)
            ts(nd(N_T0), nd(N_DEG), 1.0, None, ALU.add).then_inc(deg_ready, 1)
            dve.wait_ge(dinv_root, 1)
            link(vec.reciprocal(nd(N_DINV), nd(N_T0)))
            has = nd(N_HAS).unsqueeze(2).to_broadcast([P, NB, D])

            n_ln = 0

            def layer_norm(src, dst, done):
                nonlocal n_ln
                n_ln += 1
                for b in range(NB):
                    ins = vec.bn_stats(stats[:, b, :], src[:, b, :])
                link(ins)
                for b in range(NB):
                    ins = vec.bn_aggr(mv[:, b, :], stats[:, b, :])
                link(ins)
                ts(mv[:, :, 1], mv[:, :, 1], 1e-5, None, ALU.add).then_inc(ln_var, 1)
                link(tt(src[:, :, :], src[:, :, :], mv[:, :, 0:1].to_broadcast([P, NB, D]), ALU.subtract))
                dve.wait_ge(ln_std, n_ln)
                link(vec.reciprocal(stats[:, :, 0], mv[:, :, 1]))
                tt(dst[:, :, :], src[:, :, :], stats[:, :, 0:1].to_broadcast([P, NB, D]), ALU.mult).then_inc(done, 1)
                return n_ln

            def dense_out(d):
                hx = rows(Hx, WIDTH[d])
                for g in range(NG):
                    bs = blocks(g)
                    dve.wait_ge(h_ps, NG * d + g + 1)
                    p = ps_rows(2 + (NG * d + g) % 2, g, WIDTH[d])
                    o = hx[:, bs[0]:bs[-1] + 1, :]
                    if d in (5, 6, 7):
                        ins = vec.tensor_copy(o, p)
                    elif d >= 9:
                        ins = tt(o, p, nodes[:, N_DINV, bs[0]:bs[-1] + 1].unsqueeze(2).to_broadcast([P, len(bs), D]), ALU.mult)
                    else:
                        ins = tt(o, p, bias[:, d:d + 1, :].to_broadcast([P, len(bs), D]), ALU.add)
                    ins.then_inc(h_sb, 1)

            for k, ps in enumerate(PASSES):
                kind, ct, w, H, rw, base = ps["kind"], ps["CT"], ps["W"], ps["H"], ps["RW"], ps["slot_base"]
                it = ps["ITER"]
                d = DENSE_OF_PASS[k]
                if k == 8:
                    dense_out(CF)
                    dve.wait_ge(h_sb, NG * (CF + 1))
                    link(tt(X[:, :, :], rows(Hx, D), XRES[:, :, :], ALU.add))
                    layer_norm(X, XRES, x_ready)
                if k >= 1:
                    dve.wait_ge(table_stored, 16 * k)
                    if k > 5 and k <= 8:
                        dve.wait_ge(ad_scattered, 16 * NB * (k - 5))
                dense_out(d)
                if k == 1:
                    dve.wait_ge(aggT_ps, NG)
                if H:
                    j = k - 5
                    dve.wait_ge(ad_loaded, 16 * (j + 1))
                    dve.wait_ge(ad_first, 16 * (j + 1))
                    rr = R[:, 0:T * H].rearrange("p (t h) -> p t h", h=H)
                    link(vec.tensor_copy(rr[:, 0, :], ad0[:, D + H:D + 2 * H]))
                    for h in range(H):
                        link(vec.tensor_tensor_scan(ad_e[:, h, :], keep01[:, :], rr[:, :, h], 0.0, ALU.mult, ALU.add))

                per_chunk = {"first": 3 * ct - 1, "max": ct - 1, "sum": ct - 1,
                             "gat": (7 + 2 * H + 2 * ct - 1) if H == 4 else (7 + 2 * H + ct - 1)}[kind]
                loop0 = count

                def chunk(i, b, first):
                    c = i * SLOTS + b
                    n = 0
                    c0 = loop0 + c * per_chunk

                    def step(ins):
                        nonlocal n
                        n += 1
                        ins.then_inc(chain_v, 1)
                        return n

                    def after(m):
                        dve.wait_ge(chain_v, c0 + m)

                    gr, sr = g_rows(b, ps), s_rows(b, ps)
                    pb = (b - 1) % SLOTS
                    prev = s_rows(pb, ps)[:, ct - 1, :]
                    prev_cf = s_cf(pb)[:, CT0 - 1, :] if kind == "first" else None
                    dve.wait_ge(gathered[b], ps["gath_base"] + 16 * ct * (i + 1))
                    if not (k == 0 and first):
                        n_st = 2 * i if kind == "first" else base + i + PASSES[0]["ITER"]
                        dve.wait_ge(run_stored[b], 16 * n_st)
                    if b:
                        dve.wait_ge(chunk_done[pb], base + i + 1)
                    elif not (k == 0 and first):
                        dve.wait_ge(chunk_done[pb], base + i)
                    k01 = keep01[:, bass.ds(c * ct, ct)]
                    kM = keepM[:, bass.ds(c * ct, ct)]

                    def fold(o, p, kk, g, op0, op1):
                        return vec.scalar_tensor_tensor(o, p, kk, g, op0, op1)

                    def one(buf, t):
                        return buf[:, bass.ds(c * ct + t, 1)]

                    if kind in ("max", "sum"):
                        kk, o0, o1 = (keepM, ALU.min, ALU.max) if kind == "max" else (keep01, ALU.mult, ALU.add)
                        for t in range(ct):
                            ins = fold(sr[:, t, :], sr[:, t - 1, :] if t else prev, one(kk, t), gr[:, t, :], o0, o1)
                            if t < ct - 1:
                                after(step(ins))
                        ins.then_inc(chunk_done[b], 1)
                    elif kind == "first":
                        sc = s_cf(b)
                        dve.wait_ge(filt_ps, c + 1)
                        m_prev = a_prev = None
                        for t in range(ct):
                            f = PS[:, 2 + 2 * (b % 2) + t // 4, (t % 4) * P:(t % 4 + 1) * P]
                            m = step(vec.scalar_tensor_tensor(gr[:, t, D:2 * D], f, one(gate, t), gr[:, t, D:2 * D], ALU.mult, ALU.mult))
                            if a_prev:
                                after(a_prev)
                            a_prev = step(fold(sr[:, t, :], sr[:, t - 1, :] if t else prev, one(keepM, t), gr[:, t, 0:D], ALU.min, ALU.max))
                            after(m)
                            if t == ct - 1:
                                after(a_prev)
                            ins = fold(sc[:, t, :], sc[:, t - 1, :] if t else prev_cf, one(keep01, t), gr[:, t, D:2 * D], ALU.mult, ALU.add)
                            if t < ct - 1:
                                step(ins)
                        ins.then_inc(chunk_done[b], 1)
                    else:
                        v4 = lambda a: a[:, :, 0:H]
                        z, e = v4(zc), v4(ec)
                        mb = mbuf[:, :, 0:H]
                        adv = ad_e[:, 0:H, bass.ds(c * ct, ct)].rearrange("p h t -> p t h")
                        step(vec.tensor_copy(mb[:, 0, :], mb[:, ct, :]))
                        after(step(tt(z, gr[:, :, D:D + H], adv, ALU.add)))
                        after(step(vec.scalar_tensor_tensor(e, z, 0.2, z, ALU.mult, ALU.max)))
                        for h in range(H):
                            m = step(vec.tensor_tensor_scan(mb[:, 1:ct + 1, h], kM, e[:, :, h], mb[:, 0, h:h + 1], ALU.min, ALU.max))
                        after(m)
                        after(step(tt(v4(mp), mb[:, 0:ct, :], kM.unsqueeze(2).to_broadcast([P, ct, H]), ALU.min)))
                        m = step(tt(dc[:, 1, :, 0:H], v4(mp), mb[:, 1:ct + 1, :], ALU.subtract))
                        after(m)
                        tt(dc[:, 0, :, 0:H], e, mb[:, 1:ct + 1, :], ALU.subtract).then_inc(soft_arg, 1)
                        step(vec.tensor_copy(sr[:, :, D + H:D + 2 * H], mb[:, 1:ct + 1, :]))
                        dve.wait_ge(soft_exp, (k - 5) * SLOTS * it + c + 1)
                        for h in range(H):
                            step(vec.tensor_tensor_scan(sr[:, :, D + h], pc[:, 1, :, h], pc[:, 0, :, h],
                                                        prev[:, D + h:D + h + 1], ALU.mult, ALU.add))
                        C = D // H
                        gh = gr[:, :, 0:D].rearrange("p t (h c) -> p t h c", h=H)
                        after(step(tt(gh, gh, pc[:, 0, :, 0:H].unsqueeze(3).to_broadcast([P, ct, H, C]), ALU.mult)))
                        for t in range(ct):
                            p = (sr[:, t - 1, :] if t else prev)[:, 0:D]
                            o = sr[:, t, 0:D]
                            if H == 4:
                                hv = lambda a: a.rearrange("p (h c) -> p h c", h=H)
                                after(step(tt(hv(tmpr[:, :]), hv(p), pc[:, 1, t, 0:H].unsqueeze(2).to_broadcast([P, H, C]), ALU.mult)))
                                ins = tt(o, tmpr[:, :], gr[:, t, 0:D], ALU.add)
                            else:
                                ins = fold(o, p, pc[:, 1, t, 0:1], gr[:, t, 0:D], ALU.mult, ALU.add)
                            if t < ct - 1:
                                after(step(ins))
                        ins.then_inc(chunk_done[b], 1)
                    assert n == per_chunk, (kind, n, per_chunk)

                for b in range(SLOTS):
                    chunk(0, b, True)
                    if kind == "first":
                        dve.wait_ge(chunk_done[b], 1)
                        dve.sem_inc(filt_used, 1)
                with dve.Fori(1, it) as i:
                    for b in range(SLOTS):
                        chunk(i, b, False)
                        if kind == "first":
                            dve.wait_ge(chunk_done[b], i + 1)
                            dve.sem_inc(filt_used, 1)
                count = loop0 + per_chunk * SLOTS * it

                dve.wait_ge(tail_T, k + 1)
                if kind in ("first", "max"):
                    ins = vec.tensor_tensor_scan(V[:, 1:P + 1], kBM[:, :], PS[:, 6, 0:P], -BIG, ALU.min, ALU.max)
                    if kind == "first":
                        link(ins)
                        ins = vec.tensor_tensor_scan(V2[:, 1:P + 1], kB01[:, :], PS[:, 6, P:2 * P], 0.0, ALU.mult, ALU.add)
                    ins.then_inc(tail_V, 1)
                elif kind == "sum":
                    vec.tensor_tensor_scan(V[:, 1:P + 1], kB01[:, :], PS[:, 6, 0:P], 0.0, ALU.mult, ALU.add).then_inc(tail_V, 1)
                else:
                    mT = PS[0:H, 6, 2 * P:3 * P]
                    link(vec.tensor_tensor_scan(mV[0:H, 1:P + 1], kBM[0:H, :], mT, -BIG, ALU.min, ALU.max))
                    link(tt(prevm[0:H, :], kBM[0:H, :], mV[0:H, 0:P], ALU.min))
                    link(tt(DD[0:H, 0, :], mT, mV[0:H, 1:P + 1], ALU.subtract))
                    tt(DD[0:H, 1, :], prevm[0:H, :], mV[0:H, 1:P + 1], ALU.subtract).then_inc(tail_arg, 1)
                    accT = FX2[:, 0:P]
                    link(vec.tensor_copy(accT, PS[:, 6, 0:P]))
                    dve.wait_ge(tail_B, k - 4)
                    link(tt(accT, accT, PS[:, 7, 0:P], ALU.mult))
                    link(vec.tensor_tensor_scan(V[:, 1:P + 1], PS[:, 7, P:2 * P], accT, 0.0, ALU.mult, ALU.add))
                    link(tt(denT[0:H, :], PS[0:H, 6, P:2 * P], EE[0:H, 0, :], ALU.mult))
                    vec.tensor_tensor_scan(dV[0:H, 1:P + 1], EE[0:H, 1, :], denT[0:H, :], 0.0, ALU.mult, ALU.add).then_inc(tail_V, 1)
                dve.wait_ge(tail_C, k + 1)
                dve.wait_ge(fix_in, 16 * (k + 2))
                if kind == "first":
                    link(tt(FX2[:, 0:D], FX2[:, 0:D], PS[:, 6, P:2 * P], ALU.add))
                if not H:
                    tt(FX[:, 0:D], FX[:, 0:D], PS[:, 6, 0:P], ALU.add if kind == "sum" else ALU.max).then_inc(fix_new, 1)
                else:
                    fm, cm = FX[:, D + H:D + 2 * H], PS[:, 6, 2 * P:2 * P + H]
                    link(tt(fxm[:, 2, 0:H], fm, cm, ALU.max))
                    link(tt(fxm[:, 0, 0:H], fm, fxm[:, 2, 0:H], ALU.subtract))
                    tt(fxm[:, 1, 0:H], cm, fxm[:, 2, 0:H], ALU.subtract).then_inc(fix_arg, 1)
                    dve.wait_ge(fix_exp, k - 4)
                    hv = lambda a: a.rearrange("p (h c) -> p h c", h=H)
                    bc = lambda a: a.unsqueeze(2).to_broadcast([P, H, D // H])
                    link(tt(hv(FX[:, 0:D]), hv(FX[:, 0:D]), bc(fxe[:, 0, 0:H]), ALU.mult))
                    link(tt(hv(FX2[:, 0:D]), hv(PS[:, 6, 0:P]), bc(fxe[:, 1, 0:H]), ALU.mult))
                    link(tt(FX[:, 0:D], FX[:, 0:D], FX2[:, 0:D], ALU.add))
                    link(tt(FX[:, D:D + H], FX[:, D:D + H], fxe[:, 0, 0:H], ALU.mult))
                    link(tt(FX2[:, D:D + H], PS[:, 6, P:P + H], fxe[:, 1, 0:H], ALU.mult))
                    link(tt(FX[:, D:D + H], FX[:, D:D + H], FX2[:, D:D + H], ALU.add))
                    vec.tensor_copy(fm, fxm[:, 2, 0:H]).then_inc(fix_new, 1)

                dve.wait_ge(end_in, end_gathers(k))
                rv = rows(R, w)
                if k == 0:
                    tt(AGG[:, :, :], AGG[:, :, :], has, ALU.mult).then_inc(agg_ready, 1)
                if kind in ("first", "max"):
                    if k < NL0 - 1:
                        tt(X[:, :, :], rv, has, ALU.mult).then_inc(agg_ready, 1)
                    else:
                        link(tt(X[:, :, :], rv, has, ALU.mult))
                        link(tt(X[:, :, :], X[:, :, :], XRES[:, :, :], ALU.add))
                        layer_norm(X, XRES, x_ready)
                elif kind == "sum":
                    link(tt(X[:, :, :], rv, has, ALU.mult))
                    link(tt(X[:, :, :], X[:, :, :], rows(Hx, D), ALU.add))
                    link(tt(X[:, :, :], X[:, :, :], nd(N_DINV).unsqueeze(2).to_broadcast([P, NB, D]), ALU.mult))
                    last = tt(X[:, :, :], X[:, :, :], bias[:, d:d + 1, :].to_broadcast([P, NB, D]), ALU.add)
                    if k == 8:
                        last.then_inc(x_ready, 1)
                    else:
                        link(last)
                        link(tt(XRES[:, :, :], X[:, :, :], XRES[:, :, :], ALU.add))
                        layer_norm(XRES, X, out_ready)
                else:
                    hx = rows(Hx, rw)
                    nh = NB * H
                    v3 = lambda q: na[:, q, 0:nh].rearrange("p (b h) -> p b h", h=H)
                    hasH = nd(N_HAS).unsqueeze(2).to_broadcast([P, NB, H])
                    link(tt(v3(0), hx[:, :, D:D + H], hx[:, :, D + H:D + 2 * H], ALU.add))
                    link(vec.scalar_tensor_tensor(v3(1), v3(0), 0.2, v3(0), ALU.mult, ALU.max))
                    link(tt(v3(6), rv[:, :, D + H:D + 2 * H], hasH, ALU.mult))
                    link(ts(v3(7), hasH, BIG, -BIG, ALU.mult, ALU.add))
                    link(tt(v3(6), v3(6), v3(7), ALU.add))
                    link(tt(v3(0), v3(6), v3(1), ALU.max))
                    link(tt(v3(2), v3(6), v3(0), ALU.subtract))
                    tt(v3(3), v3(1), v3(0), ALU.subtract).then_inc(post_arg, 1)
                    dve.wait_ge(post_exp, k - 4)
                    link(tt(v3(4), v3(4), hasH, ALU.mult))
                    link(tt(v3(7), rv[:, :, D:D + H], v3(4), ALU.mult))
                    link(tt(v3(7), v3(7), v3(5), ALU.add))
                    link(ts(v3(7), v3(7), 1e-16, None, ALU.add))
                    link(vec.reciprocal(v3(7), v3(7)))
                    link(tt(v3(4), v3(4), v3(7), ALU.mult))
                    link(tt(v3(5), v3(5), v3(7), ALU.mult))
                    C = D // H
                    v4d = lambda a: a.rearrange("p b (h c) -> p b h c", h=H)
                    bc = lambda q: v3(q).unsqueeze(3).to_broadcast([P, NB, H, C])
                    link(tt(v4d(X[:, :, :]), v4d(rv[:, :, 0:D]), bc(4), ALU.mult))
                    link(tt(v4d(rv[:, :, 0:D]), v4d(hx[:, :, 0:D]), bc(5), ALU.mult))
                    link(tt(X[:, :, :], X[:, :, :], rv[:, :, 0:D], ALU.add))
                    link(tt(X[:, :, :], X[:, :, :], bias[:, d:d + 1, :].to_broadcast([P, NB, D]), ALU.add))
                    if k < 7:
                        ts(X[:, :, :], X[:, :, :], 0.0, None, ALU.max).then_inc(x_ready, 1)
                    else:
                        link(tt(X[:, :, :], X[:, :, :], XRES[:, :, :], ALU.add))
                        layer_norm(X, XRES, x_ready)


def kernel(**inputs):
    import concourse.bacc as bacc
    from concourse.bass_utils import run_bass_kernel_spmd

    def padded(a, n, fill=0):
        a = np.asarray(a)
        return np.concatenate([a, np.full((n - a.shape[0],) + a.shape[1:], fill, a.dtype)])

    arrays = {name: np.asarray(a) for name, a in inputs.items()}
    for name, n, fill in (("x", NP_, 0), ("node_type_100", NP_, 0), ("src", EP, 0), ("dst", EP, N),
                          ("edge_weight", EP, 0), ("edge_attr_64", EP, 0)):
        arrays[name] = padded(arrays[name], n, fill)
    nc = bacc.Bacc("TRN2", target_bir_lowering=False, num_devices=1)
    feed, aps = {}, {}
    for name, a in arrays.items():
        feed[f"in_{name}"] = np.ascontiguousarray(a)
        aps[name] = nc.dram_tensor(f"in_{name}", a.shape, mybir.dt.from_np(a.dtype), kind="ExternalInput").ap()
    out = nc.dram_tensor("out_nodes", (N, D), mybir.dt.float32, kind="ExternalOutput").ap()
    program(nc, aps, out)
    r = run_bass_kernel_spmd(nc, [feed], core_ids=[0])
    return r.results[0]["out_nodes"]
```

```python
from contextlib import ExitStack

import numpy as np
import concourse.bass as bass
from concourse import mybir

P = 128
N, E, D = 3125, 100000, 128
NB = -(-N // P)
NP_ = NB * P
T = 784
EP = P * T
SLOTS = 4
CT = 14
CT0 = 7
NRBF, NTYPE = 64, 100
SKIP = 1 << 20
BIG = 3.0e38
GB = 3
NG = -(-NB // GB)
NL0 = 5
GE = 4
NGRP = EP // (GE * P)
NITEM = NGRP + NB - 1
NSLOT = (NL0 - 1) * (T // CT)
assert NITEM <= NSLOT and T % CT == 0
CSCALE = 2.0 ** 40
GSZ, SSZ = 1904, 1904

PASSES = [dict(kind="first", H=0, RW=2 * D, W=D, CT=CT0)]
PASSES += [dict(kind="max", H=0, RW=D, W=D, CT=CT) for _ in range(NL0 - 1)]
PASSES += [dict(kind="gat", H=h, RW=D + 2 * h, W=D + 2 * h, CT=CT) for h in (4, 4)]
NPASS = len(PASSES)
for k, ps in enumerate(PASSES):
    ps["ITER"] = T // ps["CT"] // SLOTS
    ps["slot_base"] = sum(q["ITER"] for q in PASSES[:k])
    ps["gath_base"] = 16 * (T // SLOTS) * k
    ps["chunk_base"] = SLOTS * ps["slot_base"]
CF = 8
NDENSE = 11
DENSE_OF_PASS = [0, 1, 2, 3, 4, 5, 6]
GAT3 = 7
WIDTH = [D] * 5 + [D + 8, D + 8, D + 2] + [D] * 3


def program(nc, A, out):
    fp32, i32, i16, bf16 = mybir.dt.float32, mybir.dt.int32, mybir.dt.int16, mybir.dt.bfloat16
    ALU, ACT, AX = mybir.AluOpType, mybir.ActivationFunctionType, mybir.AxisListType
    ctx = ExitStack()
    with ctx:
        def sb(name, shape, dt=fp32):
            return ctx.enter_context(nc.sbuf_tensor(name, shape, dt))

        def sem(name):
            return ctx.enter_context(nc.semaphore(name))

        def dram(name, shape):
            return nc.dram_tensor(name, shape, fp32, kind="Internal").ap()

        table = {w: dram(f"table{w}", (NP_, w)) for w in (2 * D, D, D + 8)}
        runs = {w: dram(f"runs{w}", (EP, w)) for w in (D, D + 8)}
        adj = dram("adj", (NP_, NP_))
        runs_cf = dram("runs_cf", (EP, D))
        starts_ad = {h: dram(f"starts_ad{h}", (EP, h)) for h in (4,)}

        src_i = sb("src_i", [P, T + SLOTS * CT], i32)
        dst_f = sb("dst_f", [P, T])
        keep01 = sb("keep01", [P, T])
        keepM = sb("keepM", [P, T])
        gate = sb("gate", [P, T])
        idx = [sb(f"idx{b}", [P, CT], i32) for b in range(SLOTS)]
        G_all = sb("G_all", [P, SLOTS * GSZ])
        G = [G_all[:, b * GSZ:(b + 1) * GSZ] for b in range(SLOTS)]
        S_all = sb("S_all", [P, SLOTS * SSZ])
        S = [S_all[:, b * SSZ:(b + 1) * SSZ] for b in range(SLOTS)]
        X = sb("X", [P, NB, D])
        XRES = sb("XRES", [P, NB, D])
        R = sb("R", [P, NB * (D + 8)])
        Hx = sb("Hx", [P, NB * (D + 8)])
        dst_i = Hx[:, 0:T].bitcast(i32)
        xT = sb("xT", [P, NP_])
        aggT = sb("aggT", [P, NP_])
        AGG = S_all[:, 0:NB * D].rearrange("p (b d) -> p b d", d=D)
        ad_e = sb("ad_e", [P, 4, NP_ // 4])
        ident = sb("ident", [P, P])
        shift = sb("shift", [P, P])
        wrap = sb("wrap", [P, P])
        WR = sb("WR", [P, NDENSE + 1, D + 8])
        bias = sb("bias", [P, NDENSE, D])
        w_raw = aggT[:, 3 * T:3 * T + NL0 * D].rearrange("p (l d) -> p l d", d=D)
        wT = sb("wT", [P, D])
        att = sb("att", [P, 3, 2])
        att_m = sb("att_m", [P, 3, 8])
        head_of = sb("head_of", [P, 4])
        head_rows = sb("head_rows", [4, P])
        ones_row = sb("ones_row", [1, P])
        wd = sb("wd", [NRBF + 1, D])
        aux = sb("aux", [P, 2 * CT0 * P + SLOTS * CT0 * NRBF])
        eaT_all = aux[:, 0:2 * CT0 * P]
        eaT = eaT_all[0:NRBF + 1, :].rearrange("p (h n) -> p h n", h=2)
        ea_all = aux[:, 2 * CT0 * P:]
        ea = [ea_all[:, b * CT0 * NRBF:(b + 1) * CT0 * NRBF] for b in range(SLOTS)]
        item_src = eaT_all[:, 0:GE * NSLOT].rearrange("p (t i) -> p t i", t=GE)
        item_dst = eaT_all[:, GE * NSLOT:2 * GE * NSLOT].rearrange("p (t i) -> p t i", t=GE)
        item_keep = gate[:, 0:NSLOT]
        item_blk = gate[:, NSLOT:2 * NSLOT].bitcast(i32)
        item_last = gate[:, 2 * NSLOT:3 * NSLOT].bitcast(i32)
        iota_n = ea_all[:, 0:NP_ // 2].bitcast(i16)
        src_hot = [buf[:, j * (NP_ // 2):(j + 1) * (NP_ // 2)].bitcast(bf16) for buf in (xT, R) for j in range(2)]
        dst_hot = sb("dst_hot", [P, GE, P], bf16)
        counts = ad_e[:, :, :].rearrange("p h t -> p (h t)")
        rows_a = [S_all[:, 2 * SSZ + q * GE * P:2 * SSZ + (q + 1) * GE * P] for q in range(3)] + [S[3][:, 0:GE * P]]
        big_max = xT[:, :]
        dst_row = [S_all[:, j * NP_:(j + 1) * NP_] for j in range(2)]
        pos_exp = [R[:, 0:NP_], xT[:, :]]
        soft_w = [counts, X[:, :, :].rearrange("p b d -> p (b d)")]
        den_sum = aux[:, 0:NP_]
        nval = sb("nval", [P, NB])
        ztype = sb("ztype", [P, NB], i32)
        small = sb("small", [P, 64])
        nodes = sb("nodes", [P, 16, NB])
        nodes_i = sb("nodes_i", [P, 3, NB], i32)
        edge_i = sb("edge_i", [P, 5], i32)
        kB01 = sb("kB01", [P, P])
        kBM = sb("kBM", [P, P])
        V = sb("V", [P, P + 1])
        V2 = sb("V2", [P, P + 1])
        mV = sb("mV", [4, P + 1])
        dV = sb("dV", [4, P + 1])
        DD = sb("DD", [4, 2, P])
        EE = sb("EE", [4, 2, P])
        prevm = sb("prevm", [4, P])
        denT = sb("denT", [4, P])
        FX = sb("FX", [P, D + 8])
        FX2 = sb("FX2", [P, D + 8])
        ad0 = sb("ad0", [P, D + 8])
        fxm = sb("fxm", [P, 3, 4])
        fxe = sb("fxe", [P, 2, 4])
        zc = sb("zc", [P, CT, 4])
        ec = sb("ec", [P, CT, 4])
        mbuf = sb("mbuf", [P, CT + 1, 4])
        mp = sb("mp", [P, CT, 4])
        dc = sb("dc", [P, 2, CT, 4])
        pc = sb("pc", [P, 2, CT, 4])
        tmpr = sb("tmpr", [P, D])
        stats = ea_all[:, NP_ // 2:NP_ // 2 + 6 * NB].rearrange("p (b s) -> p b s", s=6)
        mv = sb("mv", [P, NB, 2])
        na = ea_all[:, 0:8 * NB * 4].rearrange("p (q n) -> p q n", q=8)
        PS = ctx.enter_context(nc.psum_tensor("PS", [P, 8, 512], fp32))

        (N_CNT, N_END, N_START, N_DEG, N_HAS, N_DINV, N_P, N_T0, N_T1, N_FREE, N_HI, N_BLK) = range(12)
        (N_POS, N_MAX, N_ROW1, N_ROW2, N_NEG, N_SELF, N_INV, N_E1) = (N_CNT, N_END, N_START, N_P, N_T0, N_T1, N_FREE, N_HI)
        def nd(i):
            return nodes[:, i, :]

        setup_in = sem("setup_in")
        ready_const = sem("ready_const")
        chain_v = sem("chain_v")
        chain_g = sem("chain_g")
        ends_rows = [sem(f"ends_rows{b}") for b in range(SLOTS)]
        ends_used = sem("ends_used")
        emb_rows = sem("emb_rows")
        emb_stored = sem("emb_stored")
        part_ready = sem("part_ready")
        part_rows = sem("part_rows")
        flag_ready = sem("flag_ready")
        flag_rows = sem("flag_rows")
        p_ready = sem("p_ready")
        cnt_ready = sem("cnt_ready")
        start_ps = sem("start_ps")
        nodes_ready = sem("nodes_ready")
        fix_ready = sem("fix_ready")
        deg_ready = sem("deg_ready")
        dinv_root = sem("dinv_root")
        cos_arg = sem("cos_arg")
        go = sem("go")
        cos_done = sem("cos_done")
        w_ps = sem("w_ps")
        w_sb = sem("w_sb")
        att_ready = sem("att_ready")
        zero_ready = sem("zero_ready")
        zero_stored = sem("zero_stored")
        x_ready = sem("x_ready")
        xT_ps = sem("xT_ps")
        xT_sb = sem("xT_sb")
        h_ps = sem("h_ps")
        h_sb = sem("h_sb")
        agg_ready = sem("agg_ready")
        aggT_ps = sem("aggT_ps")
        aggT_sb = sem("aggT_sb")
        table_stored = sem("table_stored")
        ad_scattered = sem("ad_scattered")
        ad_first = sem("ad_first")
        ad_loaded = sem("ad_loaded")
        idx_staged = [sem(f"idx_staged{b}") for b in range(SLOTS)]
        gathered = [sem(f"gathered{b}") for b in range(SLOTS)]
        chunk_done = [sem(f"chunk_done{b}") for b in range(SLOTS)]
        run_stored = [sem(f"run_stored{b}") for b in range(SLOTS)]
        ea_in = [sem(f"ea_in{b}") for b in range(SLOTS)]
        ea_ps = sem("ea_ps")
        ea_sb = sem("ea_sb")
        filt_ps = sem("filt_ps")
        filt_used = sem("filt_used")
        soft_arg = sem("soft_arg")
        soft_exp = sem("soft_exp")
        tail_T = sem("tail_T")
        tail_V = sem("tail_V")
        tail_C = sem("tail_C")
        tail_B = sem("tail_B")
        tail_arg = sem("tail_arg")
        tail_exp = sem("tail_exp")
        fix_in = sem("fix_in")
        fix_arg = sem("fix_arg")
        fix_exp = sem("fix_exp")
        fix_new = sem("fix_new")
        fix_out = sem("fix_out")
        end_in = sem("end_in")
        post_arg = sem("post_arg")
        post_exp = sem("post_exp")
        ln_var = sem("ln_var")
        ln_std = sem("ln_std")
        item_idx = sem("item_idx")
        item_rows = sem("item_rows")
        item_f = sem("item_f")
        item_ps = sem("item_ps")
        item_tab = sem("item_tab")
        hi_ready = sem("hi_ready")
        hi_ps = sem("hi_ps")
        iota_ready = sem("iota_ready")
        hot_ready = sem("hot_ready")
        item_sum = sem("item_sum")
        item_added = sem("item_added")
        item_stored = sem("item_stored")
        adj_in = [sem(f"adj_in{b}") for b in range(SLOTS)]
        adj_used = sem("adj_used")
        min_ready = sem("min_ready")
        min_T = sem("min_T")
        min_one = sem("min_one")
        min_ps = sem("min_ps")
        max_ready = sem("max_ready")
        max_T = sem("max_T")
        max_used = sem("max_used")
        rows_ready = sem("rows_ready")
        rows_ps = sem("rows_ps")
        rows_sb = sem("rows_sb")
        pair_exp = sem("pair_exp")
        pair_max = sem("pair_max")
        pair_w = sem("pair_w")
        pair_mm = sem("pair_mm")
        pair_den = sem("pair_den")
        den_clear = sem("den_clear")
        self_arg = sem("self_arg")
        self_exp = sem("self_exp")
        acc_sb = sem("acc_sb")
        acc_T = sem("acc_T")
        acc_used = sem("acc_used")
        den_ps = sem("den_ps")
        gcn_ps = sem("gcn_ps")
        gcn_sb = sem("gcn_sb")
        gcn_T = sem("gcn_T")
        gcn_out = sem("gcn_out")
        out_ready = sem("out_ready")
        out_stored = sem("out_stored")

        def rows(buf, w):
            return buf[:, 0:NB * w].rearrange("p (b w) -> p b w", w=w)

        def node_rows(ap):
            return ap.rearrange("(b p) w -> p b w", p=P)

        def blocks(g):
            return range(GB * g, min(NB, GB * g + GB))

        def src_of(d):
            return XRES if d in (0, 5, 8, 9) else X

        def g_rows(b, ps):
            return G[b][:, 0:ps["CT"] * ps["RW"]].rearrange("p (t w) -> p t w", w=ps["RW"])

        def s_rows(b, ps):
            return S[b][:, 0:ps["CT"] * ps["W"]].rearrange("p (t w) -> p t w", w=ps["W"])

        def s_cf(b):
            return S[b][:, CT0 * D:2 * CT0 * D].rearrange("p (t w) -> p t w", w=D)

        def ps_rows(bank, g, w):
            return PS[:, bank, 0:w * len(blocks(g))].rearrange("p (b w) -> p b w", w=w)

        def psum_row():
            return PS[:, 0:7, :].rearrange("p k c -> p (k c)")[:, 0:NP_]

        def kind_max(ps):
            return ps["kind"] == "max"

        def adj_slot(q):
            if q < 2 * NB:
                return q % 2, q // 2 + 1
            slot, n = (q - 2 * NB) % SLOTS, (q - 2 * NB) // SLOTS + 1
            return slot, n + (NB if slot < 2 else 0)

        def adj_tile(q):
            slot = adj_slot(q)[0]
            return (G_all, S_all)[slot // 2][:, (slot % 2) * NP_:(slot % 2 + 1) * NP_]

        def adj_wait(eng, q):
            slot, n = adj_slot(q)
            eng.wait_ge(adj_in[slot], 16 * n)

        def end_gathers(k):
            return 16 * NB * (k + 2)

        block = ctx.enter_context(nc.Block())

        N_SETUP = 0

        @block.sync
        def _(sp):
            nonlocal N_SETUP
            def load(dst, src):
                nonlocal N_SETUP
                N_SETUP += 1
                sp.dma_start(dst, src).then_inc(setup_in, 16)

            load(dst_i[:, :], A["dst"].rearrange("(p t) -> p t", t=T))
            load(src_i[:, 0:T], A["src"].rearrange("(p t) -> p t", t=T))
            load(gate[:, :], A["edge_weight"].rearrange("(p t) -> p t", t=T))
            load(XRES[:, :, :], node_rows(A["x"]))
            load(w_raw[:, :, :], A["L0_gnn_Ws"].rearrange("l o d -> o l d"))
            with nc.allow_non_contiguous_dma(reason="small vectors, once"):
                load(ztype[:, :], A["node_type_100"].rearrange("(b p) -> p b", p=P))
                for j in range(3):
                    load(att[:, j, 0:1], A[f"L1_gnn_as{j + 1}"].rearrange("h (c o) -> (h c) o", o=1))
                    load(att[:, j, 1:2], A[f"L1_gnn_ad{j + 1}"].rearrange("h (c o) -> (h c) o", o=1))
            for j in range(3):
                load(WR[:, 5 + j, 0:D], A[f"L1_gnn_W{j + 1}"])
                load(bias[:, 5 + j, :], A[f"L1_gnn_b{j + 1}"].rearrange("(o d) -> o d", o=1).to_broadcast([P, D]))
            load(WR[:, 8, 0:D], A["L2_gnn_Wc"][0:D, :])
            load(WR[:, NDENSE, 0:D], A["L2_gnn_Wc"][D:2 * D, :])
            load(WR[:, 9, 0:D], A["L3_gnn_W1"])
            load(WR[:, 10, 0:D], A["L3_gnn_W2"])
            for d, n in ((8, "L2_gnn_bc"), (9, "L3_gnn_b1"), (10, "L3_gnn_b2")):
                load(bias[:, d, :], A[n].rearrange("(o d) -> o d", o=1).to_broadcast([P, D]))
            for l in range(NL0):
                load(bias[:, l, :], A["L0_gnn_bs"][l:l + 1, :].to_broadcast([P, D]))
            load(wd[0:NRBF, :], A["L2_gnn_Wd"])
            load(wd[NRBF:NRBF + 1, :], A["L2_gnn_bd"].rearrange("(o d) -> o d", o=1))
            ea_view = A["edge_attr_64"].rearrange("(p t) c -> p (t c)", t=T)

            def load_ea(c, b):
                sp.dma_start(ea[b][:, :], ea_view[:, bass.ds(c * CT0 * NRBF, CT0 * NRBF)]).then_inc(ea_in[b], 16)

            for b in range(SLOTS):
                load_ea(b, b)
            sp.wait_ge(zero_ready, 1)
            for h in (4,):
                sp.dma_start(starts_ad[h].rearrange("(p t) h -> p (t h)", t=T), ad_e[:, :, :].rearrange("p h t -> p (h t)")[:, 0:T * h]).then_inc(zero_stored, 16)
            sp.wait_ge(emb_rows, 16 * NB)
            sp.dma_start(node_rows(table[2 * D])[:, :, D:2 * D], AGG[:, :, :]).then_inc(emb_stored, 16)

            for k, ps in enumerate(PASSES):
                ct, w, H, base = ps["CT"], ps["W"], ps["H"], ps["slot_base"]
                d = DENSE_OF_PASS[k]
                sp.wait_ge(h_sb, NG * (d + 1))
                sp.dma_start(node_rows(table[ps["RW"]])[:, :, 0:WIDTH[d]], rows(Hx, WIDTH[d])).then_inc(table_stored, 16)
                if H:
                    j = k - 5
                    sp.wait_ge(ad_scattered, 16 * NB * (j + 1))
                    sp.dma_start(R[:, 0:T * H], starts_ad[H].rearrange("(p t) h -> p (t h)", t=T)).then_inc(ad_loaded, 16)
                run_view = runs[w].rearrange("(p t) w -> p (t w)", t=T)
                cf_view = runs_cf.rearrange("(p t) w -> p (t w)", t=T)

                def store_block(item):
                    blk = sp.value_load(item_blk[0:1, bass.ds(item, 1)], min_val=0, max_val=NB - 1)
                    ends = sp.value_load(item_last[0:1, bass.ds(item, 1)], min_val=0, max_val=1)
                    sp.wait_ge(item_added, item + 1)
                    sp.dma_start(adj.rearrange("(b p) d -> p b d", p=P)[:, :, bass.ds(blk * P, P)],
                                 counts.rearrange("p (b d) -> p b d", d=P), cond=ends).then_inc(item_stored, 16)

                def store(i, last=False):
                    for b in range(SLOTS):
                        c = i * SLOTS + b
                        sp.wait_ge(chunk_done[b], base + i + 1)
                        sp.dma_start(run_view[:, bass.ds(c * ct * w, ct * w)], S[b][:, 0:ct * w]).then_inc(run_stored[b], 16)
                        if ps["kind"] == "first":
                            sp.dma_start(cf_view[:, bass.ds(c * ct * w, ct * w)], S[b][:, ct * w:2 * ct * w]).then_inc(run_stored[b], 16)
                        if kind_max(ps):
                            store_block((k - 1) * SLOTS * ps["ITER"] + c)
                        if ps["kind"] == "first":
                            if not last:
                                sp.wait_ge(ea_ps, c + 1)
                                load_ea(c + SLOTS, b)

                if k == 1:
                    sp.wait_ge(item_tab, 1)
                store(0)
                with sp.Fori(1, ps["ITER"] - 1) as i:
                    store(i)
                store(ps["ITER"] - 1, last=True)
            sp.wait_ge(h_sb, NG * (GAT3 + 1))
            for q in range(4 * NB):
                if q < 2:
                    pass
                elif q < NB + 2:
                    sp.wait_ge(adj_used, q - 1)
                elif q < 2 * NB:
                    sp.wait_ge(pair_w, q - NB - 1)
                elif q < 2 * NB + SLOTS:
                    sp.wait_ge(pair_w, NB)
                else:
                    sp.wait_ge(adj_used, q - NB - SLOTS + 1)
                sp.dma_start(adj_tile(q), adj[(q % NB) * P:(q % NB + 1) * P, :]).then_inc(adj_in[adj_slot(q)[0]], 16)
            sp.wait_ge(out_ready, 1)
            full = N // P
            sp.dma_start(out[0:full * P, :].rearrange("(b p) d -> p b d", p=P), X[:, 0:full, :]).then_inc(out_stored, 16)
            sp.dma_start(out[full * P:N, :], X[0:N - full * P, full, :]).then_inc(out_stored, 16)
            sp.wait_ge(out_stored, 32)

        @block.gpsimd
        def _(gp):
            count = 0

            def link(ins):
                nonlocal count
                count += 1
                ins.then_inc(chain_g, 1)
                gp.wait_ge(chain_g, count)

            link(nc.gpsimd.memset(ident[:, :], 0.0))
            link(nc.gpsimd.memset(shift[:, :], 0.0))
            link(nc.gpsimd.memset(wrap[:, :], 0.0))
            link(nc.gpsimd.memset(head_of[:, :], 1.0))
            link(nc.gpsimd.memset(head_rows[:, :], 1.0))
            for tile, base in ((ident, 0), (shift, 1), (wrap, -(P - 1))):
                link(nc.gpsimd.affine_select(out=tile[:, :], in_=tile[:, :], compare_op=ALU.not_equal, fill=1.0,
                                             base=base, pattern=[[-1, P]], channel_multiplier=1))
            C = D // 4
            link(nc.gpsimd.affine_select(out=head_of[:, :], in_=head_of[:, :], compare_op=ALU.is_ge, fill=0.0,
                                         base=0, pattern=[[-C, 4]], channel_multiplier=1))
            link(nc.gpsimd.affine_select(out=head_of[:, :], in_=head_of[:, :], compare_op=ALU.is_ge, fill=0.0,
                                         base=C - 1, pattern=[[C, 4]], channel_multiplier=-1))
            link(nc.gpsimd.affine_select(out=head_rows[:, :], in_=head_rows[:, :], compare_op=ALU.is_ge, fill=0.0,
                                         base=0, pattern=[[1, P]], channel_multiplier=-C))
            link(nc.gpsimd.affine_select(out=head_rows[:, :], in_=head_rows[:, :], compare_op=ALU.is_ge, fill=0.0,
                                         base=C - 1, pattern=[[-1, P]], channel_multiplier=C))
            link(nc.gpsimd.iota(small[:, 0:1], pattern=[[0, 1]], base=0, channel_multiplier=T, allow_small_or_imprecise_dtypes=True))
            link(nc.gpsimd.iota(nd(N_BLK), pattern=[[1, NB]], base=0, channel_multiplier=0, allow_small_or_imprecise_dtypes=True))
            nc.gpsimd.iota(nval[:, :], pattern=[[P, NB]], base=0, channel_multiplier=1,
                           allow_small_or_imprecise_dtypes=True).then_inc(ready_const, 1)

            def gather(dst, src, ix, s):
                gp.indirect_dma_start(out=dst, out_offset=None, in_=src,
                                      in_offset=bass.IndirectOffsetOnAxis(ap=ix, axis=0)).then_inc(s, 16)

            gp.wait_ge(setup_in, 16 * N_SETUP)
            for b in range(NB):
                gather(AGG[:, b, :], A["L2_gnn_emb"], ztype[:, b:b + 1], emb_rows)
            gp.wait_ge(p_ready, 1)
            for b in range(NB):
                if b >= SLOTS:
                    gp.wait_ge(ends_used, b - SLOTS + 1)
                gather(G[b % SLOTS][:, 0:T].bitcast(i32), A["dst"].rearrange("(p t) -> p t", t=T),
                       nodes_i[:, 2, b:b + 1], ends_rows[b % SLOTS])
            gp.wait_ge(ends_used, NB)
            gp.wait_ge(nodes_ready, 1)

            for k, ps in enumerate(PASSES):
                ct, w, H, base, rw = ps["CT"], ps["W"], ps["H"], ps["slot_base"], ps["RW"]
                gp.wait_ge(table_stored, 16 * (k + 1))
                if k == 0:
                    gp.wait_ge(emb_stored, 16)
                if H:
                    j = k - 5
                    gp.wait_ge(h_sb, NG * (DENSE_OF_PASS[k] + 1))
                    gp.wait_ge(zero_stored, 16)
                    hv = rows(Hx, rw)
                    for b in range(NB):
                        gp.indirect_dma_start(out=starts_ad[H], out_offset=bass.IndirectOffsetOnAxis(ap=nodes_i[:, 1, b:b + 1], axis=0),
                                              in_=hv[:, b, D + H:D + 2 * H], in_offset=None,
                                              bounds_check=EP - 1, oob_is_err=False).then_inc(ad_scattered, 16)
                    gather(ad0[:, 0:rw], table[rw], edge_i[:, 2:3], ad_first)

                def gathers(i, first=False):
                    for b in range(SLOTS):
                        gr = g_rows(b, ps)
                        if not (first and k == 0):
                            gp.wait_ge(chunk_done[b], base + i)
                        gp.wait_ge(idx_staged[b], base + i + 1)
                        gp.sem_inc(go, 1)
                        for t in range(ct):
                            gather(gr[:, t, :], table[rw], idx[b][:, t:t + 1], gathered[b])

                gathers(0, first=True)
                with gp.Fori(1, ps["ITER"]) as i:
                    gathers(i)
                seams = [(runs[w], FX)] + ([(runs_cf, FX2)] if ps["kind"] == "first" else [])
                n0 = k + (1 if k else 0)
                for b in range(SLOTS):
                    stored = 16 * (base + ps["ITER"] + PASSES[0]["ITER"])
                    gp.wait_ge(run_stored[b], stored)
                for r, fx in seams:
                    gather(fx[:, 0:w], r, edge_i[:, 0:1], fix_in)
                gp.wait_ge(fix_new, k + 1)
                for r, fx in seams:
                    gp.indirect_dma_start(out=r, out_offset=bass.IndirectOffsetOnAxis(ap=edge_i[:, 1:2], axis=0),
                                          in_=fx[:, 0:w], in_offset=None,
                                          bounds_check=EP - 1, oob_is_err=False).then_inc(fix_out, 16)
                gp.wait_ge(fix_out, 16 * (n0 + len(seams)))
                rv = rows(R, w)
                for b in range(NB):
                    gather(rv[:, b, :], runs[w], nodes_i[:, 0, b:b + 1], end_in)
                if k == 0:
                    for b in range(NB):
                        gather(AGG[:, b, :], runs_cf, nodes_i[:, 0, b:b + 1], end_in)
                    gp.wait_ge(item_idx, 1)
                    for q, name in enumerate(("src", "dst")):
                        edges = A[name].rearrange("(g e) -> g e", e=GE * P)
                        for half, m in ((0, P), (1, NSLOT - P)):
                            gather(rows_a[2 * q + half][0:m, :].bitcast(i32), edges, edge_i[0:m, 3 + half:4 + half], item_rows)
                    nc.gpsimd.iota(iota_n, pattern=[[1, NP_]], base=0, channel_multiplier=0).then_inc(iota_ready, 1)
            gp.wait_ge(min_ready, 1)
            nc.gpsimd.memset(den_sum, 0.0).then_inc(den_clear, 1)
            gp.wait_ge(den_clear, 1)
            for m in range(NB):
                gp.wait_ge(pair_w, m + 1)
                if m:
                    gp.wait_ge(pair_den, m)
                nc.gpsimd.tensor_tensor(den_sum, den_sum, soft_w[m % 2], ALU.add).then_inc(pair_den, 1)

        @block.scalar
        def _(act):
            act.wait_ge(setup_in, 16 * N_SETUP)
            act.wait_ge(cos_arg, 1)
            nc.scalar.activation(gate[:, :], gate[:, :], ACT.Sin).then_inc(cos_done, 1)
            n_w = 0

            def weight(dst, src):
                nonlocal n_w
                n_w += 1
                act.wait_ge(w_ps, n_w)
                nc.scalar.copy(dst, src).then_inc(w_sb, 1)

            for l in range(NL0):
                weight(WR[:, l, 0:D], PS[:, 4, 0:D])
            for j, h in enumerate((4, 4, 1)):
                weight(wT[:, :], PS[:, 4, 0:D])
                weight(WR[:, 5 + j, D:D + 2 * h], PS[:, 4, 0:2 * h])
            act.wait_ge(deg_ready, 1)
            nc.scalar.activation(nd(N_T0), nd(N_T0), ACT.Sqrt).then_inc(dinv_root, 1)

            def transposed(d, dst, ps_sem, sb_sem, n0):
                for g in range(NG):
                    m = P * len(blocks(g))
                    act.wait_ge(ps_sem, n0 + g + 1)
                    if g == 0 and d >= 1 and sb_sem is xT_sb:
                        act.wait_ge(h_ps, NG * d)
                    nc.scalar.copy(dst[:, GB * P * g:GB * P * g + m], PS[:, g % 2, 0:m]).then_inc(sb_sem, 1)

            n_tail = n_fix = n_soft = n_post = n_ln = 0

            def norm_root():
                nonlocal n_ln
                n_ln += 1
                act.wait_ge(ln_var, n_ln)
                nc.scalar.activation(mv[:, :, 1], mv[:, :, 1], ACT.Sqrt).then_inc(ln_std, 1)

            for k, ps in enumerate(PASSES):
                ct, H, base, kind = ps["CT"], ps["H"], ps["slot_base"], ps["kind"]
                d = DENSE_OF_PASS[k]
                transposed(d, xT, xT_ps, xT_sb, NG * d)
                gbase = ps["gath_base"]

                def stage(i, b):
                    nc.scalar.copy(idx[b][:, 0:ct], src_i[:, bass.ds((i * SLOTS + b) * ct, ct)]).then_inc(idx_staged[b], 1)

                def chunk_work(i):
                    for b in range(SLOTS):
                        c = i * SLOTS + b
                        if kind == "first":
                            act.wait_ge(ea_ps, c + 1)
                            if not (isinstance(i, int) and c < 2):
                                act.wait_ge(filt_ps, c - 1)
                            for hf, m in ((0, 4), (1, 3)):
                                ins = nc.scalar.copy(eaT[0:NRBF, b % 2, hf * 512:hf * 512 + m * P], PS[0:NRBF, hf, 0:m * P])
                            ins.then_inc(ea_sb, 1)
                        if kind == "gat":
                            act.wait_ge(soft_arg, (k - 5) * SLOTS * ps["ITER"] + c + 1)
                            nc.scalar.activation(pc[:, :, :, 0:H], dc[:, :, :, 0:H], ACT.Exp).then_inc(soft_exp, 1)
                        act.wait_ge(gathered[b], gbase + 16 * ct * (i + 1))
                        stage(i + 1, b)

                for b in range(SLOTS):
                    stage(0, b)
                chunk_work(0)
                if ps["ITER"] > 2:
                    with act.Fori(1, ps["ITER"] - 1) as i:
                        chunk_work(i)
                i = ps["ITER"] - 1
                for b in range(SLOTS):
                    c = i * SLOTS + b
                    if kind == "first":
                        act.wait_ge(ea_ps, c + 1)
                        act.wait_ge(filt_ps, c - 1)
                        for hf, m in ((0, 4), (1, 3)):
                            ins = nc.scalar.copy(eaT[0:NRBF, b % 2, hf * 512:hf * 512 + m * P], PS[0:NRBF, hf, 0:m * P])
                        ins.then_inc(ea_sb, 1)
                    if kind == "gat":
                        act.wait_ge(soft_arg, (k - 5) * SLOTS * ps["ITER"] + c + 1)
                        nc.scalar.activation(pc[:, :, :, 0:H], dc[:, :, :, 0:H], ACT.Exp).then_inc(soft_exp, 1)
                    act.wait_ge(gathered[b], gbase + 16 * ct * (i + 1))
                if kind == "gat":
                    n_tail += 1
                    act.wait_ge(tail_arg, n_tail)
                    nc.scalar.activation(EE[0:H, :, :], DD[0:H, :, :], ACT.Exp).then_inc(tail_exp, 1)
                    n_fix += 1
                    act.wait_ge(fix_arg, n_fix)
                    nc.scalar.activation(fxe[:, :, 0:H], fxm[:, 0:2, 0:H], ACT.Exp).then_inc(fix_exp, 1)
                    n_post += 1
                    act.wait_ge(post_arg, n_post)
                    nc.scalar.activation(na[:, 4:6, 0:NB * H], na[:, 2:4, 0:NB * H], ACT.Exp).then_inc(post_exp, 1)
                if kind in ("first", "max") and k < NL0 - 1:
                    n_post += 0
                    act.wait_ge(agg_ready, k + 2)
                    nc.scalar.activation(X[:, :, :], X[:, :, :], ACT.Silu).then_inc(x_ready, 1)
                if k == 0:
                    transposed(0, aggT, aggT_ps, aggT_sb, 0)
                if k == 4:
                    norm_root()
            transposed(GAT3, xT, xT_ps, xT_sb, NG * GAT3)
            for j in range(2):
                act.wait_ge(rows_ps, j + 1)
                nc.scalar.copy(dst_row[j], psum_row()).then_inc(rows_sb, 1)
            act.wait_ge(rows_sb, 2)
            hx = rows(Hx, WIDTH[GAT3])
            for m in range(NB):
                if m >= 2:
                    act.wait_ge(pair_max, m - 1)
                    act.wait_ge(pair_mm, m - 1)
                    act.wait_ge(pair_den, m - 1)
                nc.scalar.activation(pos_exp[m % 2], dst_row[0], ACT.Exp, bias=hx[:, m, D:D + 1])
                nc.scalar.activation(soft_w[m % 2], dst_row[1], ACT.Exp, bias=nodes[:, N_NEG, m:m + 1]).then_inc(pair_exp, 1)
            act.wait_ge(pair_mm, NB)
            act.wait_ge(pair_max, NB)
            nc.scalar.copy(xT[:, :], psum_row()).then_inc(acc_sb, 1)
            act.wait_ge(self_arg, 1)
            nc.scalar.activation(nd(N_SELF), nd(N_SELF), ACT.Exp).then_inc(self_exp, 1)
            norm_root()
            transposed(CF, xT, xT_ps, xT_sb, NG * CF)
            norm_root()
            for r in range(2):
                d = CF + 1 + r
                transposed(d, xT, xT_ps, xT_sb, NG * d)
                act.wait_ge(gcn_ps, r + 1)
                nc.scalar.copy(xT[:, :], psum_row()).then_inc(gcn_sb, 1)
            norm_root()

        @block.tensor
        def _(pe):
            pe.wait_ge(ready_const, 1)
            pe.wait_ge(part_ready, 1)
            nc.tensor.matmul(PS[:, 5, 0:P], small[:, 1:2].to_broadcast([P, P]), ident[:, :], start=True, stop=True)
            nc.tensor.matmul(PS[:, 5, P:P + 1], shift[:, :], small[:, 1:2], start=True, stop=True).then_inc(part_rows, 1)
            pe.wait_ge(flag_ready, 1)
            nc.tensor.matmul(PS[:, 5, 2 * P:3 * P], small[:, 8:9].to_broadcast([P, P]), ident[:, :], start=True, stop=True).then_inc(flag_rows, 1)
            pe.wait_ge(setup_in, 16 * N_SETUP)
            n_w = 0

            def weight(ins):
                nonlocal n_w
                n_w += 1
                ins.then_inc(w_ps, 1)
                pe.wait_ge(w_sb, n_w)

            for l in range(NL0):
                weight(nc.tensor.transpose(PS[:, 4, 0:D], w_raw[:, l, :], ident[:, :]))
            pe.wait_ge(att_ready, 1)
            for j, h in enumerate((4, 4, 1)):
                weight(nc.tensor.transpose(PS[:, 4, 0:D], WR[:, 5 + j, 0:D], ident[:, :]))
                weight(nc.tensor.matmul(PS[:, 4, 0:2 * h], wT[:, :], att_m[:, j, 0:2 * h], start=True, stop=True))
            pe.wait_ge(cnt_ready, 1)
            nc.tensor.matmul(PS[:, 6, 0:NB], shift[:, :], nd(N_CNT), start=True, stop=False)
            nc.tensor.matmul(PS[:, 6, 0:NB], wrap[:, :], nd(N_T1), start=False, stop=True).then_inc(start_ps, 1)

            nc.tensor.matmul(PS[:, 5, 0:NB], ident[:, P - 1:P].to_broadcast([P, P]), nd(N_CNT), start=True, stop=True).then_inc(hi_ps, 1)

            def dense(d):
                src, w = src_of(d), WIDTH[d]
                if d:
                    pe.wait_ge(x_ready, d)
                for g in range(NG):
                    if g >= 2:
                        pe.wait_ge(xT_sb, NG * d + g - 1)
                    for n, b in enumerate(blocks(g)):
                        ins = nc.tensor.transpose(PS[:, g % 2, n * P:(n + 1) * P], src[:, b, :], ident[:, :])
                    ins.then_inc(xT_ps, 1)
                    if g:
                        product(d, g - 1)
                product(d, NG - 1)

            def product(d, g):
                w = WIDTH[d]
                pe.wait_ge(xT_sb, NG * d + g + 1)
                if NG * d + g >= 2:
                    pe.wait_ge(h_sb, NG * d + g - 1)
                for n, b in enumerate(blocks(g)):
                    o = PS[:, 2 + (NG * d + g) % 2, n * w:(n + 1) * w]
                    ins = nc.tensor.matmul(o, xT[:, b * P:(b + 1) * P], WR[:, d, 0:w], start=True, stop=(d != CF))
                    if d == CF:
                        ins = nc.tensor.matmul(o, aggT[:, b * P:(b + 1) * P], WR[:, NDENSE, 0:w], start=False, stop=True)
                ins.then_inc(h_ps, 1)

            for k, ps in enumerate(PASSES):
                H, kind, w = ps["H"], ps["kind"], ps["W"]
                dense(DENSE_OF_PASS[k])
                if k == 1:
                    pe.wait_ge(h_sb, 2 * NG)
                    pe.wait_ge(item_f, 1)
                    for q in range(2):
                        for t in range(GE):
                            for half, m in ((0, P), (1, NSLOT - P)):
                                ins = nc.tensor.transpose(PS[:, GE * q + t, half * P:half * P + m],
                                                          rows_a[2 * q + half][0:m, t * P:(t + 1) * P], ident[0:m, 0:m])
                    ins.then_inc(item_ps, 1)
                    pe.wait_ge(item_tab, 1)
                if kind_max(ps):
                    def items(i, first=False):
                        for b in range(SLOTS):
                            item = (k - 1) * SLOTS * ps["ITER"] + i * SLOTS + b
                            if not (k == 1 and first and b == 0):
                                pe.wait_ge(item_added, item)
                            elif k > 1:
                                pe.wait_ge(h_sb, NG * (k + 1))
                            for t in range(GE):
                                pe.wait_ge(hot_ready, item * GE + t + 1)
                                for m in range(NB):
                                    ins = nc.tensor.matmul(PS[:, m // 4, m % 4 * P:(m % 4 + 1) * P],
                                                           src_hot[t][:, m * P:(m + 1) * P], dst_hot[:, t, :],
                                                           start=(t == 0 and m % 4 == 0), stop=(t == GE - 1 and (m % 4 == 3 or m == NB - 1)),
                                                           skip_group_check=True)
                            ins.then_inc(item_sum, 1)

                    if k > 1:
                        pe.wait_ge(h_sb, NG * (k + 1))
                    items(0, first=True)
                    with pe.Fori(1, ps["ITER"]) as i:
                        items(i)
                    pe.wait_ge(item_added, k * SLOTS * ps["ITER"])
                if kind == "first":
                    pe.wait_ge(h_sb, NG)

                    def filters(i, first=False):
                        for b in range(SLOTS):
                            c = i * SLOTS + b
                            pe.wait_ge(ea_in[b], 16 * (i + 1))
                            if not (first and b == 0):
                                pe.wait_ge(ea_sb, c)
                            pe.sem_inc(go, 1)
                            for t in range(CT0):
                                ins = nc.tensor.transpose(PS[0:NRBF, t // 4, (t % 4) * P:(t % 4 + 1) * P],
                                                          ea[b][:, t * NRBF:(t + 1) * NRBF], ident[:, :])
                            ins.then_inc(ea_ps, 1)
                            pe.wait_ge(ea_sb, c + 1)
                            if not (first and b < 2):
                                pe.wait_ge(filt_used, c - 1)
                            for t in range(CT0):
                                ins = nc.tensor.matmul(PS[:, 2 + 2 * (b % 2) + t // 4, (t % 4) * P:(t % 4 + 1) * P],
                                                       eaT[:, b % 2, t * P:(t + 1) * P], wd[:, :], start=True, stop=True)
                            ins.then_inc(filt_ps, 1)

                    filters(0, first=True)
                    with pe.Fori(1, ps["ITER"]) as i:
                        filters(i)
                pe.wait_ge(chunk_done[SLOTS - 1], ps["slot_base"] + ps["ITER"])
                last = s_rows(SLOTS - 1, ps)[:, ps["CT"] - 1, :]
                ins = nc.tensor.transpose(PS[:, 6, 0:P], last[:, 0:D], ident[:, :])
                if kind == "first":
                    ins = nc.tensor.transpose(PS[:, 6, P:2 * P], s_cf(SLOTS - 1)[:, CT0 - 1, :], ident[:, :])
                if H:
                    nc.tensor.transpose(PS[0:H, 6, P:2 * P], last[:, D:D + H], ident[:, :])
                    ins = nc.tensor.transpose(PS[0:H, 6, 2 * P:3 * P], last[:, D + H:D + 2 * H], ident[:, :])
                ins.then_inc(tail_T, 1)
                if H:
                    pe.wait_ge(tail_exp, k - 4)
                    hr = head_rows[0:4, :] if H == 4 else ones_row[0:1, :]
                    nc.tensor.matmul(PS[:, 7, 0:P], hr, EE[0:H, 0, :], start=True, stop=True)
                    nc.tensor.matmul(PS[:, 7, P:2 * P], hr, EE[0:H, 1, :], start=True, stop=True).then_inc(tail_B, 1)
                pe.wait_ge(tail_V, k + 1)
                ins = nc.tensor.transpose(PS[:, 6, 0:P], V[:, 0:P], ident[:, :])
                if kind == "first":
                    ins = nc.tensor.transpose(PS[:, 6, P:2 * P], V2[:, 0:P], ident[:, :])
                if H:
                    nc.tensor.transpose(PS[:, 6, P:P + H], dV[0:H, 0:P], ident[0:H, 0:H])
                    ins = nc.tensor.transpose(PS[:, 6, 2 * P:2 * P + H], mV[0:H, 0:P], ident[0:H, 0:H])
                ins.then_inc(tail_C, 1)
                if k == 0:
                    pe.wait_ge(agg_ready, 1)
                    for g in range(NG):
                        if g >= 2:
                            pe.wait_ge(aggT_sb, g - 1)
                        for n, b in enumerate(blocks(g)):
                            ins = nc.tensor.transpose(PS[:, g % 2, n * P:(n + 1) * P], AGG[:, b, :], ident[:, :])
                        ins.then_inc(aggT_ps, 1)
                    pe.wait_ge(aggT_sb, NG)
            dense(GAT3)
            pe.wait_ge(min_ready, 1)
            nc.tensor.transpose(PS[0:1, 7, 0:P], small[:, 20:21], ident[:, :]).then_inc(min_T, 1)
            pe.wait_ge(min_one, 1)
            nc.tensor.matmul(PS[:, 7, P:P + 1], ones_row[0:1, :], small[0:1, 21:22], start=True, stop=True).then_inc(min_ps, 1)
            pe.wait_ge(max_ready, 1)
            for g in range(NG):
                if g >= 2:
                    pe.wait_ge(max_used, g - 1)
                for n, b in enumerate(blocks(g)):
                    ins = nc.tensor.transpose(PS[:, g % 2, n * P:(n + 1) * P], big_max[:, b * P:(b + 1) * P], ident[:, :])
                ins.then_inc(max_T, 1)
            pe.wait_ge(rows_ready, 1)
            for j, q in enumerate((N_ROW1, N_ROW2)):
                if j:
                    pe.wait_ge(rows_sb, 1)
                for b in range(NB):
                    ins = nc.tensor.matmul(PS[:, b // 4, (b % 4) * P:(b % 4 + 1) * P], nodes[:, q, b:b + 1].to_broadcast([P, P]),
                                           ident[:, :], start=True, stop=True)
                ins.then_inc(rows_ps, 1)
            pe.wait_ge(rows_sb, 2)
            hx = rows(Hx, WIDTH[GAT3])
            for m in range(NB):
                pe.wait_ge(pair_w, m + 1)
                for c in range(0, NP_, 512):
                    n = min(512, NP_ - c)
                    ins = nc.tensor.matmul(PS[:, c // 512, 0:n], hx[:, m, 0:D], soft_w[m % 2][:, c:c + n],
                                           start=(m == 0), stop=(m == NB - 1))
                ins.then_inc(pair_mm, 1)
            pe.wait_ge(pair_den, NB)
            for b in range(NB):
                ins = nc.tensor.matmul(PS[:, 7, b:b + 1], den_sum[:, b * P:(b + 1) * P], small[:, 30:31], start=True, stop=True)
            ins.then_inc(den_ps, 1)
            pe.wait_ge(acc_sb, 1)
            for g in range(NG):
                if g >= 2:
                    pe.wait_ge(acc_used, g - 1)
                for n, b in enumerate(blocks(g)):
                    ins = nc.tensor.transpose(PS[:, g % 2, n * P:(n + 1) * P], xT[:, b * P:(b + 1) * P], ident[:, :])
                ins.then_inc(acc_T, 1)
            dense(CF)
            for r in range(2):
                d = CF + 1 + r
                dense(d)
                pe.wait_ge(h_sb, NG * (d + 1))
                for m in range(NB):
                    q = (2 + r) * NB + m
                    adj_wait(pe, q)
                    for c in range(0, NP_, 512):
                        n = min(512, NP_ - c)
                        ins = nc.tensor.matmul(PS[:, c // 512, 0:n], rows(Hx, D)[:, m, :], adj_tile(q)[:, c:c + n],
                                               start=(m == 0), stop=(m == NB - 1))
                    ins.then_inc(adj_used, 1)
                pe.wait_ge(adj_used, (r + 2) * NB)
                pe.sem_inc(gcn_ps, 1)
                pe.wait_ge(gcn_sb, r + 1)
                for g in range(NG):
                    if g >= 2:
                        pe.wait_ge(gcn_out, r * NG + g - 1)
                    for n, b in enumerate(blocks(g)):
                        ins = nc.tensor.transpose(PS[:, g % 2, n * P:(n + 1) * P], xT[:, b * P:(b + 1) * P], ident[:, :])
                    ins.then_inc(gcn_T, 1)
                pe.wait_ge(gcn_out, (r + 1) * NG)

        @block.vector
        def _(dve):
            vec = nc.vector
            count = 0

            def link(ins):
                nonlocal count
                count += 1
                ins.then_inc(chain_v, 1)
                dve.wait_ge(chain_v, count)

            def tt(o, a, b, op):
                return vec.tensor_tensor(o, a, b, op)

            def ts(o, a, s1, s2, op0, op1=None):
                return vec.tensor_scalar(o, a, s1, s2, op0, op1) if op1 is not None else vec.tensor_scalar(o, a, s1, None, op0)

            link(vec.memset(ad_e[:, :, :], 0.0))
            vec.memset(src_i[:, T:T + SLOTS * CT], 0).then_inc(zero_ready, 1)
            link(vec.memset(eaT[NRBF:NRBF + 1, :, :], 1.0))
            link(vec.memset(ones_row[:, :], 1.0))
            link(vec.memset(small[:, 30:31], 1.0))
            link(vec.memset(S[SLOTS - 1][:, :], 0.0))
            link(vec.memset(V[:, 0:1], 0.0))
            link(vec.memset(V2[:, 0:1], 0.0))
            link(vec.memset(mV[:, 0:1], -BIG))
            link(vec.memset(dV[:, 0:1], 0.0))
            link(vec.memset(mbuf[:, :, :], 0.0))
            dve.wait_ge(setup_in, 16 * N_SETUP)
            dve.wait_ge(ready_const, 1)
            link(vec.tensor_copy(dst_f[:, :], dst_i[:, :]))
            link(ts(small[:, 1:2], dst_f[:, T - 1:T], 1.0, None, ALU.add))
            ts(small[:, 2:3], dst_f[:, 0:1], 1.0, None, ALU.add).then_inc(part_ready, 1)
            link(tt(keep01[:, 1:T], dst_f[:, 1:T], dst_f[:, 0:T - 1], ALU.is_equal))
            link(vec.memset(keep01[:, 0:1], 0.0))
            link(ts(keepM[:, :], keep01[:, :], 2.0, -1.0, ALU.mult, ALU.add))
            link(ts(keepM[:, :], keepM[:, :], BIG, None, ALU.mult))
            dve.wait_ge(part_rows, 1)
            lastB = xT[:, 0:P]
            link(vec.tensor_copy(lastB, PS[:, 5, 0:P]))
            link(vec.tensor_copy(small[:, 3:4], PS[:, 5, P:P + 1]))
            link(ts(nd(N_T0), nval[:, :], 1.0, None, ALU.add))
            cmp = X[:, :, :]
            link(tt(cmp, lastB.unsqueeze(1).to_broadcast([P, NB, P]), nd(N_T0).unsqueeze(2).to_broadcast([P, NB, P]), ALU.is_le))
            link(vec.tensor_reduce(nd(N_P), cmp, AX.X, ALU.add))
            link(ts(nd(N_P), nd(N_P), float(P - 1), None, ALU.min))
            vec.tensor_copy(nodes_i[:, 2, :], nd(N_P)).then_inc(p_ready, 1)
            link(tt(small[:, 4:5], small[:, 2:3], small[:, 3:4], ALU.is_equal))
            link(tt(small[:, 5:6], small[:, 1:2], small[:, 2:3], ALU.is_equal))
            tt(small[:, 8:9], small[:, 4:5], small[:, 5:6], ALU.mult).then_inc(flag_ready, 1)
            eqf = aggT[:, 0:T]
            link(ts(eqf, dst_f[:, :], dst_f[:, 0:1], None, ALU.is_equal))
            link(vec.tensor_reduce(small[:, 6:7], eqf, AX.X, ALU.add))
            link(tt(small[:, 7:8], small[:, 6:7], small[:, 0:1], ALU.add))
            link(ts(small[:, 7:8], small[:, 7:8], -1.0, None, ALU.add))
            link(ts(small[:, 9:10], small[:, 4:5], -float(SKIP), float(SKIP), ALU.mult, ALU.add))
            link(tt(small[:, 9:10], small[:, 9:10], small[:, 7:8], ALU.add))
            link(vec.tensor_copy(edge_i[:, 0:1], small[:, 7:8]))
            link(vec.tensor_copy(edge_i[:, 1:2], small[:, 9:10]))
            link(vec.tensor_copy(edge_i[:, 2:3], dst_f[:, 0:1]))
            dve.wait_ge(flag_rows, 1)
            link(vec.tensor_copy(kB01[:, :], PS[:, 5, 2 * P:3 * P]))
            link(ts(kBM[:, :], kB01[:, :], 2.0, -1.0, ALU.mult, ALU.add))
            link(ts(kBM[:, :], kBM[:, :], BIG, None, ALU.mult))
            for j, h in enumerate((4, 4, 1)):
                for q in range(2):
                    o = att_m[:, j, q * h:(q + 1) * h]
                    if h == 4:
                        ins = ts(o, head_of[:, :], att[:, j, q:q + 1], None, ALU.mult)
                    else:
                        ins = vec.tensor_copy(o, att[:, j, q:q + 1])
            ins.then_inc(att_ready, 1)
            mask = aggT[:, T:2 * T]
            same = aggT[:, 2 * T:3 * T]
            link(ts(mask, gate[:, :], 5.0, None, ALU.is_lt))
            link(vec.tensor_copy(same, src_i[:, 0:T]))
            link(tt(same, same, dst_f[:, :], ALU.not_equal))
            link(tt(mask, mask, same, ALU.mult))
            link(ts(same.bitcast(i32), gate[:, :], 0.1, None, ALU.mult))
            link(ts(same, same.bitcast(i32), -10.0, None, ALU.mult))
            link(tt(gate[:, :], gate[:, :], same, ALU.add))
            link(ts(same, gate[:, :], -1.0, None, ALU.mult))
            link(tt(gate[:, :], gate[:, :], same, ALU.max))
            link(ts(same, gate[:, :], -1.0, 10.0, ALU.mult, ALU.add))
            link(tt(gate[:, :], gate[:, :], same, ALU.min))
            ts(gate[:, :], gate[:, :], -float(np.pi) / 5.0, float(np.pi) / 2.0, ALU.mult, ALU.add).then_inc(cos_arg, 1)
            dve.wait_ge(cos_done, 1)
            link(ts(gate[:, :], gate[:, :], 0.5, 0.5, ALU.mult, ALU.add))
            link(tt(gate[:, :], gate[:, :], mask, ALU.mult))
            for b in range(NB):
                dve.wait_ge(ends_rows[b % SLOTS], 16 * (b // SLOTS + 1))
                o = R[:, (b % 2) * T:(b % 2 + 1) * T]
                ts(o, G[b % SLOTS][:, 0:T].bitcast(i32), nval[:, b:b + 1], None, ALU.is_le).then_inc(ends_used, 1)
                dve.wait_ge(ends_used, b + 1)
                link(vec.tensor_reduce(nodes[:, N_CNT, b:b + 1], o, AX.X, ALU.add))
            link(ts(nd(N_T0), nd(N_P), float(T), None, ALU.mult))
            link(tt(nd(N_CNT), nd(N_CNT), nd(N_T0), ALU.add))
            link(vec.memset(nodes[:, N_T1, 0:1], 0.0))
            vec.tensor_copy(nodes[:, N_T1, 1:NB], nodes[:, N_CNT, 0:NB - 1]).then_inc(cnt_ready, 1)
            dve.wait_ge(start_ps, 1)
            dve.wait_ge(cnt_ready, 1)
            link(vec.tensor_copy(nd(N_START), PS[:, 6, 0:NB]))
            link(tt(nd(N_DEG), nd(N_CNT), nd(N_START), ALU.subtract))
            link(ts(nd(N_HAS), nd(N_DEG), 1.0, None, ALU.min))
            link(ts(nd(N_END), nd(N_CNT), -1.0, 0.0, ALU.add, ALU.max))
            link(vec.tensor_copy(nodes_i[:, 0, :], nd(N_END)))
            link(ts(nd(N_T1), nd(N_HAS), -float(SKIP), float(SKIP), ALU.mult, ALU.add))
            link(tt(nd(N_T1), nd(N_T1), nd(N_START), ALU.add))
            vec.tensor_copy(nodes_i[:, 1, :], nd(N_T1)).then_inc(nodes_ready, 1)
            ts(nd(N_T0), nd(N_DEG), 1.0, None, ALU.add).then_inc(deg_ready, 1)
            dve.wait_ge(dinv_root, 1)
            link(vec.reciprocal(nd(N_DINV), nd(N_T0)))
            def item_list():
                link(vec.tensor_copy(nd(N_T0), PS[:, 5, 0:NB]))
                link(ts(nd(N_T0), nd(N_T0), -1.0, 0.0, ALU.add, ALU.max))
                floor_of(nd(N_T1), nd(N_T0), 1.0 / (GE * P), nodes_i[:, 2, :], nodes[:, N_FREE, :])
                link(tt(nd(N_HI), nd(N_T1), nval_blk(), ALU.add))
                iv = small[:, 16:18]
                cv = small[:, 18:20]
                link(ts(iv[:, 0:1], nval[:, 0:1], 0.0, None, ALU.add))
                link(ts(iv[:, 1:2], nval[:, 0:1], float(P), None, ALU.add))
                for j in range(2):
                    link(ts(nodes[:, N_FREE, 0:NB - 1], nodes[:, N_HI, 0:NB - 1], iv[:, j:j + 1], None, ALU.is_lt))
                    link(vec.tensor_reduce(cv[:, j:j + 1], nodes[:, N_FREE, 0:NB - 1], AX.X, ALU.add))
                link(tt(cv, iv, cv, ALU.subtract))
                link(ts(cv, cv, float(NGRP - 1), None, ALU.min))
                vec.tensor_copy(edge_i[:, 3:5], cv).then_inc(item_idx, 1)

            def floor_of(o, a, scale, ti, tf):
                link(ts(tf, a, scale, None, ALU.mult))
                link(vec.tensor_copy(ti, tf))
                link(vec.tensor_copy(o, ti))
                link(tt(tf, o, tf, ALU.is_gt))
                link(tt(o, o, tf, ALU.subtract))

            def nval_blk():
                return nodes[:, N_BLK, :]

            def staircase():
                dve.wait_ge(item_rows, 64)
                for q in range(3):
                    vec.tensor_copy(rows_a[q][:, :], rows_a[q][:, :].bitcast(i32)) if q != 1 else vec.tensor_copy(rows_a[q][0:NSLOT - P, :], rows_a[q][0:NSLOT - P, :].bitcast(i32))
                vec.tensor_copy(rows_a[3][0:NSLOT - P, :], rows_a[3][0:NSLOT - P, :].bitcast(i32)).then_inc(item_f, 1)
                dve.wait_ge(iota_ready, 1)
                cb = dst_f[:, 0:NSLOT]
                ii = dst_f[:, NSLOT:2 * NSLOT]
                link(vec.tensor_copy(ii, iota_n[:, 0:NSLOT]))
                link(vec.memset(cb, 0.0))
                for c in range(NB - 1):
                    link(vec.scalar_tensor_tensor(cb, ii, nodes[:, N_HI, c:c + 1], cb, ALU.is_gt, ALU.add))
                link(tt(item_keep[:, 1:NSLOT], cb[:, 1:NSLOT], cb[:, 0:NSLOT - 1], ALU.is_equal))
                link(vec.memset(item_keep[:, 0:1], 0.0))
                link(vec.tensor_copy(item_blk, cb))
                link(vec.memset(ii, 0.0))
                link(tt(ii[:, 0:NITEM - 1], cb[:, 1:NITEM], cb[:, 0:NITEM - 1], ALU.is_gt))
                link(vec.memset(ii[:, NITEM - 1:NITEM], 1.0))
                link(vec.tensor_copy(item_last, ii))
                link(ts(cb, cb, -float(P), None, ALU.mult))
                dve.wait_ge(item_ps, 1)
                link(vec.tensor_copy(item_src, PS[:, 0:GE, 0:NSLOT]))
                link(tt(item_dst, PS[:, GE:2 * GE, 0:NSLOT], cb.unsqueeze(1).to_broadcast([P, GE, NSLOT]), ALU.add))
                vec.memset(item_src[:, :, NITEM:NSLOT], -1.0).then_inc(item_tab, 1)
                dve.wait_ge(item_tab, 1)

            dve.wait_ge(hi_ps, 1)
            item_list()
            has = nd(N_HAS).unsqueeze(2).to_broadcast([P, NB, D])

            n_ln = 0

            def layer_norm(src, dst, done):
                nonlocal n_ln
                n_ln += 1
                for b in range(NB):
                    ins = vec.bn_stats(stats[:, b, :], src[:, b, :])
                link(ins)
                for b in range(NB):
                    ins = vec.bn_aggr(mv[:, b, :], stats[:, b, :])
                link(ins)
                ts(mv[:, :, 1], mv[:, :, 1], 1e-5, None, ALU.add).then_inc(ln_var, 1)
                link(tt(src[:, :, :], src[:, :, :], mv[:, :, 0:1].to_broadcast([P, NB, D]), ALU.subtract))
                dve.wait_ge(ln_std, n_ln)
                link(vec.reciprocal(stats[:, :, 0], mv[:, :, 1]))
                tt(dst[:, :, :], src[:, :, :], stats[:, :, 0:1].to_broadcast([P, NB, D]), ALU.mult).then_inc(done, 1)
                return n_ln

            def dense_out(d):
                hx = rows(Hx, WIDTH[d])
                for g in range(NG):
                    bs = blocks(g)
                    dve.wait_ge(h_ps, NG * d + g + 1)
                    p = ps_rows(2 + (NG * d + g) % 2, g, WIDTH[d])
                    o = hx[:, bs[0]:bs[-1] + 1, :]
                    if d in (5, 6, 7):
                        ins = vec.tensor_copy(o, p)
                    elif d >= 9:
                        ins = tt(o, p, nodes[:, N_DINV, bs[0]:bs[-1] + 1].unsqueeze(2).to_broadcast([P, len(bs), D]), ALU.mult)
                    else:
                        ins = tt(o, p, bias[:, d:d + 1, :].to_broadcast([P, len(bs), D]), ALU.add)
                    ins.then_inc(h_sb, 1)

            for k, ps in enumerate(PASSES):
                kind, ct, w, H, rw, base = ps["kind"], ps["CT"], ps["W"], ps["H"], ps["RW"], ps["slot_base"]
                it = ps["ITER"]
                d = DENSE_OF_PASS[k]
                if k >= 1:
                    dve.wait_ge(table_stored, 16 * k)
                    if k > 5:
                        dve.wait_ge(ad_scattered, 16 * NB * (k - 5))
                dense_out(d)
                if k == 1:
                    dve.wait_ge(aggT_ps, NG)
                    staircase()
                if H:
                    if k == 5:
                        dve.wait_ge(item_stored, 16 * NSLOT)
                    j = k - 5
                    dve.wait_ge(ad_loaded, 16 * (j + 1))
                    dve.wait_ge(ad_first, 16 * (j + 1))
                    rr = R[:, 0:T * H].rearrange("p (t h) -> p t h", h=H)
                    link(vec.tensor_copy(rr[:, 0, :], ad0[:, D + H:D + 2 * H]))
                    for h in range(H):
                        link(vec.tensor_tensor_scan(ad_e[:, h, 0:T], keep01[:, :], rr[:, :, h], 0.0, ALU.mult, ALU.add))

                per_chunk = {"first": 3 * ct - 1, "max": ct - 1, "sum": ct - 1,
                             "gat": (7 + 2 * H + 2 * ct - 1) if H == 4 else (7 + 2 * H + ct - 1)}[kind]
                loop0 = count

                def chunk(i, b, first):
                    c = i * SLOTS + b
                    n = 0
                    c0 = loop0 + c * per_chunk

                    def step(ins):
                        nonlocal n
                        n += 1
                        ins.then_inc(chain_v, 1)
                        return n

                    def after(m):
                        dve.wait_ge(chain_v, c0 + m)

                    gr, sr = g_rows(b, ps), s_rows(b, ps)
                    pb = (b - 1) % SLOTS
                    prev = s_rows(pb, ps)[:, ct - 1, :]
                    prev_cf = s_cf(pb)[:, CT0 - 1, :] if kind == "first" else None
                    dve.wait_ge(gathered[b], ps["gath_base"] + 16 * ct * (i + 1))
                    if not (k == 0 and first):
                        n_st = 2 * i if kind == "first" else base + i + PASSES[0]["ITER"]
                        dve.wait_ge(run_stored[b], 16 * n_st)
                    if b:
                        dve.wait_ge(chunk_done[pb], base + i + 1)
                    elif not (k == 0 and first):
                        dve.wait_ge(chunk_done[pb], base + i)
                    k01 = keep01[:, bass.ds(c * ct, ct)]
                    kM = keepM[:, bass.ds(c * ct, ct)]

                    def fold(o, p, kk, g, op0, op1):
                        return vec.scalar_tensor_tensor(o, p, kk, g, op0, op1)

                    def one(buf, t):
                        return buf[:, bass.ds(c * ct + t, 1)]

                    if kind == "max":
                        item = (k - 1) * SLOTS * it + c
                        for t in range(GE):
                            ts(dst_hot[:, t, :], iota_n[:, 0:P], item_dst[:, t, bass.ds(item, 1)], CSCALE, ALU.is_equal, ALU.mult)
                            ts(src_hot[t], iota_n, item_src[:, t, bass.ds(item, 1)], None, ALU.is_equal).then_inc(hot_ready, 1)
                    if kind in ("max", "sum"):
                        kk, o0, o1 = (keepM, ALU.min, ALU.max) if kind == "max" else (keep01, ALU.mult, ALU.add)
                        for t in range(ct):
                            ins = fold(sr[:, t, :], sr[:, t - 1, :] if t else prev, one(kk, t), gr[:, t, :], o0, o1)
                            if t < ct - 1:
                                after(step(ins))
                        ins.then_inc(chunk_done[b], 1)
                        if kind == "max":
                            dve.wait_ge(item_sum, item + 1)
                            if not (k == 1 and first and b == 0):
                                dve.wait_ge(item_stored, 16 * item)
                            vec.scalar_tensor_tensor(counts, counts, item_keep[:, bass.ds(item, 1)], psum_row(), ALU.mult, ALU.add).then_inc(item_added, 1)
                    elif kind == "first":
                        sc = s_cf(b)
                        dve.wait_ge(filt_ps, c + 1)
                        m_prev = a_prev = None
                        for t in range(ct):
                            f = PS[:, 2 + 2 * (b % 2) + t // 4, (t % 4) * P:(t % 4 + 1) * P]
                            m = step(vec.scalar_tensor_tensor(gr[:, t, D:2 * D], f, one(gate, t), gr[:, t, D:2 * D], ALU.mult, ALU.mult))
                            if a_prev:
                                after(a_prev)
                            a_prev = step(fold(sr[:, t, :], sr[:, t - 1, :] if t else prev, one(keepM, t), gr[:, t, 0:D], ALU.min, ALU.max))
                            after(m)
                            if t == ct - 1:
                                after(a_prev)
                            ins = fold(sc[:, t, :], sc[:, t - 1, :] if t else prev_cf, one(keep01, t), gr[:, t, D:2 * D], ALU.mult, ALU.add)
                            if t < ct - 1:
                                step(ins)
                        ins.then_inc(chunk_done[b], 1)
                    else:
                        v4 = lambda a: a[:, :, 0:H]
                        z, e = v4(zc), v4(ec)
                        mb = mbuf[:, :, 0:H]
                        adv = ad_e[:, 0:H, bass.ds(c * ct, ct)].rearrange("p h t -> p t h")
                        step(vec.tensor_copy(mb[:, 0, :], mb[:, ct, :]))
                        after(step(tt(z, gr[:, :, D:D + H], adv, ALU.add)))
                        after(step(vec.scalar_tensor_tensor(e, z, 0.2, z, ALU.mult, ALU.max)))
                        for h in range(H):
                            m = step(vec.tensor_tensor_scan(mb[:, 1:ct + 1, h], kM, e[:, :, h], mb[:, 0, h:h + 1], ALU.min, ALU.max))
                        after(m)
                        after(step(tt(v4(mp), mb[:, 0:ct, :], kM.unsqueeze(2).to_broadcast([P, ct, H]), ALU.min)))
                        m = step(tt(dc[:, 1, :, 0:H], v4(mp), mb[:, 1:ct + 1, :], ALU.subtract))
                        after(m)
                        tt(dc[:, 0, :, 0:H], e, mb[:, 1:ct + 1, :], ALU.subtract).then_inc(soft_arg, 1)
                        step(vec.tensor_copy(sr[:, :, D + H:D + 2 * H], mb[:, 1:ct + 1, :]))
                        dve.wait_ge(soft_exp, (k - 5) * SLOTS * it + c + 1)
                        for h in range(H):
                            step(vec.tensor_tensor_scan(sr[:, :, D + h], pc[:, 1, :, h], pc[:, 0, :, h],
                                                        prev[:, D + h:D + h + 1], ALU.mult, ALU.add))
                        C = D // H
                        gh = gr[:, :, 0:D].rearrange("p t (h c) -> p t h c", h=H)
                        after(step(tt(gh, gh, pc[:, 0, :, 0:H].unsqueeze(3).to_broadcast([P, ct, H, C]), ALU.mult)))
                        for t in range(ct):
                            p = (sr[:, t - 1, :] if t else prev)[:, 0:D]
                            o = sr[:, t, 0:D]
                            if H == 4:
                                hv = lambda a: a.rearrange("p (h c) -> p h c", h=H)
                                after(step(tt(hv(tmpr[:, :]), hv(p), pc[:, 1, t, 0:H].unsqueeze(2).to_broadcast([P, H, C]), ALU.mult)))
                                ins = tt(o, tmpr[:, :], gr[:, t, 0:D], ALU.add)
                            else:
                                ins = fold(o, p, pc[:, 1, t, 0:1], gr[:, t, 0:D], ALU.mult, ALU.add)
                            if t < ct - 1:
                                after(step(ins))
                        ins.then_inc(chunk_done[b], 1)
                    assert n == per_chunk, (kind, n, per_chunk)

                for b in range(SLOTS):
                    chunk(0, b, True)
                    if kind == "first":
                        dve.wait_ge(chunk_done[b], 1)
                        dve.sem_inc(filt_used, 1)
                with dve.Fori(1, it) as i:
                    for b in range(SLOTS):
                        chunk(i, b, False)
                        if kind == "first":
                            dve.wait_ge(chunk_done[b], i + 1)
                            dve.sem_inc(filt_used, 1)
                count = loop0 + per_chunk * SLOTS * it

                dve.wait_ge(tail_T, k + 1)
                if kind in ("first", "max"):
                    ins = vec.tensor_tensor_scan(V[:, 1:P + 1], kBM[:, :], PS[:, 6, 0:P], -BIG, ALU.min, ALU.max)
                    if kind == "first":
                        link(ins)
                        ins = vec.tensor_tensor_scan(V2[:, 1:P + 1], kB01[:, :], PS[:, 6, P:2 * P], 0.0, ALU.mult, ALU.add)
                    ins.then_inc(tail_V, 1)
                elif kind == "sum":
                    vec.tensor_tensor_scan(V[:, 1:P + 1], kB01[:, :], PS[:, 6, 0:P], 0.0, ALU.mult, ALU.add).then_inc(tail_V, 1)
                else:
                    mT = PS[0:H, 6, 2 * P:3 * P]
                    link(vec.tensor_tensor_scan(mV[0:H, 1:P + 1], kBM[0:H, :], mT, -BIG, ALU.min, ALU.max))
                    link(tt(prevm[0:H, :], kBM[0:H, :], mV[0:H, 0:P], ALU.min))
                    link(tt(DD[0:H, 0, :], mT, mV[0:H, 1:P + 1], ALU.subtract))
                    tt(DD[0:H, 1, :], prevm[0:H, :], mV[0:H, 1:P + 1], ALU.subtract).then_inc(tail_arg, 1)
                    accT = FX2[:, 0:P]
                    link(vec.tensor_copy(accT, PS[:, 6, 0:P]))
                    dve.wait_ge(tail_B, k - 4)
                    link(tt(accT, accT, PS[:, 7, 0:P], ALU.mult))
                    link(vec.tensor_tensor_scan(V[:, 1:P + 1], PS[:, 7, P:2 * P], accT, 0.0, ALU.mult, ALU.add))
                    link(tt(denT[0:H, :], PS[0:H, 6, P:2 * P], EE[0:H, 0, :], ALU.mult))
                    vec.tensor_tensor_scan(dV[0:H, 1:P + 1], EE[0:H, 1, :], denT[0:H, :], 0.0, ALU.mult, ALU.add).then_inc(tail_V, 1)
                dve.wait_ge(tail_C, k + 1)
                dve.wait_ge(fix_in, 16 * (k + 2))
                if kind == "first":
                    link(tt(FX2[:, 0:D], FX2[:, 0:D], PS[:, 6, P:2 * P], ALU.add))
                if not H:
                    tt(FX[:, 0:D], FX[:, 0:D], PS[:, 6, 0:P], ALU.add if kind == "sum" else ALU.max).then_inc(fix_new, 1)
                else:
                    fm, cm = FX[:, D + H:D + 2 * H], PS[:, 6, 2 * P:2 * P + H]
                    link(tt(fxm[:, 2, 0:H], fm, cm, ALU.max))
                    link(tt(fxm[:, 0, 0:H], fm, fxm[:, 2, 0:H], ALU.subtract))
                    tt(fxm[:, 1, 0:H], cm, fxm[:, 2, 0:H], ALU.subtract).then_inc(fix_arg, 1)
                    dve.wait_ge(fix_exp, k - 4)
                    hv = lambda a: a.rearrange("p (h c) -> p h c", h=H)
                    bc = lambda a: a.unsqueeze(2).to_broadcast([P, H, D // H])
                    link(tt(hv(FX[:, 0:D]), hv(FX[:, 0:D]), bc(fxe[:, 0, 0:H]), ALU.mult))
                    link(tt(hv(FX2[:, 0:D]), hv(PS[:, 6, 0:P]), bc(fxe[:, 1, 0:H]), ALU.mult))
                    link(tt(FX[:, 0:D], FX[:, 0:D], FX2[:, 0:D], ALU.add))
                    link(tt(FX[:, D:D + H], FX[:, D:D + H], fxe[:, 0, 0:H], ALU.mult))
                    link(tt(FX2[:, D:D + H], PS[:, 6, P:P + H], fxe[:, 1, 0:H], ALU.mult))
                    link(tt(FX[:, D:D + H], FX[:, D:D + H], FX2[:, D:D + H], ALU.add))
                    vec.tensor_copy(fm, fxm[:, 2, 0:H]).then_inc(fix_new, 1)

                dve.wait_ge(end_in, end_gathers(k))
                rv = rows(R, w)
                if k == 0:
                    tt(AGG[:, :, :], AGG[:, :, :], has, ALU.mult).then_inc(agg_ready, 1)
                if kind in ("first", "max"):
                    if k < NL0 - 1:
                        tt(X[:, :, :], rv, has, ALU.mult).then_inc(agg_ready, 1)
                    else:
                        link(tt(X[:, :, :], rv, has, ALU.mult))
                        link(tt(X[:, :, :], X[:, :, :], XRES[:, :, :], ALU.add))
                        layer_norm(X, XRES, x_ready)
                else:
                    hx = rows(Hx, rw)
                    nh = NB * H
                    v3 = lambda q: na[:, q, 0:nh].rearrange("p (b h) -> p b h", h=H)
                    hasH = nd(N_HAS).unsqueeze(2).to_broadcast([P, NB, H])
                    link(tt(v3(0), hx[:, :, D:D + H], hx[:, :, D + H:D + 2 * H], ALU.add))
                    link(vec.scalar_tensor_tensor(v3(1), v3(0), 0.2, v3(0), ALU.mult, ALU.max))
                    link(tt(v3(6), rv[:, :, D + H:D + 2 * H], hasH, ALU.mult))
                    link(ts(v3(7), hasH, BIG, -BIG, ALU.mult, ALU.add))
                    link(tt(v3(6), v3(6), v3(7), ALU.add))
                    link(tt(v3(0), v3(6), v3(1), ALU.max))
                    link(tt(v3(2), v3(6), v3(0), ALU.subtract))
                    tt(v3(3), v3(1), v3(0), ALU.subtract).then_inc(post_arg, 1)
                    dve.wait_ge(post_exp, k - 4)
                    link(tt(v3(4), v3(4), hasH, ALU.mult))
                    link(tt(v3(7), rv[:, :, D:D + H], v3(4), ALU.mult))
                    link(tt(v3(7), v3(7), v3(5), ALU.add))
                    link(ts(v3(7), v3(7), 1e-16, None, ALU.add))
                    link(vec.reciprocal(v3(7), v3(7)))
                    link(tt(v3(4), v3(4), v3(7), ALU.mult))
                    link(tt(v3(5), v3(5), v3(7), ALU.mult))
                    C = D // H
                    v4d = lambda a: a.rearrange("p b (h c) -> p b h c", h=H)
                    bc = lambda q: v3(q).unsqueeze(3).to_broadcast([P, NB, H, C])
                    link(tt(v4d(X[:, :, :]), v4d(rv[:, :, 0:D]), bc(4), ALU.mult))
                    link(tt(v4d(rv[:, :, 0:D]), v4d(hx[:, :, 0:D]), bc(5), ALU.mult))
                    link(tt(X[:, :, :], X[:, :, :], rv[:, :, 0:D], ALU.add))
                    link(tt(X[:, :, :], X[:, :, :], bias[:, d:d + 1, :].to_broadcast([P, NB, D]), ALU.add))
                    ts(X[:, :, :], X[:, :, :], 0.0, None, ALU.max).then_inc(x_ready, 1)

            dve.wait_ge(table_stored, 16 * NPASS)
            dve.wait_ge(ad_scattered, 16 * NB * 2)
            dense_out(GAT3)
            dve.wait_ge(h_sb, NG * (GAT3 + 1))
            hx = rows(Hx, WIDTH[GAT3])
            a_s, a_d = hx[:, :, D], hx[:, :, D + 1]
            vec.tensor_reduce(small[:, 20:21], a_s, AX.X, ALU.min).then_inc(min_ready, 1)
            dve.wait_ge(min_T, 1)
            vec.tensor_reduce(small[0:1, 21:22], PS[0:1, 7, 0:P], AX.X, ALU.min).then_inc(min_one, 1)
            link(vec.memset(big_max, 0.0))
            dve.wait_ge(min_ps, 1)
            link(ts(small[:, 22:23], PS[:, 7, P:P + 1], -1.0, None, ALU.add))
            link(ts(nd(N_POS), a_s, small[:, 22:23], None, ALU.subtract))
            for m in range(NB):
                adj_wait(dve, m)
                vec.scalar_tensor_tensor(big_max, adj_tile(m), nodes[:, N_POS, m:m + 1], big_max, ALU.min, ALU.max).then_inc(adj_used, 1)
                dve.wait_ge(adj_used, m + 1)
            dve.sem_inc(max_ready, 1)
            for g in range(NG):
                bs = slice(blocks(g)[0], blocks(g)[-1] + 1)
                dve.wait_ge(max_T, g + 1)
                vec.tensor_reduce(nodes[:, N_MAX, bs], ps_rows(g % 2, g, D), AX.X, ALU.max).then_inc(max_used, 1)
            dve.wait_ge(max_used, NG)
            link(tt(nd(N_MAX), nd(N_MAX), nd(N_POS), ALU.max))
            link(ts(nd(N_MAX), nd(N_MAX), small[:, 22:23], None, ALU.add))
            link(tt(nd(N_MAX), nd(N_MAX), a_d, ALU.add))
            link(vec.scalar_tensor_tensor(nd(N_MAX), nd(N_MAX), 0.2, nd(N_MAX), ALU.mult, ALU.max))
            link(tt(nd(N_ROW1), a_d, nd(N_MAX), ALU.subtract))
            link(ts(nd(N_NEG), a_s, 0.2, None, ALU.mult))
            vec.scalar_tensor_tensor(nd(N_ROW2), a_d, 0.2, nd(N_MAX), ALU.mult, ALU.subtract).then_inc(rows_ready, 1)
            link(tt(nd(N_E1), a_s, a_d, ALU.add))
            link(vec.scalar_tensor_tensor(nd(N_E1), nd(N_E1), 0.2, nd(N_E1), ALU.mult, ALU.max))
            tt(nd(N_SELF), nd(N_E1), nd(N_MAX), ALU.subtract).then_inc(self_arg, 1)
            for m in range(NB):
                w = soft_w[m % 2]
                dve.wait_ge(pair_exp, m + 1)
                tt(w, w, pos_exp[m % 2], ALU.max).then_inc(pair_max, 1)
                adj_wait(dve, NB + m)
                dve.wait_ge(pair_max, m + 1)
                vec.scalar_tensor_tensor(w, w, 2.0, adj_tile(NB + m), ALU.min, ALU.mult).then_inc(pair_w, 1)
            dve.wait_ge(den_ps, 1)
            dve.wait_ge(self_exp, 1)
            link(vec.scalar_tensor_tensor(nd(N_INV), PS[:, 7, 0:NB], 1.0 / CSCALE, nd(N_SELF), ALU.mult, ALU.add))
            link(ts(nd(N_INV), nd(N_INV), 1e-16, None, ALU.add))
            link(vec.reciprocal(nd(N_INV), nd(N_INV)))
            link(tt(nd(N_SELF), nd(N_SELF), nd(N_INV), ALU.mult))
            link(ts(nd(N_INV), nd(N_INV), 1.0 / CSCALE, None, ALU.mult))
            for g in range(NG):
                bs = slice(blocks(g)[0], blocks(g)[-1] + 1)
                nb = len(blocks(g))
                dve.wait_ge(acc_T, g + 1)
                tt(X[:, bs, :], ps_rows(g % 2, g, D), nodes[:, N_INV, bs].unsqueeze(2).to_broadcast([P, nb, D]), ALU.mult).then_inc(acc_used, 1)
            own = rows(R, D)
            link(tt(own, hx[:, :, 0:D], nd(N_SELF).unsqueeze(2).to_broadcast([P, NB, D]), ALU.mult))
            dve.wait_ge(acc_used, NG)
            link(tt(X[:, :, :], X[:, :, :], own, ALU.add))
            link(tt(X[:, :, :], X[:, :, :], bias[:, GAT3:GAT3 + 1, :].to_broadcast([P, NB, D]), ALU.add))
            link(tt(X[:, :, :], X[:, :, :], XRES[:, :, :], ALU.add))
            layer_norm(X, XRES, x_ready)

            dense_out(CF)
            dve.wait_ge(h_sb, NG * (CF + 1))
            link(tt(X[:, :, :], rows(Hx, D), XRES[:, :, :], ALU.add))
            layer_norm(X, XRES, x_ready)

            for r in range(2):
                d = CF + 1 + r
                dense_out(d)
                hx = rows(Hx, D)
                for g in range(NG):
                    bs = slice(blocks(g)[0], blocks(g)[-1] + 1)
                    nb = len(blocks(g))
                    dve.wait_ge(gcn_T, r * NG + g + 1)
                    link(vec.scalar_tensor_tensor(X[:, bs, :], ps_rows(g % 2, g, D), 1.0 / CSCALE, hx[:, bs, :], ALU.mult, ALU.add))
                    link(tt(X[:, bs, :], X[:, bs, :], nodes[:, N_DINV, bs].unsqueeze(2).to_broadcast([P, nb, D]), ALU.mult))
                    tt(X[:, bs, :], X[:, bs, :], bias[:, d:d + 1, :].to_broadcast([P, nb, D]), ALU.add).then_inc(gcn_out, 1)
                dve.wait_ge(gcn_out, NG * (r + 1))
                if r == 0:
                    dve.sem_inc(x_ready, 1)
            link(tt(XRES[:, :, :], X[:, :, :], XRES[:, :, :], ALU.add))
            layer_norm(XRES, X, out_ready)


def kernel(**inputs):
    import concourse.bacc as bacc
    from concourse.bass_utils import run_bass_kernel_spmd

    def padded(a, n, fill=0):
        a = np.asarray(a)
        return np.concatenate([a, np.full((n - a.shape[0],) + a.shape[1:], fill, a.dtype)])

    arrays = {name: np.asarray(a) for name, a in inputs.items()}
    for name, n, fill in (("x", NP_, 0), ("node_type_100", NP_, 0), ("src", EP, 0), ("dst", EP, N),
                          ("edge_weight", EP, 0), ("edge_attr_64", EP, 0)):
        arrays[name] = padded(arrays[name], n, fill)
    nc = bacc.Bacc("TRN2", target_bir_lowering=False, num_devices=1)
    feed, aps = {}, {}
    for name, a in arrays.items():
        feed[f"in_{name}"] = np.ascontiguousarray(a)
        aps[name] = nc.dram_tensor(f"in_{name}", a.shape, mybir.dt.from_np(a.dtype), kind="ExternalInput").ap()
    out = nc.dram_tensor("out_nodes", (N, D), mybir.dt.float32, kind="ExternalOutput").ap()
    program(nc, aps, out)
    r = run_bass_kernel_spmd(nc, [feed], core_ids=[0])
    return r.results[0]["out_nodes"]
```

```python
from contextlib import ExitStack

import numpy as np
import concourse.bass as bass
from concourse import mybir

P = 128
N, E, D = 3125, 100000, 128
NB = -(-N // P)
NP_ = NB * P
T = 784
EP = P * T
SLOTS = 4
CT = 14
CT0 = 7
NRBF = 64
SKIP = 1 << 20
BIG = 3.0e38
GB = 3
NG = -(-NB // GB)
NL0 = 5
HEADS = 4
GE = 4
NGRP = EP // (GE * P)
NITEM = NGRP + NB - 1
IPP = T // CT - 1
NSLOT = (NL0 - 1) * IPP
NBANK = -(-NB // 4)
assert NITEM <= NSLOT and T % CT == 0
CSCALE = 2.0 ** 40
SZ = CT * (D + 2 * HEADS)

PASSES = [dict(kind="first", H=0, RW=2 * D, W=D, CT=CT0)]
PASSES += [dict(kind="max", H=0, RW=D, W=D, CT=CT) for _ in range(NL0 - 1)]
PASSES += [dict(kind="gat", H=HEADS, RW=D + 2 * HEADS, W=D + 2 * HEADS, CT=CT) for _ in range(2)]
NPASS = len(PASSES)
for k, ps in enumerate(PASSES):
    ps["ITER"] = T // ps["CT"] // SLOTS
    ps["slot_base"] = sum(q["ITER"] for q in PASSES[:k])
    ps["gath_base"] = 16 * (T // SLOTS) * k
GAT1, GAT2, GAT3, CF, GCN1, GCN2 = 5, 6, 7, 8, 9, 10
NDENSE = 11
POST = [range(0, 4), range(4, 7), range(7, NG)]
WIDTH = [D] * NL0 + [D + 2 * HEADS, D + 2 * HEADS, D + 2] + [D] * 3


def program(nc, A, out):
    fp32, i32, i16, bf16 = mybir.dt.float32, mybir.dt.int32, mybir.dt.int16, mybir.dt.bfloat16
    ALU, ACT, AX = mybir.AluOpType, mybir.ActivationFunctionType, mybir.AxisListType
    ctx = ExitStack()
    with ctx:
        def sb(name, shape, dt=fp32):
            return ctx.enter_context(nc.sbuf_tensor(name, shape, dt))

        def sem(name):
            return ctx.enter_context(nc.semaphore(name))

        def dram(name, shape):
            return nc.dram_tensor(name, shape, fp32, kind="Internal").ap()

        table = {w: dram(f"table{w}", (NP_, w)) for w in (2 * D, D, D + 2 * HEADS)}
        runs = {w: dram(f"runs{w}", (EP, w)) for w in (D, D + 2 * HEADS)}
        adj = dram("adj", (NP_, NP_))
        runs_cf = dram("runs_cf", (EP, D))
        starts_ad = dram("starts_ad", (EP, HEADS))

        edges = sb("edges", [P, 5 * T + SLOTS * CT])
        dst_f, keep01, keepM, gate = (edges[:, q * T:(q + 1) * T] for q in range(4))
        src_i = edges[:, 4 * T:].bitcast(i32)
        idx = [sb(f"idx{b}", [P, CT], i32) for b in range(SLOTS)]
        G_all = sb("G_all", [P, SLOTS * SZ])
        G = [G_all[:, b * SZ:(b + 1) * SZ] for b in range(SLOTS)]
        S_all = sb("S_all", [P, SLOTS * SZ])
        S = [S_all[:, b * SZ:(b + 1) * SZ] for b in range(SLOTS)]
        X = sb("X", [P, NB, D])
        XRES = sb("XRES", [P, NB, D])
        R = sb("R", [P, NB * (D + 8)])
        Hx = sb("Hx", [P, NB * (D + 8)])
        dst_i = Hx[:, 0:T].bitcast(i32)
        xT = sb("xT", [P, NP_])
        aggT = sb("aggT", [P, NP_])
        AGG = aggT[:, :].rearrange("p (b d) -> p b d", d=D)
        EMB = S_all[:, 0:NB * D].rearrange("p (b d) -> p b d", d=D)
        ad_e = sb("ad_e", [P, 4, NP_ // 4])
        ident = sb("ident", [P, P])
        shift = sb("shift", [P, P])
        wrap = sb("wrap", [P, P])
        WR = sb("WR", [P, NDENSE + 1, D + 8])
        bias = sb("bias", [P, NDENSE, D])
        w_raw = aggT[:, 3 * T:3 * T + NL0 * D].rearrange("p (l d) -> p l d", d=D)
        wT = sb("wT", [P, D])
        att = sb("att", [P, 3, 2])
        att_m = sb("att_m", [P, 3, 8])
        head_of = sb("head_of", [P, 4])
        head_rows = sb("head_rows", [4, P])
        ones_row = sb("ones_row", [1, P])
        wd = sb("wd", [NRBF + 1, D])
        aux = sb("aux", [P, 2 * CT0 * P + SLOTS * CT0 * NRBF])
        eaT_all = aux[:, 0:2 * CT0 * P]
        eaT = eaT_all[0:NRBF + 1, :].rearrange("p (h n) -> p h n", h=2)
        ea_all = aux[:, 2 * CT0 * P:]
        ea = [ea_all[:, b * CT0 * NRBF:(b + 1) * CT0 * NRBF] for b in range(SLOTS)]
        item_src = eaT_all[:, 0:GE * NSLOT].rearrange("p (t i) -> p t i", t=GE)
        item_dst = eaT_all[:, GE * NSLOT:2 * GE * NSLOT].rearrange("p (t i) -> p t i", t=GE)
        item_keep = gate[:, 0:NSLOT]
        item_blk = gate[:, NSLOT:2 * NSLOT].bitcast(i32)
        item_last = gate[:, 2 * NSLOT:3 * NSLOT].bitcast(i32)
        iota_n = ea_all[:, 0:NP_ // 2].bitcast(i16)
        src_hot = [buf[:, j * (NP_ // 2):(j + 1) * (NP_ // 2)].bitcast(bf16) for buf in (xT, R) for j in range(2)]
        dst_hot = sb("dst_hot", [P, GE, P], bf16)
        counts = ad_e[:, :, :].rearrange("p h t -> p (h t)")
        rows_a = [S_all[:, 2 * SZ + q * GE * P:2 * SZ + (q + 1) * GE * P] for q in range(3)] + [S[3][:, 0:GE * P]]
        big_max = xT[:, :]
        dst_row = [S_all[:, j * NP_:(j + 1) * NP_] for j in range(2)]
        pos_exp = [R[:, 0:NP_], xT[:, :]]
        soft_w = [counts, X[:, :, :].rearrange("p b d -> p (b d)"), edges[:, 0:NP_]]
        den_sum = aux[:, 0:NP_]
        nval = sb("nval", [P, NB])
        ztype = sb("ztype", [P, NB], i32)
        small = sb("small", [P, 64])
        nodes = sb("nodes", [P, 16, NB])
        nodes_i = sb("nodes_i", [P, 3, NB], i32)
        edge_i = sb("edge_i", [P, 5], i32)
        kB01 = sb("kB01", [P, P])
        kBM = sb("kBM", [P, P])
        V = sb("V", [P, P + 1])
        V2 = sb("V2", [P, P + 1])
        mV = sb("mV", [4, P + 1])
        dV = sb("dV", [4, P + 1])
        DD = sb("DD", [4, 2, P])
        EE = sb("EE", [4, 2, P])
        prevm = sb("prevm", [4, P])
        denT = sb("denT", [4, P])
        FX = sb("FX", [P, D + 8])
        FX2 = sb("FX2", [P, D + 8])
        ad0 = sb("ad0", [P, D + 8])
        fxm = sb("fxm", [P, 3, 4])
        fxe = sb("fxe", [P, 2, 4])
        zc = sb("zc", [P, CT, 4])
        ec = sb("ec", [P, CT, 4])
        mbuf = sb("mbuf", [P, CT + 1, 4])
        mp = sb("mp", [P, CT, 4])
        dc = sb("dc", [P, 2, CT, 4])
        pc = sb("pc", [P, 2, CT, 4])
        tmpr = sb("tmpr", [P, D])
        tmpg = ea_all[:, 8 * NB * 4:8 * NB * 4 + GB * D].rearrange("p (b d) -> p b d", d=D)
        stats = ea_all[:, NP_ // 2:NP_ // 2 + 6 * NB].rearrange("p (b s) -> p b s", s=6)
        mv = sb("mv", [P, NB, 2])
        na = ea_all[:, 0:8 * NB * 4].rearrange("p (q n) -> p q n", q=8)
        PS = ctx.enter_context(nc.psum_tensor("PS", [P, 8, 512], fp32))

        (N_CNT, N_END, N_START, N_DEG, N_HAS, N_DINV, N_P, N_T0, N_T1, N_FREE, N_HI, N_BLK, N_DSC) = range(13)
        (N_POS, N_MAX, N_ROW1, N_ROW2, N_NEG, N_SELF, N_INV, N_E1) = (N_CNT, N_END, N_START, N_P, N_T0, N_T1, N_FREE, N_HI)
        def nd(i):
            return nodes[:, i, :]

        edges_in = sem("edges_in")
        setup_in = sem("setup_in")
        ready_const = sem("ready_const")
        chain_v = sem("chain_v")
        chain_g = sem("chain_g")
        ends_rows = [sem(f"ends_rows{b}") for b in range(SLOTS)]
        ends_used = sem("ends_used")
        emb_rows = sem("emb_rows")
        emb_stored = sem("emb_stored")
        part_ready = sem("part_ready")
        part_rows = sem("part_rows")
        flag_ready = sem("flag_ready")
        flag_rows = sem("flag_rows")
        p_ready = sem("p_ready")
        cnt_ready = sem("cnt_ready")
        start_ps = sem("start_ps")
        nodes_ready = sem("nodes_ready")
        deg_ready = sem("deg_ready")
        dinv_root = sem("dinv_root")
        cos_arg = sem("cos_arg")
        go = sem("go")
        cos_done = sem("cos_done")
        w_ps = sem("w_ps")
        w_sb = sem("w_sb")
        att_ready = sem("att_ready")
        zero_ready = sem("zero_ready")
        zero_stored = sem("zero_stored")
        x_ready = sem("x_ready")
        xT_ps = sem("xT_ps")
        xT_sb = sem("xT_sb")
        h_ps = sem("h_ps")
        h_sb = sem("h_sb")
        agg_ready = sem("agg_ready")
        aggT_ps = sem("aggT_ps")
        aggT_sb = sem("aggT_sb")
        table_stored = sem("table_stored")
        ad_scattered = sem("ad_scattered")
        ad_first = sem("ad_first")
        ad_loaded = sem("ad_loaded")
        idx_staged = [sem(f"idx_staged{b}") for b in range(SLOTS)]
        gathered = [sem(f"gathered{b}") for b in range(SLOTS)]
        chunk_done = [sem(f"chunk_done{b}") for b in range(SLOTS)]
        run_stored = [sem(f"run_stored{b}") for b in range(SLOTS)]
        ea_in = [sem(f"ea_in{b}") for b in range(SLOTS)]
        ea_ps = sem("ea_ps")
        ea_sb = sem("ea_sb")
        filt_ps = sem("filt_ps")
        filt_used = sem("filt_used")
        soft_arg = sem("soft_arg")
        soft_exp = sem("soft_exp")
        tail_T = sem("tail_T")
        tail_V = sem("tail_V")
        tail_C = sem("tail_C")
        tail_B = sem("tail_B")
        tail_arg = sem("tail_arg")
        tail_exp = sem("tail_exp")
        fix_in = sem("fix_in")
        fix_arg = sem("fix_arg")
        fix_exp = sem("fix_exp")
        fix_new = sem("fix_new")
        fix_out = sem("fix_out")
        end_in = [sem(f"end_in{g}") for g in range(NG)]
        cf_in = sem("cf_in")
        cf_ready = sem("cf_ready")
        post_arg = sem("post_arg")
        post_exp = sem("post_exp")
        ln_var = sem("ln_var")
        ln_std = sem("ln_std")
        item_idx = sem("item_idx")
        item_rows = sem("item_rows")
        item_f = sem("item_f")
        item_ps = sem("item_ps")
        item_tab = sem("item_tab")
        hi_ps = sem("hi_ps")
        iota_ready = sem("iota_ready")
        hot_ready = sem("hot_ready")
        item_sum = sem("item_sum")
        item_added = sem("item_added")
        item_stored = sem("item_stored")
        adj_in = [sem(f"adj_in{b}") for b in range(SLOTS)]
        adj_used = sem("adj_used")
        min_ready = sem("min_ready")
        min_T = sem("min_T")
        min_one = sem("min_one")
        min_ps = sem("min_ps")
        max_ready = sem("max_ready")
        max_T = sem("max_T")
        max_used = sem("max_used")
        rows_ready = sem("rows_ready")
        rows_ps = sem("rows_ps")
        rows_sb = sem("rows_sb")
        pair_exp = sem("pair_exp")
        pair_max = sem("pair_max")
        pair_w = sem("pair_w")
        pair_mm = sem("pair_mm")
        pair_den = sem("pair_den")
        den_clear = sem("den_clear")
        self_arg = sem("self_arg")
        self_exp = sem("self_exp")
        acc_sb = sem("acc_sb")
        acc_T = sem("acc_T")
        acc_used = sem("acc_used")
        den_ps = sem("den_ps")
        gcn_ps = sem("gcn_ps")
        gcn_sb = sem("gcn_sb")
        gcn_T = sem("gcn_T")
        gcn_out = sem("gcn_out")
        out_ready = sem("out_ready")
        out_stored = sem("out_stored")

        def rows(buf, w):
            return buf[:, 0:NB * w].rearrange("p (b w) -> p b w", w=w)

        def node_rows(ap):
            return ap.rearrange("(b p) w -> p b w", p=P)

        def blocks(g):
            return range(GB * g, min(NB, GB * g + GB))

        def span(g):
            return slice(blocks(g)[0], blocks(g)[-1] + 1)

        def src_of(d):
            return XRES if d in (0, GAT1, CF, GCN1) else X

        def g_rows(b, ps):
            return G[b][:, 0:ps["CT"] * ps["RW"]].rearrange("p (t w) -> p t w", w=ps["RW"])

        def s_rows(b, ps):
            return S[b][:, 0:ps["CT"] * ps["W"]].rearrange("p (t w) -> p t w", w=ps["W"])

        def s_cf(b):
            return S[b][:, CT0 * D:2 * CT0 * D].rearrange("p (t w) -> p t w", w=D)

        def ps_rows(bank, g, w):
            return PS[:, bank, 0:w * len(blocks(g))].rearrange("p (b w) -> p b w", w=w)

        def psum_row():
            return PS[:, 0:7, :].rearrange("p k c -> p (k c)")[:, 0:NP_]

        def kind_max(ps):
            return ps["kind"] == "max"

        def tail_bank(ps):
            return NBANK if kind_max(ps) else 6

        def adj_slot(q):
            def slot(r):
                return (r - NB) % 2 if NB <= r < 2 * NB else (r % SLOTS if r < NB else (r - 2 * NB) % SLOTS)
            return slot(q), sum(slot(r) == slot(q) for r in range(q + 1))

        def adj_tile(q):
            slot = adj_slot(q)[0]
            return (G_all, S_all)[slot // 2][:, (slot % 2) * NP_:(slot % 2 + 1) * NP_]

        def adj_wait(eng, q):
            slot, n = adj_slot(q)
            eng.wait_ge(adj_in[slot], 16 * n)

        block = ctx.enter_context(nc.Block())

        N_SETUP = 0

        @block.sync
        def _(sp):
            nonlocal N_SETUP
            def load(dst, src):
                nonlocal N_SETUP
                N_SETUP += 1
                sp.dma_start(dst, src).then_inc(setup_in, 16)

            for tile, name in ((dst_i, "dst"), (src_i, "src"), (gate, "edge_weight")):
                sp.dma_start(tile[:, 0:T], A[name].rearrange("(p t) -> p t", t=T)).then_inc(edges_in, 16)
            with nc.allow_non_contiguous_dma(reason="small vector, once"):
                sp.dma_start(ztype[:, :], A["node_type_100"].rearrange("(b p) -> p b", p=P)).then_inc(edges_in, 16)
            load(XRES[:, :, :], node_rows(A["x"]))
            load(w_raw[:, :, :], A["L0_gnn_Ws"].rearrange("l o d -> o l d"))
            with nc.allow_non_contiguous_dma(reason="small vectors, once"):
                for j in range(3):
                    load(att[:, j, 0:1], A[f"L1_gnn_as{j + 1}"].rearrange("h (c o) -> (h c) o", o=1))
                    load(att[:, j, 1:2], A[f"L1_gnn_ad{j + 1}"].rearrange("h (c o) -> (h c) o", o=1))
            for j in range(3):
                load(WR[:, GAT1 + j, 0:D], A[f"L1_gnn_W{j + 1}"])
                load(bias[:, GAT1 + j, :], A[f"L1_gnn_b{j + 1}"].rearrange("(o d) -> o d", o=1).to_broadcast([P, D]))
            load(WR[:, CF, 0:D], A["L2_gnn_Wc"][0:D, :])
            load(WR[:, NDENSE, 0:D], A["L2_gnn_Wc"][D:2 * D, :])
            load(WR[:, GCN1, 0:D], A["L3_gnn_W1"])
            load(WR[:, GCN2, 0:D], A["L3_gnn_W2"])
            for d, n in ((CF, "L2_gnn_bc"), (GCN1, "L3_gnn_b1"), (GCN2, "L3_gnn_b2")):
                load(bias[:, d, :], A[n].rearrange("(o d) -> o d", o=1).to_broadcast([P, D]))
            for l in range(NL0):
                load(bias[:, l, :], A["L0_gnn_bs"][l:l + 1, :].to_broadcast([P, D]))
            load(wd[0:NRBF, :], A["L2_gnn_Wd"])
            load(wd[NRBF:NRBF + 1, :], A["L2_gnn_bd"].rearrange("(o d) -> o d", o=1))
            ea_view = A["edge_attr_64"].rearrange("(p t) c -> p (t c)", t=T)

            def load_ea(c, b):
                sp.dma_start(ea[b][:, :], ea_view[:, bass.ds(c * CT0 * NRBF, CT0 * NRBF)]).then_inc(ea_in[b], 16)

            for b in range(SLOTS):
                load_ea(b, b)
            sp.wait_ge(zero_ready, 1)
            sp.dma_start(starts_ad.rearrange("(p t) h -> p (t h)", t=T), ad_e[:, :, :].rearrange("p h t -> p (h t)")[:, 0:T * HEADS]).then_inc(zero_stored, 16)
            sp.wait_ge(emb_rows, 16 * NB)
            sp.dma_start(node_rows(table[2 * D])[:, :, D:2 * D], EMB[:, :, :]).then_inc(emb_stored, 16)

            for k, ps in enumerate(PASSES):
                ct, w, H, base = ps["CT"], ps["W"], ps["H"], ps["slot_base"]
                for g in range(NG):
                    sp.wait_ge(h_sb, NG * k + g + 1)
                    sp.dma_start(node_rows(table[ps["RW"]])[:, span(g), 0:WIDTH[k]], rows(Hx, WIDTH[k])[:, span(g), :]).then_inc(table_stored, 16)
                if H:
                    j = k - GAT1
                    sp.wait_ge(ad_scattered, 16 * NB * (j + 1))
                    sp.dma_start(R[:, 0:T * H], starts_ad.rearrange("(p t) h -> p (t h)", t=T)).then_inc(ad_loaded, 16)
                run_view = runs[w].rearrange("(p t) w -> p (t w)", t=T)
                cf_view = runs_cf.rearrange("(p t) w -> p (t w)", t=T)

                def store_block(item):
                    blk = sp.value_load(item_blk[0:1, bass.ds(item, 1)], min_val=0, max_val=NB - 1)
                    ends = sp.value_load(item_last[0:1, bass.ds(item, 1)], min_val=0, max_val=1)
                    sp.wait_ge(item_added, NBANK * item + NBANK)
                    sp.dma_start(adj.rearrange("(b p) d -> p b d", p=P)[:, :, bass.ds(blk * P, P)],
                                 counts.rearrange("p (b d) -> p b d", d=P), cond=ends).then_inc(item_stored, 16)

                def store(i, last=False):
                    for b in range(SLOTS):
                        c = i * SLOTS + b
                        if kind_max(ps) and not (last and b == SLOTS - 1):
                            store_block((k - 1) * IPP + c)
                        sp.wait_ge(chunk_done[b], base + i + 1)
                        sp.dma_start(run_view[:, bass.ds(c * ct * w, ct * w)], S[b][:, 0:ct * w]).then_inc(run_stored[b], 16)
                        if ps["kind"] == "first":
                            sp.dma_start(cf_view[:, bass.ds(c * ct * w, ct * w)], S[b][:, ct * w:2 * ct * w]).then_inc(run_stored[b], 16)
                        if ps["kind"] == "first":
                            if not last:
                                sp.wait_ge(ea_ps, c + 1)
                                load_ea(c + SLOTS, b)

                if k == 1:
                    sp.wait_ge(item_tab, 1)
                store(0)
                with sp.Fori(1, ps["ITER"] - 1) as i:
                    store(i)
                store(ps["ITER"] - 1, last=True)
            n_out = 0
            for b in range(SLOTS):
                sp.wait_ge(chunk_done[b], PASSES[-1]["slot_base"] + PASSES[-1]["ITER"])
                sp.wait_ge(run_stored[b], 16 * (PASSES[-1]["slot_base"] + PASSES[-1]["ITER"] + PASSES[0]["ITER"]))
            sp.wait_ge(tail_T, NPASS)
            for g in range(NG):
                sp.wait_ge(end_in[g], 16 * len(blocks(g)) * NPASS)
            sp.wait_ge(item_stored, 16 * NSLOT)
            for q in range(4 * NB):
                if SLOTS <= q < NB:
                    sp.wait_ge(adj_used, q - SLOTS + 1)
                elif NB <= q < NB + 2:
                    sp.wait_ge(adj_used, NB)
                elif NB + 2 <= q < 2 * NB:
                    sp.wait_ge(pair_w, q - NB - 1)
                elif 2 * NB <= q < 2 * NB + SLOTS:
                    sp.wait_ge(pair_w, NB)
                elif q >= 2 * NB + SLOTS:
                    sp.wait_ge(adj_used, q - NB - SLOTS + 1)
                sp.dma_start(adj_tile(q), adj[(q % NB) * P:(q % NB + 1) * P, :]).then_inc(adj_in[adj_slot(q)[0]], 16)
            for g in range(NG):
                sp.wait_ge(out_ready, g + 1)
                a, n = blocks(g)[0] * P, min(N - blocks(g)[0] * P, len(blocks(g)) * P)
                full = n // P
                if full:
                    sp.dma_start(out[a:a + full * P, :].rearrange("(b p) d -> p b d", p=P), X[:, blocks(g)[0]:blocks(g)[0] + full, :]).then_inc(out_stored, 16)
                    n_out += 1
                if n % P:
                    sp.dma_start(out[a + full * P:a + n, :], X[0:n % P, blocks(g)[0] + full, :]).then_inc(out_stored, 16)
                    n_out += 1
            sp.wait_ge(out_stored, 16 * n_out)

        @block.gpsimd
        def _(gp):
            count = 0

            def link(ins):
                nonlocal count
                count += 1
                ins.then_inc(chain_g, 1)
                gp.wait_ge(chain_g, count)

            link(nc.gpsimd.memset(ident[:, :], 0.0))
            link(nc.gpsimd.memset(shift[:, :], 0.0))
            link(nc.gpsimd.memset(wrap[:, :], 0.0))
            link(nc.gpsimd.memset(head_of[:, :], 1.0))
            link(nc.gpsimd.memset(head_rows[:, :], 1.0))
            for tile, base in ((ident, 0), (shift, 1), (wrap, -(P - 1))):
                link(nc.gpsimd.affine_select(out=tile[:, :], in_=tile[:, :], compare_op=ALU.not_equal, fill=1.0,
                                             base=base, pattern=[[-1, P]], channel_multiplier=1))
            C = D // 4
            link(nc.gpsimd.affine_select(out=head_of[:, :], in_=head_of[:, :], compare_op=ALU.is_ge, fill=0.0,
                                         base=0, pattern=[[-C, 4]], channel_multiplier=1))
            link(nc.gpsimd.affine_select(out=head_of[:, :], in_=head_of[:, :], compare_op=ALU.is_ge, fill=0.0,
                                         base=C - 1, pattern=[[C, 4]], channel_multiplier=-1))
            link(nc.gpsimd.affine_select(out=head_rows[:, :], in_=head_rows[:, :], compare_op=ALU.is_ge, fill=0.0,
                                         base=0, pattern=[[1, P]], channel_multiplier=-C))
            link(nc.gpsimd.affine_select(out=head_rows[:, :], in_=head_rows[:, :], compare_op=ALU.is_ge, fill=0.0,
                                         base=C - 1, pattern=[[-1, P]], channel_multiplier=C))
            link(nc.gpsimd.iota(small[:, 0:1], pattern=[[0, 1]], base=0, channel_multiplier=T, allow_small_or_imprecise_dtypes=True))
            link(nc.gpsimd.iota(nd(N_BLK), pattern=[[1, NB]], base=0, channel_multiplier=0, allow_small_or_imprecise_dtypes=True))
            nc.gpsimd.iota(nval[:, :], pattern=[[P, NB]], base=0, channel_multiplier=1,
                           allow_small_or_imprecise_dtypes=True).then_inc(ready_const, 1)

            def gather(dst, src, ix, s):
                gp.indirect_dma_start(out=dst, out_offset=None, in_=src,
                                      in_offset=bass.IndirectOffsetOnAxis(ap=ix, axis=0)).then_inc(s, 16)

            gp.wait_ge(edges_in, 64)
            for b in range(NB):
                gather(EMB[:, b, :], A["L2_gnn_emb"], ztype[:, b:b + 1], emb_rows)
            gp.wait_ge(p_ready, 1)
            for b in range(NB):
                if b >= SLOTS:
                    gp.wait_ge(ends_used, b - SLOTS + 1)
                gather(G[b % SLOTS][:, 0:T].bitcast(i32), A["dst"].rearrange("(p t) -> p t", t=T),
                       nodes_i[:, 2, b:b + 1], ends_rows[b % SLOTS])
            gp.wait_ge(ends_used, NB)

            for k, ps in enumerate(PASSES):
                ct, w, H, base, rw = ps["CT"], ps["W"], ps["H"], ps["slot_base"], ps["RW"]
                if k == 0:
                    gp.wait_ge(emb_stored, 16)
                if H:
                    gp.wait_ge(zero_stored, 16)
                    hv = rows(Hx, rw)
                    for b in range(NB):
                        if b % GB == 0:
                            gp.wait_ge(h_sb, NG * k + b // GB + 1)
                        gp.indirect_dma_start(out=starts_ad, out_offset=bass.IndirectOffsetOnAxis(ap=nodes_i[:, 1, b:b + 1], axis=0),
                                              in_=hv[:, b, D + H:D + 2 * H], in_offset=None,
                                              bounds_check=EP - 1, oob_is_err=False).then_inc(ad_scattered, 16)
                gp.wait_ge(table_stored, 16 * NG * (k + 1))
                if H:
                    gather(ad0[:, 0:rw], table[rw], edge_i[:, 2:3], ad_first)

                def gathers(i, first=False):
                    for b in range(SLOTS):
                        gr = g_rows(b, ps)
                        if not (first and k == 0):
                            gp.wait_ge(chunk_done[b], base + i)
                        gp.wait_ge(idx_staged[b], base + i + 1)
                        gp.sem_inc(go, 1)
                        for t in range(ct):
                            gather(gr[:, t, :], table[rw], idx[b][:, t:t + 1], gathered[b])

                gathers(0, first=True)
                with gp.Fori(1, ps["ITER"]) as i:
                    gathers(i)
                if k == 0:
                    gp.wait_ge(nodes_ready, 1)
                if k in (1, 2):
                    for b in (range(NB // 2), range(NB // 2, NB))[k - 1]:
                        gather(AGG[:, b, :], runs_cf, nodes_i[:, 0, b:b + 1], cf_in)
                seams = [(runs[w], FX)] + ([(runs_cf, FX2)] if ps["kind"] == "first" else [])
                n0 = k + (1 if k else 0)
                for b in range(SLOTS):
                    stored = 16 * (base + ps["ITER"] + PASSES[0]["ITER"])
                    gp.wait_ge(run_stored[b], stored)
                for r, fx in seams:
                    gather(fx[:, 0:w], r, edge_i[:, 0:1], fix_in)
                gp.wait_ge(fix_new, k + 1)
                for r, fx in seams:
                    gp.indirect_dma_start(out=r, out_offset=bass.IndirectOffsetOnAxis(ap=edge_i[:, 1:2], axis=0),
                                          in_=fx[:, 0:w], in_offset=None,
                                          bounds_check=EP - 1, oob_is_err=False).then_inc(fix_out, 16)
                gp.wait_ge(fix_out, 16 * (n0 + len(seams)))
                rv = rows(R, w)
                for b in range(NB):
                    gather(rv[:, b, :], runs[w], nodes_i[:, 0, b:b + 1], end_in[b // GB])
                if k == 0:
                    gp.wait_ge(item_idx, 1)
                    for q, name in enumerate(("src", "dst")):
                        edges = A[name].rearrange("(g e) -> g e", e=GE * P)
                        for half, m in ((0, P), (1, NSLOT - P)):
                            gather(rows_a[2 * q + half][0:m, :].bitcast(i32), edges, edge_i[0:m, 3 + half:4 + half], item_rows)
                    nc.gpsimd.iota(iota_n, pattern=[[1, NP_]], base=0, channel_multiplier=0).then_inc(iota_ready, 1)
            gp.wait_ge(min_ready, 1)
            nc.gpsimd.memset(den_sum, 0.0).then_inc(den_clear, 1)
            gp.wait_ge(den_clear, 1)
            for m in range(NB):
                gp.wait_ge(pair_w, m + 1)
                if m:
                    gp.wait_ge(pair_den, m)
                nc.gpsimd.tensor_tensor(den_sum, den_sum, soft_w[m % 3], ALU.add).then_inc(pair_den, 1)

        @block.scalar
        def _(act):
            act.wait_ge(setup_in, 16 * N_SETUP)
            n_w = 0

            def weight(dst, src):
                nonlocal n_w
                n_w += 1
                act.wait_ge(w_ps, n_w)
                nc.scalar.copy(dst, src).then_inc(w_sb, 1)

            def transposed(dst, ps_sem, sb_sem, g, n0):
                m = P * len(blocks(g))
                act.wait_ge(ps_sem, n0 + g + 1)
                if g == 0 and sb_sem is xT_sb and n0:
                    act.wait_ge(h_ps, n0)
                nc.scalar.copy(dst[:, GB * P * g:GB * P * g + m], PS[:, g % 2, 0:m]).then_inc(sb_sem, 1)

            weight(WR[:, 0, 0:D], PS[:, 4, 0:D])
            act.wait_ge(p_ready, 1)
            for g in range(NG):
                transposed(xT, xT_ps, xT_sb, g, 0)
            for l in range(1, NL0):
                weight(WR[:, l, 0:D], PS[:, 4, 0:D])
            for j, h in enumerate((HEADS, HEADS, 1)):
                weight(wT[:, :], PS[:, 4, 0:D])
                weight(WR[:, GAT1 + j, D:D + 2 * h], PS[:, 4, 0:2 * h])
            act.wait_ge(cos_arg, 1)
            nc.scalar.activation(gate[:, :], gate[:, :], ACT.Sin).then_inc(cos_done, 1)
            act.wait_ge(deg_ready, 1)
            nc.scalar.activation(nd(N_T0), nd(N_T0), ACT.Sqrt).then_inc(dinv_root, 1)

            n_tail = n_fix = n_ln = 0

            def norms(d=None):
                nonlocal n_ln
                for g in range(NG + 1):
                    if g < NG:
                        act.wait_ge(ln_var, n_ln + g + 1)
                        nc.scalar.activation(mv[:, span(g), 1], mv[:, span(g), 1], ACT.Sqrt).then_inc(ln_std, 1)
                    if g and d is not None:
                        transposed(xT, xT_ps, xT_sb, g - 1, NG * d)
                n_ln += NG

            def layer_function(f, k, g):
                act.wait_ge(agg_ready, NG * (k if k < NL0 - 1 else k - 1) + g + 1)
                nc.scalar.activation(X[:, span(g), :], X[:, span(g), :], f).then_inc(x_ready, 1)
                transposed(xT, xT_ps, xT_sb, g, NG * (k + 1))

            def stage(ct, i, b):
                nc.scalar.copy(idx[b][:, 0:ct], src_i[:, bass.ds((i * SLOTS + b) * ct, ct)]).then_inc(idx_staged[b], 1)

            for b in range(SLOTS):
                stage(CT0, 0, b)
            for k, ps in enumerate(PASSES):
                ct, H, base, kind = ps["CT"], ps["H"], ps["slot_base"], ps["kind"]
                gbase = ps["gath_base"]

                def chunk_work(i):
                    for b in range(SLOTS):
                        c = i * SLOTS + b
                        if kind == "first":
                            act.wait_ge(ea_ps, c + 1)
                            if not (isinstance(i, int) and c < 2):
                                act.wait_ge(filt_ps, c - 1)
                            for hf, m in ((0, 4), (1, 3)):
                                ins = nc.scalar.copy(eaT[0:NRBF, b % 2, hf * 512:hf * 512 + m * P], PS[0:NRBF, hf, 0:m * P])
                            ins.then_inc(ea_sb, 1)
                        if kind == "gat":
                            act.wait_ge(soft_arg, (k - GAT1) * SLOTS * ps["ITER"] + c + 1)
                            nc.scalar.activation(pc[:, :, :, 0:H], dc[:, :, :, 0:H], ACT.Exp).then_inc(soft_exp, 1)
                        act.wait_ge(gathered[b], gbase + 16 * ct * (i + 1))
                        stage(ct, i + 1, b)

                chunk_work(0)
                if ps["ITER"] > 2:
                    with act.Fori(1, ps["ITER"] - 1) as i:
                        chunk_work(i)
                i = ps["ITER"] - 1
                for b in range(SLOTS):
                    c = i * SLOTS + b
                    if kind == "first":
                        act.wait_ge(ea_ps, c + 1)
                        act.wait_ge(filt_ps, c - 1)
                        for hf, m in ((0, 4), (1, 3)):
                            ins = nc.scalar.copy(eaT[0:NRBF, b % 2, hf * 512:hf * 512 + m * P], PS[0:NRBF, hf, 0:m * P])
                        ins.then_inc(ea_sb, 1)
                    if kind == "gat":
                        act.wait_ge(soft_arg, (k - GAT1) * SLOTS * ps["ITER"] + c + 1)
                        nc.scalar.activation(pc[:, :, :, 0:H], dc[:, :, :, 0:H], ACT.Exp).then_inc(soft_exp, 1)
                    act.wait_ge(gathered[b], gbase + 16 * ct * (i + 1))
                    if k + 1 < NPASS:
                        stage(PASSES[k + 1]["CT"], 0, b)
                if kind == "gat":
                    n_tail += 1
                    act.wait_ge(tail_arg, n_tail)
                    nc.scalar.activation(EE[0:H, :, :], DD[0:H, :, :], ACT.Exp).then_inc(tail_exp, 1)
                    n_fix += 1
                    act.wait_ge(fix_arg, n_fix)
                    nc.scalar.activation(fxe[:, :, 0:H], fxm[:, 0:2, 0:H], ACT.Exp).then_inc(fix_exp, 1)
                    for q, groups in enumerate(POST):
                        act.wait_ge(post_arg, len(POST) * (k - GAT1) + q + 1)
                        cs = slice(span(groups[0]).start * H, span(groups[-1]).stop * H)
                        nc.scalar.activation(na[:, 4:6, cs], na[:, 2:4, cs], ACT.Exp).then_inc(post_exp, 1)
                        for g in groups:
                            layer_function(ACT.Relu, k, g)
                elif k < NL0 - 1:
                    for g in range(NG):
                        layer_function(ACT.Silu, k, g)
                else:
                    norms(k + 1)
            for g in range(NG):
                transposed(aggT, aggT_ps, aggT_sb, g, 0)
            for j in range(2):
                act.wait_ge(rows_ps, j + 1)
                nc.scalar.copy(dst_row[j], psum_row()).then_inc(rows_sb, 1)
            act.wait_ge(rows_sb, 2)
            hx = rows(Hx, WIDTH[GAT3])
            for m in range(NB):
                if m >= 2:
                    act.wait_ge(pair_max, m - 1)
                if m >= 3:
                    act.wait_ge(pair_mm, m - 2)
                    act.wait_ge(pair_den, m - 2)
                nc.scalar.activation(pos_exp[m % 2], dst_row[0], ACT.Exp, bias=hx[:, m, D:D + 1])
                nc.scalar.activation(soft_w[m % 3], dst_row[1], ACT.Exp, bias=nodes[:, N_NEG, m:m + 1]).then_inc(pair_exp, 1)
            act.wait_ge(pair_mm, NB)
            act.wait_ge(pair_max, NB)
            nc.scalar.copy(xT[:, :], psum_row()).then_inc(acc_sb, 1)
            act.wait_ge(self_arg, 1)
            nc.scalar.activation(nd(N_SELF), nd(N_SELF), ACT.Exp).then_inc(self_exp, 1)
            norms()
            for g in range(NG):
                transposed(xT, xT_ps, xT_sb, g, NG * CF)
            norms(GCN1)
            for r in range(2):
                act.wait_ge(gcn_ps, r + 1)
                nc.scalar.copy(xT[:, :], psum_row()).then_inc(gcn_sb, 1)
                if r == 0:
                    for g in range(NG):
                        transposed(xT, xT_ps, xT_sb, g, NG * GCN2)
            norms()

        @block.tensor
        def _(pe):
            pe.wait_ge(ready_const, 1)
            pe.wait_ge(part_ready, 1)
            nc.tensor.matmul(PS[:, 5, 0:P], small[:, 1:2].to_broadcast([P, P]), ident[:, :], start=True, stop=True)
            nc.tensor.matmul(PS[:, 5, P:P + 1], shift[:, :], small[:, 1:2], start=True, stop=True).then_inc(part_rows, 1)
            pe.wait_ge(flag_ready, 1)
            nc.tensor.matmul(PS[:, 5, 2 * P:3 * P], small[:, 8:9].to_broadcast([P, P]), ident[:, :], start=True, stop=True).then_inc(flag_rows, 1)
            pe.wait_ge(setup_in, 16 * N_SETUP)
            n_w = 0

            def weight(ins):
                nonlocal n_w
                n_w += 1
                ins.then_inc(w_ps, 1)
                pe.wait_ge(w_sb, n_w)

            def dense(d):
                src, w = src_of(d), WIDTH[d]
                for g in range(NG):
                    if d:
                        pe.wait_ge(x_ready, NG * (d - 1) + g + 1)
                    if g >= 2:
                        pe.wait_ge(xT_sb, NG * d + g - 1)
                    for n, b in enumerate(blocks(g)):
                        ins = nc.tensor.transpose(PS[:, g % 2, n * P:(n + 1) * P], src[:, b, :], ident[:, :])
                    ins.then_inc(xT_ps, 1)
                    if g:
                        product(d, g - 1)
                product(d, NG - 1)

            def product(d, g):
                w = WIDTH[d]
                pe.wait_ge(xT_sb, NG * d + g + 1)
                if NG * d + g >= 2:
                    pe.wait_ge(h_sb, NG * d + g - 1)
                for n, b in enumerate(blocks(g)):
                    o = PS[:, 2 + (NG * d + g) % 2, n * w:(n + 1) * w]
                    ins = nc.tensor.matmul(o, xT[:, b * P:(b + 1) * P], WR[:, d, 0:w], start=True, stop=(d != CF))
                    if d == CF:
                        ins = nc.tensor.matmul(o, aggT[:, b * P:(b + 1) * P], WR[:, NDENSE, 0:w], start=False, stop=True)
                ins.then_inc(h_ps, 1)

            weight(nc.tensor.transpose(PS[:, 4, 0:D], w_raw[:, 0, :], ident[:, :]))
            dense(0)
            for l in range(1, NL0):
                weight(nc.tensor.transpose(PS[:, 4, 0:D], w_raw[:, l, :], ident[:, :]))
            pe.wait_ge(att_ready, 1)
            for j, h in enumerate((HEADS, HEADS, 1)):
                weight(nc.tensor.transpose(PS[:, 4, 0:D], WR[:, GAT1 + j, 0:D], ident[:, :]))
                weight(nc.tensor.matmul(PS[:, 4, 0:2 * h], wT[:, :], att_m[:, j, 0:2 * h], start=True, stop=True))
            pe.wait_ge(cnt_ready, 1)
            nc.tensor.matmul(PS[:, 6, 0:NB], shift[:, :], nd(N_CNT), start=True, stop=False)
            nc.tensor.matmul(PS[:, 6, 0:NB], wrap[:, :], nd(N_T1), start=False, stop=True).then_inc(start_ps, 1)

            nc.tensor.matmul(PS[:, 5, 0:NB], ident[:, P - 1:P].to_broadcast([P, P]), nd(N_CNT), start=True, stop=True).then_inc(hi_ps, 1)

            for k, ps in enumerate(PASSES):
                H, kind, w = ps["H"], ps["kind"], ps["W"]
                if k:
                    dense(k)
                if k == 1:
                    pe.wait_ge(h_sb, 2 * NG)
                    pe.wait_ge(item_f, 1)
                    for q in range(2):
                        for t in range(GE):
                            for half, m in ((0, P), (1, NSLOT - P)):
                                ins = nc.tensor.transpose(PS[:, GE * q + t, half * P:half * P + m],
                                                          rows_a[2 * q + half][0:m, t * P:(t + 1) * P], ident[0:m, 0:m])
                    ins.then_inc(item_ps, 1)
                    pe.wait_ge(item_tab, 1)
                if kind_max(ps):
                    def counts_of(t, j):
                        for m in range(4 * j, min(NB, 4 * j + 4)):
                            ins = nc.tensor.matmul(PS[:, j, m % 4 * P:(m % 4 + 1) * P],
                                                   src_hot[t][:, m * P:(m + 1) * P], dst_hot[:, t, :],
                                                   start=(t == 0 and m % 4 == 0), stop=(t == GE - 1 and (m % 4 == 3 or m == NB - 1)),
                                                   skip_group_check=True)
                        return ins

                    def items(i, first=False, n=SLOTS):
                        for b in range(n):
                            item = (k - 1) * IPP + i * SLOTS + b
                            for t in range(2):
                                pe.wait_ge(hot_ready, item * GE + t + 1)
                                for j in range(NBANK):
                                    if t == 0 and not (k == 1 and first and b == 0):
                                        pe.wait_ge(item_added, NBANK * item - NBANK + j + 1)
                                    counts_of(t, j)
                            pe.wait_ge(hot_ready, item * GE + GE)
                            for j in range(NBANK):
                                for t in range(2, GE):
                                    ins = counts_of(t, j)
                                ins.then_inc(item_sum, 1)

                    if k > 1:
                        pe.wait_ge(h_sb, NG * (k + 1))
                    items(0, first=True)
                    with pe.Fori(1, ps["ITER"] - 1) as i:
                        items(i)
                    items(ps["ITER"] - 1, n=SLOTS - 1)
                if kind == "first":
                    pe.wait_ge(h_sb, NG)
                    pe.wait_ge(item_idx, 1)

                    def filters(i, first=False):
                        for b in range(SLOTS):
                            c = i * SLOTS + b
                            pe.wait_ge(ea_in[b], 16 * (i + 1))
                            if not (first and b == 0):
                                pe.wait_ge(ea_sb, c)
                            pe.sem_inc(go, 1)
                            for t in range(CT0):
                                ins = nc.tensor.transpose(PS[0:NRBF, t // 4, (t % 4) * P:(t % 4 + 1) * P],
                                                          ea[b][:, t * NRBF:(t + 1) * NRBF], ident[:, :])
                            ins.then_inc(ea_ps, 1)
                            pe.wait_ge(ea_sb, c + 1)
                            if not (first and b < 2):
                                pe.wait_ge(filt_used, c - 1)
                            for t in range(CT0):
                                ins = nc.tensor.matmul(PS[:, 2 + 2 * (b % 2) + t // 4, (t % 4) * P:(t % 4 + 1) * P],
                                                       eaT[:, b % 2, t * P:(t + 1) * P], wd[:, :], start=True, stop=True)
                            ins.then_inc(filt_ps, 1)

                    filters(0, first=True)
                    with pe.Fori(1, ps["ITER"]) as i:
                        filters(i)
                pe.wait_ge(chunk_done[SLOTS - 1], ps["slot_base"] + ps["ITER"])
                last = s_rows(SLOTS - 1, ps)[:, ps["CT"] - 1, :]
                ins = nc.tensor.transpose(PS[:, tail_bank(ps), 0:P], last[:, 0:D], ident[:, :])
                if kind == "first":
                    ins = nc.tensor.transpose(PS[:, 6, P:2 * P], s_cf(SLOTS - 1)[:, CT0 - 1, :], ident[:, :])
                if H:
                    nc.tensor.transpose(PS[0:H, 6, P:2 * P], last[:, D:D + H], ident[:, :])
                    ins = nc.tensor.transpose(PS[0:H, 6, 2 * P:3 * P], last[:, D + H:D + 2 * H], ident[:, :])
                ins.then_inc(tail_T, 1)
                if H:
                    pe.wait_ge(tail_exp, k - GAT1 + 1)
                    nc.tensor.matmul(PS[:, 7, 0:P], head_rows[:, :], EE[0:H, 0, :], start=True, stop=True)
                    nc.tensor.matmul(PS[:, 7, P:2 * P], head_rows[:, :], EE[0:H, 1, :], start=True, stop=True).then_inc(tail_B, 1)
                pe.wait_ge(tail_V, k + 1)
                ins = nc.tensor.transpose(PS[:, tail_bank(ps), 0:P], V[:, 0:P], ident[:, :])
                if kind == "first":
                    ins = nc.tensor.transpose(PS[:, 6, P:2 * P], V2[:, 0:P], ident[:, :])
                if H:
                    nc.tensor.transpose(PS[:, 6, P:P + H], dV[0:H, 0:P], ident[0:H, 0:H])
                    ins = nc.tensor.transpose(PS[:, 6, 2 * P:2 * P + H], mV[0:H, 0:P], ident[0:H, 0:H])
                ins.then_inc(tail_C, 1)
                if kind == "max":
                    pe.wait_ge(item_added, NBANK * k * IPP)
            dense(GAT3)
            pe.wait_ge(min_ready, 1)
            nc.tensor.transpose(PS[0:1, 7, 0:P], small[:, 20:21], ident[:, :]).then_inc(min_T, 1)
            pe.wait_ge(min_one, 1)
            nc.tensor.matmul(PS[:, 7, P:P + 1], ones_row[0:1, :], small[0:1, 21:22], start=True, stop=True).then_inc(min_ps, 1)
            pe.wait_ge(cf_ready, 1)
            for g in range(NG):
                if g >= 2:
                    pe.wait_ge(aggT_sb, g - 1)
                for n, b in enumerate(blocks(g)):
                    ins = nc.tensor.transpose(PS[:, g % 2, n * P:(n + 1) * P], AGG[:, b, :], ident[:, :])
                ins.then_inc(aggT_ps, 1)
            pe.wait_ge(aggT_sb, NG)
            pe.wait_ge(max_ready, 1)
            for g in range(NG):
                if g >= 2:
                    pe.wait_ge(max_used, g - 1)
                for n, b in enumerate(blocks(g)):
                    ins = nc.tensor.transpose(PS[:, g % 2, n * P:(n + 1) * P], big_max[:, b * P:(b + 1) * P], ident[:, :])
                ins.then_inc(max_T, 1)
            pe.wait_ge(rows_ready, 1)
            for j, q in enumerate((N_ROW1, N_ROW2)):
                if j:
                    pe.wait_ge(rows_sb, 1)
                for b in range(NB):
                    ins = nc.tensor.matmul(PS[:, b // 4, (b % 4) * P:(b % 4 + 1) * P], nodes[:, q, b:b + 1].to_broadcast([P, P]),
                                           ident[:, :], start=True, stop=True)
                ins.then_inc(rows_ps, 1)
            pe.wait_ge(rows_sb, 2)
            hx = rows(Hx, WIDTH[GAT3])
            for m in range(NB):
                pe.wait_ge(pair_w, m + 1)
                for c in range(0, NP_, 512):
                    n = min(512, NP_ - c)
                    ins = nc.tensor.matmul(PS[:, c // 512, 0:n], hx[:, m, 0:D], soft_w[m % 3][:, c:c + n],
                                           start=(m == 0), stop=(m == NB - 1))
                ins.then_inc(pair_mm, 1)
            pe.wait_ge(pair_den, NB)
            for b in range(NB):
                ins = nc.tensor.matmul(PS[:, 7, b:b + 1], den_sum[:, b * P:(b + 1) * P], small[:, 30:31], start=True, stop=True)
            ins.then_inc(den_ps, 1)
            pe.wait_ge(acc_sb, 1)
            for g in range(NG):
                if g >= 2:
                    pe.wait_ge(acc_used, g - 1)
                for n, b in enumerate(blocks(g)):
                    ins = nc.tensor.transpose(PS[:, g % 2, n * P:(n + 1) * P], xT[:, b * P:(b + 1) * P], ident[:, :])
                ins.then_inc(acc_T, 1)
            pe.wait_ge(acc_used, NG)
            dense(CF)
            for r in range(2):
                d = GCN1 + r
                dense(d)
                pe.wait_ge(h_sb, NG * (d + 1))
                for m in range(NB):
                    q = (2 + r) * NB + m
                    adj_wait(pe, q)
                    for c in range(0, NP_, 512):
                        n = min(512, NP_ - c)
                        ins = nc.tensor.matmul(PS[:, c // 512, 0:n], rows(Hx, D)[:, m, :], adj_tile(q)[:, c:c + n],
                                               start=(m == 0), stop=(m == NB - 1))
                    ins.then_inc(adj_used, 1)
                pe.wait_ge(adj_used, (r + 2) * NB)
                pe.sem_inc(gcn_ps, 1)
                pe.wait_ge(gcn_sb, r + 1)
                for g in range(NG):
                    if g >= 2:
                        pe.wait_ge(gcn_out, r * NG + g - 1)
                    for n, b in enumerate(blocks(g)):
                        ins = nc.tensor.transpose(PS[:, g % 2, n * P:(n + 1) * P], xT[:, b * P:(b + 1) * P], ident[:, :])
                    ins.then_inc(gcn_T, 1)
                pe.wait_ge(gcn_out, (r + 1) * NG)

        @block.vector
        def _(dve):
            vec = nc.vector
            count = 0

            def link(ins):
                nonlocal count
                count += 1
                ins.then_inc(chain_v, 1)
                dve.wait_ge(chain_v, count)

            def tt(o, a, b, op):
                return vec.tensor_tensor(o, a, b, op)

            def ts(o, a, s1, s2, op0, op1=None):
                return vec.tensor_scalar(o, a, s1, s2, op0, op1) if op1 is not None else vec.tensor_scalar(o, a, s1, None, op0)

            link(vec.memset(ad_e[:, :, :], 0.0))
            vec.memset(src_i[:, T:T + SLOTS * CT], 0).then_inc(zero_ready, 1)
            link(vec.memset(eaT[NRBF:NRBF + 1, :, :], 1.0))
            link(vec.memset(ones_row[:, :], 1.0))
            link(vec.memset(small[:, 30:31], 1.0))
            link(vec.memset(S[SLOTS - 1][:, :], 0.0))
            link(vec.memset(V[:, 0:1], 0.0))
            link(vec.memset(V2[:, 0:1], 0.0))
            link(vec.memset(mV[:, 0:1], -BIG))
            link(vec.memset(dV[:, 0:1], 0.0))
            link(vec.memset(mbuf[:, :, :], 0.0))
            dve.wait_ge(edges_in, 64)
            dve.wait_ge(ready_const, 1)
            link(vec.tensor_copy(dst_f[:, :], dst_i[:, :]))
            link(ts(small[:, 1:2], dst_f[:, T - 1:T], 1.0, None, ALU.add))
            ts(small[:, 2:3], dst_f[:, 0:1], 1.0, None, ALU.add).then_inc(part_ready, 1)
            link(tt(keep01[:, 1:T], dst_f[:, 1:T], dst_f[:, 0:T - 1], ALU.is_equal))
            link(vec.memset(keep01[:, 0:1], 0.0))
            link(ts(keepM[:, :], keep01[:, :], 2.0, -1.0, ALU.mult, ALU.add))
            link(ts(keepM[:, :], keepM[:, :], BIG, None, ALU.mult))
            dve.wait_ge(part_rows, 1)
            lastB = xT[:, 0:P]
            link(vec.tensor_copy(lastB, PS[:, 5, 0:P]))
            link(vec.tensor_copy(small[:, 3:4], PS[:, 5, P:P + 1]))
            link(ts(nd(N_T0), nval[:, :], 1.0, None, ALU.add))
            cmp = X[:, :, :]
            link(tt(cmp, lastB.unsqueeze(1).to_broadcast([P, NB, P]), nd(N_T0).unsqueeze(2).to_broadcast([P, NB, P]), ALU.is_le))
            link(vec.tensor_reduce(nd(N_P), cmp, AX.X, ALU.add))
            link(ts(nd(N_P), nd(N_P), float(P - 1), None, ALU.min))
            vec.tensor_copy(nodes_i[:, 2, :], nd(N_P)).then_inc(p_ready, 1)
            link(tt(small[:, 4:5], small[:, 2:3], small[:, 3:4], ALU.is_equal))
            link(tt(small[:, 5:6], small[:, 1:2], small[:, 2:3], ALU.is_equal))
            tt(small[:, 8:9], small[:, 4:5], small[:, 5:6], ALU.mult).then_inc(flag_ready, 1)
            eqf = aggT[:, 0:T]
            link(ts(eqf, dst_f[:, :], dst_f[:, 0:1], None, ALU.is_equal))
            link(vec.tensor_reduce(small[:, 6:7], eqf, AX.X, ALU.add))
            link(tt(small[:, 7:8], small[:, 6:7], small[:, 0:1], ALU.add))
            link(ts(small[:, 7:8], small[:, 7:8], -1.0, None, ALU.add))
            link(ts(small[:, 9:10], small[:, 4:5], -float(SKIP), float(SKIP), ALU.mult, ALU.add))
            link(tt(small[:, 9:10], small[:, 9:10], small[:, 7:8], ALU.add))
            link(vec.tensor_copy(edge_i[:, 0:1], small[:, 7:8]))
            link(vec.tensor_copy(edge_i[:, 1:2], small[:, 9:10]))
            link(vec.tensor_copy(edge_i[:, 2:3], dst_f[:, 0:1]))
            dve.wait_ge(flag_rows, 1)
            link(vec.tensor_copy(kB01[:, :], PS[:, 5, 2 * P:3 * P]))
            link(ts(kBM[:, :], kB01[:, :], 2.0, -1.0, ALU.mult, ALU.add))
            link(ts(kBM[:, :], kBM[:, :], BIG, None, ALU.mult))
            dve.wait_ge(setup_in, 16 * N_SETUP)
            for j, h in enumerate((HEADS, HEADS, 1)):
                for q in range(2):
                    o = att_m[:, j, q * h:(q + 1) * h]
                    if h == 4:
                        ins = ts(o, head_of[:, :], att[:, j, q:q + 1], None, ALU.mult)
                    else:
                        ins = vec.tensor_copy(o, att[:, j, q:q + 1])
            ins.then_inc(att_ready, 1)
            def dense_out(d, g):
                hx = rows(Hx, WIDTH[d])
                bs = blocks(g)
                dve.wait_ge(h_ps, NG * d + g + 1)
                p = ps_rows(2 + (NG * d + g) % 2, g, WIDTH[d])
                o = hx[:, span(g), :]
                if d in (GAT1, GAT2, GAT3):
                    ins = vec.tensor_copy(o, p)
                elif d in (GCN1, GCN2):
                    ins = tt(o, p, nodes[:, N_DINV, span(g)].unsqueeze(2).to_broadcast([P, len(bs), D]), ALU.mult)
                else:
                    ins = tt(o, p, bias[:, d:d + 1, :].to_broadcast([P, len(bs), D]), ALU.add)
                ins.then_inc(h_sb, 1)

            for g in range(NG):
                dense_out(0, g)
            mask = aggT[:, T:2 * T]
            same = aggT[:, 2 * T:3 * T]
            link(ts(mask, gate[:, :], 5.0, None, ALU.is_lt))
            link(vec.tensor_copy(same, src_i[:, 0:T]))
            link(tt(same, same, dst_f[:, :], ALU.not_equal))
            link(tt(mask, mask, same, ALU.mult))
            link(ts(same.bitcast(i32), gate[:, :], 0.1, None, ALU.mult))
            link(ts(same, same.bitcast(i32), -10.0, None, ALU.mult))
            link(tt(gate[:, :], gate[:, :], same, ALU.add))
            link(ts(same, gate[:, :], -1.0, None, ALU.mult))
            link(tt(gate[:, :], gate[:, :], same, ALU.max))
            link(ts(same, gate[:, :], -1.0, 10.0, ALU.mult, ALU.add))
            link(tt(gate[:, :], gate[:, :], same, ALU.min))
            ts(gate[:, :], gate[:, :], -float(np.pi) / 5.0, float(np.pi) / 2.0, ALU.mult, ALU.add).then_inc(cos_arg, 1)
            dve.wait_ge(cos_done, 1)
            link(ts(gate[:, :], gate[:, :], 0.5, 0.5, ALU.mult, ALU.add))
            link(tt(gate[:, :], gate[:, :], mask, ALU.mult))
            for b in range(NB):
                dve.wait_ge(ends_rows[b % SLOTS], 16 * (b // SLOTS + 1))
                o = R[:, (b % 2) * T:(b % 2 + 1) * T]
                ts(o, G[b % SLOTS][:, 0:T].bitcast(i32), nval[:, b:b + 1], None, ALU.is_le).then_inc(ends_used, 1)
                dve.wait_ge(ends_used, b + 1)
                link(vec.tensor_reduce(nodes[:, N_CNT, b:b + 1], o, AX.X, ALU.add))
            link(ts(nd(N_T0), nd(N_P), float(T), None, ALU.mult))
            link(tt(nd(N_CNT), nd(N_CNT), nd(N_T0), ALU.add))
            link(vec.memset(nodes[:, N_T1, 0:1], 0.0))
            vec.tensor_copy(nodes[:, N_T1, 1:NB], nodes[:, N_CNT, 0:NB - 1]).then_inc(cnt_ready, 1)
            dve.wait_ge(start_ps, 1)
            dve.wait_ge(cnt_ready, 1)
            link(vec.tensor_copy(nd(N_START), PS[:, 6, 0:NB]))
            link(tt(nd(N_DEG), nd(N_CNT), nd(N_START), ALU.subtract))
            link(ts(nd(N_HAS), nd(N_DEG), 1.0, None, ALU.min))
            link(ts(nd(N_END), nd(N_CNT), -1.0, 0.0, ALU.add, ALU.max))
            link(vec.tensor_copy(nodes_i[:, 0, :], nd(N_END)))
            link(ts(nd(N_T1), nd(N_HAS), -float(SKIP), float(SKIP), ALU.mult, ALU.add))
            link(tt(nd(N_T1), nd(N_T1), nd(N_START), ALU.add))
            vec.tensor_copy(nodes_i[:, 1, :], nd(N_T1)).then_inc(nodes_ready, 1)
            ts(nd(N_T0), nd(N_DEG), 1.0, None, ALU.add).then_inc(deg_ready, 1)
            dve.wait_ge(dinv_root, 1)
            link(vec.reciprocal(nd(N_DINV), nd(N_T0)))
            def item_list():
                link(vec.tensor_copy(nd(N_T0), PS[:, 5, 0:NB]))
                link(ts(nd(N_T0), nd(N_T0), -1.0, 0.0, ALU.add, ALU.max))
                floor_of(nd(N_T1), nd(N_T0), 1.0 / (GE * P), nodes_i[:, 2, :], nodes[:, N_FREE, :])
                link(tt(nd(N_HI), nd(N_T1), nd(N_BLK), ALU.add))
                iv = small[:, 16:18]
                cv = small[:, 18:20]
                link(ts(iv[:, 0:1], nval[:, 0:1], 0.0, None, ALU.add))
                link(ts(iv[:, 1:2], nval[:, 0:1], float(P), None, ALU.add))
                for j in range(2):
                    link(ts(nodes[:, N_FREE, 0:NB - 1], nodes[:, N_HI, 0:NB - 1], iv[:, j:j + 1], None, ALU.is_lt))
                    link(vec.tensor_reduce(cv[:, j:j + 1], nodes[:, N_FREE, 0:NB - 1], AX.X, ALU.add))
                link(tt(cv, iv, cv, ALU.subtract))
                link(ts(cv, cv, float(NGRP - 1), None, ALU.min))
                vec.tensor_copy(edge_i[:, 3:5], cv).then_inc(item_idx, 1)

            def floor_of(o, a, scale, ti, tf):
                link(ts(tf, a, scale, None, ALU.mult))
                link(vec.tensor_copy(ti, tf))
                link(vec.tensor_copy(o, ti))
                link(tt(tf, o, tf, ALU.is_gt))
                link(tt(o, o, tf, ALU.subtract))

            def staircase():
                dve.wait_ge(item_rows, 64)
                for q in range(4):
                    r = rows_a[q][0:(P, NSLOT - P)[q % 2], :]
                    ins = vec.tensor_copy(r, r.bitcast(i32))
                ins.then_inc(item_f, 1)
                dve.wait_ge(iota_ready, 1)
                cb = dst_f[:, 0:NSLOT]
                ii = dst_f[:, NSLOT:2 * NSLOT]
                link(vec.tensor_copy(ii, iota_n[:, 0:NSLOT]))
                link(vec.memset(cb, 0.0))
                for c in range(NB - 1):
                    link(vec.scalar_tensor_tensor(cb, ii, nodes[:, N_HI, c:c + 1], cb, ALU.is_gt, ALU.add))
                link(tt(item_keep[:, 1:NSLOT], cb[:, 1:NSLOT], cb[:, 0:NSLOT - 1], ALU.is_equal))
                link(vec.memset(item_keep[:, 0:1], 0.0))
                link(vec.tensor_copy(item_blk, cb))
                link(vec.memset(ii, 0.0))
                link(tt(ii[:, 0:NITEM - 1], cb[:, 1:NITEM], cb[:, 0:NITEM - 1], ALU.is_gt))
                link(vec.memset(ii[:, NITEM - 1:NITEM], 1.0))
                link(vec.tensor_copy(item_last, ii))
                link(ts(cb, cb, -float(P), None, ALU.mult))
                dve.wait_ge(item_ps, 1)
                link(vec.tensor_copy(item_src, PS[:, 0:GE, 0:NSLOT]))
                if NSLOT > NITEM:
                    link(vec.memset(item_src[:, :, NITEM:NSLOT], -1.0))
                tt(item_dst, PS[:, GE:2 * GE, 0:NSLOT], cb.unsqueeze(1).to_broadcast([P, GE, NSLOT]), ALU.add).then_inc(item_tab, 1)
                dve.wait_ge(item_tab, 1)

            dve.wait_ge(hi_ps, 1)
            item_list()
            has = nd(N_HAS).unsqueeze(2).to_broadcast([P, NB, D])

            n_ln = 0

            def layer_norm(src, dst, done, before=None, d=None):
                nonlocal n_ln
                for g in range(NG + 3):
                    if g < NG:
                        if before:
                            before(g)
                        bs = span(g)
                        for b in blocks(g):
                            ins = vec.bn_stats(stats[:, b, :], src[:, b, :])
                        link(ins)
                        for b in blocks(g):
                            ins = vec.bn_aggr(mv[:, b, :], stats[:, b, :])
                        link(ins)
                        ts(mv[:, bs, 1], mv[:, bs, 1], 1e-5, None, ALU.add).then_inc(ln_var, 1)
                        link(tt(src[:, bs, :], src[:, bs, :], mv[:, bs, 0:1].to_broadcast([P, len(blocks(g)), D]), ALU.subtract))
                    if 1 <= g <= NG:
                        bs, n = span(g - 1), len(blocks(g - 1))
                        dve.wait_ge(ln_std, n_ln + g)
                        link(vec.reciprocal(stats[:, bs, 0], mv[:, bs, 1]))
                        tt(dst[:, bs, :], src[:, bs, :], stats[:, bs, 0:1].to_broadcast([P, n, D]), ALU.mult).then_inc(done, 1)
                    if g >= 3 and d is not None:
                        dense_out(d, g - 3)
                n_ln += NG

            for k, ps in enumerate(PASSES):
                kind, ct, w, H, rw, base = ps["kind"], ps["CT"], ps["W"], ps["H"], ps["RW"], ps["slot_base"]
                it = ps["ITER"]
                if k == 1:
                    staircase()
                if H:
                    if k == GAT1:
                        dve.wait_ge(item_stored, 16 * NSLOT)
                    else:
                        link(tt(XRES[:, :, :], XRES[:, :, :], bias[:, GAT3:GAT3 + 1, :].to_broadcast([P, NB, D]), ALU.add))
                    if k == GAT1:
                        dve.wait_ge(cf_in, 16 * NB)
                        tt(AGG[:, :, :], AGG[:, :, :], has, ALU.mult).then_inc(cf_ready, 1)
                    j = k - GAT1
                    dve.wait_ge(ad_loaded, 16 * (j + 1))
                    dve.wait_ge(ad_first, 16 * (j + 1))
                    rr = R[:, 0:T * H].rearrange("p (t h) -> p t h", h=H)
                    link(vec.tensor_copy(rr[:, 0, :], ad0[:, D + H:D + 2 * H]))
                    for h in range(H):
                        link(vec.tensor_tensor_scan(ad_e[:, h, 0:T], keep01[:, :], rr[:, :, h], 0.0, ALU.mult, ALU.add))

                per_chunk = {"first": 3 * ct - 1, "max": ct - 1,
                             "gat": 7 + 2 * H + 2 * ct - 1}[kind]
                loop0 = count

                def one_hot(item, t):
                    ts(dst_hot[:, t, :], iota_n[:, 0:P], item_dst[:, t, bass.ds(item, 1)], CSCALE, ALU.is_equal, ALU.mult)
                    ts(src_hot[t], iota_n, item_src[:, t, bass.ds(item, 1)], None, ALU.is_equal).then_inc(hot_ready, 1)

                def add_bank(item, j):
                    n = min(512, NP_ - 512 * j)
                    own = counts[:, 512 * j:512 * j + n]
                    vec.scalar_tensor_tensor(own, own, item_keep[:, bass.ds(item, 1)], PS[:, j, 0:n], ALU.mult, ALU.add).then_inc(item_added, 1)

                def chunk(i, b, first, last=False):
                    c = i * SLOTS + b
                    n = 0
                    c0 = loop0 + c * per_chunk

                    def step(ins):
                        nonlocal n
                        n += 1
                        ins.then_inc(chain_v, 1)
                        return n

                    def after(m):
                        dve.wait_ge(chain_v, c0 + m)

                    gr, sr = g_rows(b, ps), s_rows(b, ps)
                    pb = (b - 1) % SLOTS
                    prev = s_rows(pb, ps)[:, ct - 1, :]
                    prev_cf = s_cf(pb)[:, CT0 - 1, :] if kind == "first" else None
                    dve.wait_ge(gathered[b], ps["gath_base"] + 16 * ct * (i + 1))
                    if not (k == 0 and first):
                        n_st = 2 * i if kind == "first" else base + i + PASSES[0]["ITER"]
                        dve.wait_ge(run_stored[b], 16 * n_st)
                    if b:
                        dve.wait_ge(chunk_done[pb], base + i + 1)
                    elif not (k == 0 and first):
                        dve.wait_ge(chunk_done[pb], base + i)
                    kM = keepM[:, bass.ds(c * ct, ct)]

                    def fold(o, p, kk, g, op0, op1):
                        return vec.scalar_tensor_tensor(o, p, kk, g, op0, op1)

                    def one(buf, t):
                        return buf[:, bass.ds(c * ct + t, 1)]

                    if kind == "max":
                        item = (k - 1) * IPP + c
                        very_first = k == 1 and first and b == 0
                        for t in range(ct):
                            ins = fold(sr[:, t, :], sr[:, t - 1, :] if t else prev, one(keepM, t), gr[:, t, :], ALU.min, ALU.max)
                            if t == ct - 1:
                                ins.then_inc(chunk_done[b], 1)
                                continue
                            m = step(ins)
                            if last:
                                pass
                            elif t < GE:
                                if t == 0 and not very_first:
                                    dve.wait_ge(item_sum, NBANK * item)
                                one_hot(item, t)
                            elif GE < t <= GE + NBANK:
                                if t == GE + 1 and not very_first:
                                    dve.wait_ge(item_stored, 16 * item)
                                dve.wait_ge(item_sum, NBANK * item + t - GE)
                                add_bank(item, t - GE - 1)
                            after(m)
                    elif kind == "first":
                        sc = s_cf(b)
                        dve.wait_ge(filt_ps, c + 1)
                        a_prev = None
                        for t in range(ct):
                            f = PS[:, 2 + 2 * (b % 2) + t // 4, (t % 4) * P:(t % 4 + 1) * P]
                            m = step(vec.scalar_tensor_tensor(gr[:, t, D:2 * D], f, one(gate, t), gr[:, t, D:2 * D], ALU.mult, ALU.mult))
                            if a_prev:
                                after(a_prev)
                            a_prev = step(fold(sr[:, t, :], sr[:, t - 1, :] if t else prev, one(keepM, t), gr[:, t, 0:D], ALU.min, ALU.max))
                            after(m)
                            if t == ct - 1:
                                after(a_prev)
                            ins = fold(sc[:, t, :], sc[:, t - 1, :] if t else prev_cf, one(keep01, t), gr[:, t, D:2 * D], ALU.mult, ALU.add)
                            if t < ct - 1:
                                step(ins)
                        ins.then_inc(chunk_done[b], 1)
                    else:
                        v4 = lambda a: a[:, :, 0:H]
                        z, e = v4(zc), v4(ec)
                        mb = mbuf[:, :, 0:H]
                        adv = ad_e[:, 0:H, bass.ds(c * ct, ct)].rearrange("p h t -> p t h")
                        step(vec.tensor_copy(mb[:, 0, :], mb[:, ct, :]))
                        after(step(tt(z, gr[:, :, D:D + H], adv, ALU.add)))
                        after(step(vec.scalar_tensor_tensor(e, z, 0.2, z, ALU.mult, ALU.max)))
                        for h in range(H):
                            m = step(vec.tensor_tensor_scan(mb[:, 1:ct + 1, h], kM, e[:, :, h], mb[:, 0, h:h + 1], ALU.min, ALU.max))
                        after(m)
                        after(step(tt(v4(mp), mb[:, 0:ct, :], kM.unsqueeze(2).to_broadcast([P, ct, H]), ALU.min)))
                        m = step(tt(dc[:, 1, :, 0:H], v4(mp), mb[:, 1:ct + 1, :], ALU.subtract))
                        after(m)
                        tt(dc[:, 0, :, 0:H], e, mb[:, 1:ct + 1, :], ALU.subtract).then_inc(soft_arg, 1)
                        step(vec.tensor_copy(sr[:, :, D + H:D + 2 * H], mb[:, 1:ct + 1, :]))
                        dve.wait_ge(soft_exp, (k - GAT1) * SLOTS * it + c + 1)
                        for h in range(H):
                            step(vec.tensor_tensor_scan(sr[:, :, D + h], pc[:, 1, :, h], pc[:, 0, :, h],
                                                        prev[:, D + h:D + h + 1], ALU.mult, ALU.add))
                        C = D // H
                        gh = gr[:, :, 0:D].rearrange("p t (h c) -> p t h c", h=H)
                        after(step(tt(gh, gh, pc[:, 0, :, 0:H].unsqueeze(3).to_broadcast([P, ct, H, C]), ALU.mult)))
                        for t in range(ct):
                            p = (sr[:, t - 1, :] if t else prev)[:, 0:D]
                            o = sr[:, t, 0:D]
                            hv = lambda a: a.rearrange("p (h c) -> p h c", h=H)
                            after(step(tt(hv(tmpr[:, :]), hv(p), pc[:, 1, t, 0:H].unsqueeze(2).to_broadcast([P, H, C]), ALU.mult)))
                            ins = tt(o, tmpr[:, :], gr[:, t, 0:D], ALU.add)
                            if t < ct - 1:
                                after(step(ins))
                        ins.then_inc(chunk_done[b], 1)
                    assert n == per_chunk, (kind, n, per_chunk)

                for b in range(SLOTS):
                    chunk(0, b, True)
                    if kind == "first":
                        dve.wait_ge(chunk_done[b], 1)
                        dve.sem_inc(filt_used, 1)
                with dve.Fori(1, it - 1 if kind == "max" else it) as i:
                    for b in range(SLOTS):
                        chunk(i, b, False)
                        if kind == "first":
                            dve.wait_ge(chunk_done[b], i + 1)
                            dve.sem_inc(filt_used, 1)
                if kind == "max":
                    for b in range(SLOTS):
                        chunk(it - 1, b, False, last=b == SLOTS - 1)
                count = loop0 + per_chunk * SLOTS * it

                dve.wait_ge(tail_T, k + 1)
                if kind in ("first", "max"):
                    ins = vec.tensor_tensor_scan(V[:, 1:P + 1], kBM[:, :], PS[:, tail_bank(ps), 0:P], -BIG, ALU.min, ALU.max)
                    if kind == "first":
                        link(ins)
                        ins = vec.tensor_tensor_scan(V2[:, 1:P + 1], kB01[:, :], PS[:, 6, P:2 * P], 0.0, ALU.mult, ALU.add)
                    ins.then_inc(tail_V, 1)
                else:
                    mT = PS[0:H, 6, 2 * P:3 * P]
                    link(vec.tensor_tensor_scan(mV[0:H, 1:P + 1], kBM[0:H, :], mT, -BIG, ALU.min, ALU.max))
                    link(tt(prevm[0:H, :], kBM[0:H, :], mV[0:H, 0:P], ALU.min))
                    link(tt(DD[0:H, 0, :], mT, mV[0:H, 1:P + 1], ALU.subtract))
                    tt(DD[0:H, 1, :], prevm[0:H, :], mV[0:H, 1:P + 1], ALU.subtract).then_inc(tail_arg, 1)
                    accT = FX2[:, 0:P]
                    link(vec.tensor_copy(accT, PS[:, 6, 0:P]))
                    dve.wait_ge(tail_B, k - GAT1 + 1)
                    link(tt(accT, accT, PS[:, 7, 0:P], ALU.mult))
                    link(vec.tensor_tensor_scan(V[:, 1:P + 1], PS[:, 7, P:2 * P], accT, 0.0, ALU.mult, ALU.add))
                    link(tt(denT[0:H, :], PS[0:H, 6, P:2 * P], EE[0:H, 0, :], ALU.mult))
                    vec.tensor_tensor_scan(dV[0:H, 1:P + 1], EE[0:H, 1, :], denT[0:H, :], 0.0, ALU.mult, ALU.add).then_inc(tail_V, 1)
                dve.wait_ge(tail_C, k + 1)
                dve.wait_ge(fix_in, 16 * (k + 2))
                if kind == "first":
                    link(tt(FX2[:, 0:D], FX2[:, 0:D], PS[:, 6, P:2 * P], ALU.add))
                if not H:
                    tt(FX[:, 0:D], FX[:, 0:D], PS[:, tail_bank(ps), 0:P], ALU.max).then_inc(fix_new, 1)
                else:
                    fm, cm = FX[:, D + H:D + 2 * H], PS[:, 6, 2 * P:2 * P + H]
                    link(tt(fxm[:, 2, 0:H], fm, cm, ALU.max))
                    link(tt(fxm[:, 0, 0:H], fm, fxm[:, 2, 0:H], ALU.subtract))
                    tt(fxm[:, 1, 0:H], cm, fxm[:, 2, 0:H], ALU.subtract).then_inc(fix_arg, 1)
                    dve.wait_ge(fix_exp, k - GAT1 + 1)
                    hv = lambda a: a.rearrange("p (h c) -> p h c", h=H)
                    bc = lambda a: a.unsqueeze(2).to_broadcast([P, H, D // H])
                    link(tt(hv(FX[:, 0:D]), hv(FX[:, 0:D]), bc(fxe[:, 0, 0:H]), ALU.mult))
                    link(tt(hv(FX2[:, 0:D]), hv(PS[:, 6, 0:P]), bc(fxe[:, 1, 0:H]), ALU.mult))
                    link(tt(FX[:, 0:D], FX[:, 0:D], FX2[:, 0:D], ALU.add))
                    link(tt(FX[:, D:D + H], FX[:, D:D + H], fxe[:, 0, 0:H], ALU.mult))
                    link(tt(FX2[:, D:D + H], PS[:, 6, P:P + H], fxe[:, 1, 0:H], ALU.mult))
                    link(tt(FX[:, D:D + H], FX[:, D:D + H], FX2[:, D:D + H], ALU.add))
                    vec.tensor_copy(fm, fxm[:, 2, 0:H]).then_inc(fix_new, 1)

                dve.wait_ge(table_stored, 16 * NG * (k + 1))
                if H:
                    dve.wait_ge(ad_scattered, 16 * NB * (k - GAT1 + 1))
                rv = rows(R, w)

                def arrived(g):
                    dve.wait_ge(end_in[g], 16 * len(blocks(g)) * (k + 1))

                def has_of(g):
                    return has[:, span(g), :]

                if k < NL0 - 1:
                    for g in range(NG + 2):
                        if g < NG:
                            arrived(g)
                            tt(X[:, span(g), :], rv[:, span(g), :], has_of(g), ALU.mult).then_inc(agg_ready, 1)
                        if g >= 2:
                            dense_out(k + 1, g - 2)
                elif not H:
                    def residual(g):
                        arrived(g)
                        link(tt(X[:, span(g), :], rv[:, span(g), :], has_of(g), ALU.mult))
                        link(tt(X[:, span(g), :], X[:, span(g), :], XRES[:, span(g), :], ALU.add))

                    layer_norm(X, XRES, x_ready, residual, k + 1)
                else:
                    hx = rows(Hx, rw)
                    v3 = lambda q, bs=slice(0, NB): na[:, q, bs.start * H:bs.stop * H].rearrange("p (b h) -> p b h", h=H)
                    C = D // H
                    v4d = lambda a: a.rearrange("p b (h c) -> p b h c", h=H)
                    hasH = nd(N_HAS).unsqueeze(2).to_broadcast([P, NB, H])
                    link(tt(v3(0), hx[:, :, D:D + H], hx[:, :, D + H:D + 2 * H], ALU.add))
                    link(vec.scalar_tensor_tensor(v3(1), v3(0), 0.2, v3(0), ALU.mult, ALU.max))
                    link(ts(v3(7), hasH, BIG, -BIG, ALU.mult, ALU.add))
                    for q, groups in enumerate(POST):
                        bs = slice(span(groups[0]).start, span(groups[-1]).stop)
                        v = lambda q: v3(q, bs)
                        hs = hasH[:, bs, :]
                        for g in groups:
                            arrived(g)
                        link(tt(v(6), rv[:, bs, D + H:D + 2 * H], hs, ALU.mult))
                        link(tt(v(6), v(6), v(7), ALU.add))
                        link(tt(v(0), v(6), v(1), ALU.max))
                        link(tt(v(2), v(6), v(0), ALU.subtract))
                        tt(v(3), v(1), v(0), ALU.subtract).then_inc(post_arg, 1)
                        dve.wait_ge(post_exp, len(POST) * (k - GAT1) + q + 1)
                        link(tt(v(4), v(4), hs, ALU.mult))
                        link(tt(v(7), rv[:, bs, D:D + H], v(4), ALU.mult))
                        link(tt(v(7), v(7), v(5), ALU.add))
                        link(ts(v(7), v(7), 1e-16, None, ALU.add))
                        link(vec.reciprocal(v(7), v(7)))
                        link(tt(v(4), v(4), v(7), ALU.mult))
                        link(tt(v(5), v(5), v(7), ALU.mult))
                        for g in groups:
                            gs, n = span(g), len(blocks(g))
                            bc = lambda q: v3(q, gs).unsqueeze(3).to_broadcast([P, n, H, C])
                            tt(v4d(X[:, gs, :]), v4d(rv[:, gs, 0:D]), bc(4), ALU.mult)
                            link(tt(v4d(tmpg[:, 0:n, :]), v4d(hx[:, gs, 0:D]), bc(5), ALU.mult))
                            link(tt(X[:, gs, :], X[:, gs, :], tmpg[:, 0:n, :], ALU.add))
                            tt(X[:, gs, :], X[:, gs, :], bias[:, k:k + 1, :].to_broadcast([P, n, D]), ALU.add).then_inc(agg_ready, 1)
                            if g >= 2:
                                dense_out(k + 1, g - 2)
                    for g in (NG - 2, NG - 1):
                        dense_out(k + 1, g)

            dve.wait_ge(h_sb, NG * (GAT3 + 1))
            hx = rows(Hx, WIDTH[GAT3])
            a_s, a_d = hx[:, :, D], hx[:, :, D + 1]
            vec.tensor_reduce(small[:, 20:21], a_s, AX.X, ALU.min).then_inc(min_ready, 1)
            dve.wait_ge(min_T, 1)
            vec.tensor_reduce(small[0:1, 21:22], PS[0:1, 7, 0:P], AX.X, ALU.min).then_inc(min_one, 1)
            link(vec.memset(big_max, 0.0))
            dve.wait_ge(min_ps, 1)
            link(ts(small[:, 22:23], PS[:, 7, P:P + 1], -1.0, None, ALU.add))
            link(ts(nd(N_POS), a_s, small[:, 22:23], None, ALU.subtract))
            for m in range(NB):
                adj_wait(dve, m)
                vec.scalar_tensor_tensor(big_max, adj_tile(m), nodes[:, N_POS, m:m + 1], big_max, ALU.min, ALU.max).then_inc(adj_used, 1)
                dve.wait_ge(adj_used, m + 1)
            dve.sem_inc(max_ready, 1)
            for g in range(NG):
                bs = slice(blocks(g)[0], blocks(g)[-1] + 1)
                dve.wait_ge(max_T, g + 1)
                vec.tensor_reduce(nodes[:, N_MAX, bs], ps_rows(g % 2, g, D), AX.X, ALU.max).then_inc(max_used, 1)
            dve.wait_ge(max_used, NG)
            link(tt(nd(N_MAX), nd(N_MAX), nd(N_POS), ALU.max))
            link(ts(nd(N_MAX), nd(N_MAX), small[:, 22:23], None, ALU.add))
            link(tt(nd(N_MAX), nd(N_MAX), a_d, ALU.add))
            link(vec.scalar_tensor_tensor(nd(N_MAX), nd(N_MAX), 0.2, nd(N_MAX), ALU.mult, ALU.max))
            link(tt(nd(N_ROW1), a_d, nd(N_MAX), ALU.subtract))
            link(ts(nd(N_NEG), a_s, 0.2, None, ALU.mult))
            vec.scalar_tensor_tensor(nd(N_ROW2), a_d, 0.2, nd(N_MAX), ALU.mult, ALU.subtract).then_inc(rows_ready, 1)
            link(tt(nd(N_E1), a_s, a_d, ALU.add))
            link(vec.scalar_tensor_tensor(nd(N_E1), nd(N_E1), 0.2, nd(N_E1), ALU.mult, ALU.max))
            tt(nd(N_SELF), nd(N_E1), nd(N_MAX), ALU.subtract).then_inc(self_arg, 1)
            for m in range(NB):
                w = soft_w[m % 3]
                dve.wait_ge(pair_exp, m + 1)
                tt(w, w, pos_exp[m % 2], ALU.max).then_inc(pair_max, 1)
                adj_wait(dve, NB + m)
                dve.wait_ge(pair_max, m + 1)
                vec.scalar_tensor_tensor(w, w, 2.0, adj_tile(NB + m), ALU.min, ALU.mult).then_inc(pair_w, 1)
            dve.wait_ge(self_exp, 1)
            own = rows(R, D)
            link(tt(own, hx[:, :, 0:D], nd(N_SELF).unsqueeze(2).to_broadcast([P, NB, D]), ALU.mult))
            dve.wait_ge(den_ps, 1)
            link(vec.scalar_tensor_tensor(nd(N_INV), PS[:, 7, 0:NB], 1.0 / CSCALE, nd(N_SELF), ALU.mult, ALU.add))
            link(ts(nd(N_INV), nd(N_INV), 1e-16, None, ALU.add))
            link(vec.reciprocal(nd(N_INV), nd(N_INV)))

            def attention_out(g):
                bs = span(g)
                dve.wait_ge(acc_T, g + 1)
                link(vec.scalar_tensor_tensor(X[:, bs, :], ps_rows(g % 2, g, D), 1.0 / CSCALE, own[:, bs, :], ALU.mult, ALU.add))
                dve.sem_inc(acc_used, 1)
                for b in blocks(g):
                    ins = vec.scalar_tensor_tensor(X[:, b, :], X[:, b, :], nodes[:, N_INV, b:b + 1], XRES[:, b, :], ALU.mult, ALU.add)
                link(ins)

            layer_norm(X, XRES, x_ready, attention_out)
            for g in range(NG):
                dense_out(CF, g)

            dve.wait_ge(h_sb, NG * (CF + 1))

            def gated_out(g):
                link(tt(X[:, span(g), :], rows(Hx, D)[:, span(g), :], XRES[:, span(g), :], ALU.add))

            layer_norm(X, XRES, x_ready, gated_out, GCN1)

            link(ts(nd(N_DSC), nd(N_DINV), 1.0 / CSCALE, None, ALU.mult))
            base = rows(R, D)

            def gcn_base(r):
                d = GCN1 + r
                dve.wait_ge(h_sb, NG * (d + 1))
                link(tt(base, rows(Hx, D), nd(N_DINV).unsqueeze(2).to_broadcast([P, NB, D]), ALU.mult))
                link(tt(base, base, bias[:, d:d + 1, :].to_broadcast([P, NB, D]), ALU.add))
                if r:
                    link(tt(base, base, XRES[:, :, :], ALU.add))

            def gcn_sum(r, g):
                dve.wait_ge(gcn_T, r * NG + g + 1)
                for n, b in enumerate(blocks(g)):
                    ins = vec.scalar_tensor_tensor(X[:, b, :], PS[:, g % 2, n * D:(n + 1) * D], nodes[:, N_DSC, b:b + 1],
                                                   base[:, b, :], ALU.mult, ALU.add)
                ins.then_inc(gcn_out, 1)
                dve.wait_ge(gcn_out, r * NG + g + 1)

            gcn_base(0)
            for g in range(NG):
                gcn_sum(0, g)
            dve.sem_inc(x_ready, NG)
            for g in range(NG):
                dense_out(GCN2, g)
            gcn_base(1)
            layer_norm(X, X, out_ready, lambda g: gcn_sum(1, g))


def kernel(**inputs):
    import concourse.bacc as bacc
    from concourse.bass_utils import run_bass_kernel_spmd

    def padded(a, n, fill=0):
        a = np.asarray(a)
        return np.concatenate([a, np.full((n - a.shape[0],) + a.shape[1:], fill, a.dtype)])

    arrays = {name: np.asarray(a) for name, a in inputs.items()}
    for name, n, fill in (("x", NP_, 0), ("node_type_100", NP_, 0), ("src", EP, 0), ("dst", EP, N),
                          ("edge_weight", EP, 0), ("edge_attr_64", EP, 0)):
        arrays[name] = padded(arrays[name], n, fill)
    nc = bacc.Bacc("TRN2", target_bir_lowering=False, num_devices=1)
    feed, aps = {}, {}
    for name, a in arrays.items():
        feed[f"in_{name}"] = np.ascontiguousarray(a)
        aps[name] = nc.dram_tensor(f"in_{name}", a.shape, mybir.dt.from_np(a.dtype), kind="ExternalInput").ap()
    out = nc.dram_tensor("out_nodes", (N, D), mybir.dt.float32, kind="ExternalOutput").ap()
    program(nc, aps, out)
    r = run_bass_kernel_spmd(nc, [feed], core_ids=[0])
    return r.results[0]["out_nodes"]
```
